# Optimizing a Trainium2 kernel written in Bass

```python
import numpy as np
import jax
import jax.numpy as jnp

def _softmax(x, axis=-1):
    return jax.nn.softmax(x, axis=axis)

def _gelu(x):
    return jax.nn.gelu(x, approximate=True)

def _silu(x):
    return jax.nn.silu(x)

def _sigmoid(x):
    return jax.nn.sigmoid(x)

def _layernorm(x, axis=-1, eps=1e-05):
    m = jnp.mean(x, axis=axis, keepdims=True)
    v = jnp.var(x, axis=axis, keepdims=True)
    return (x - m) / jnp.sqrt(v + eps)

def _scatter_add(tgt, idx, src, axis=0):
    return tgt.at[idx].add(src)

def _segment_sum(src, seg, n):
    return jax.ops.segment_sum(src, seg, n)
kernel_name = 'mk_vit_tower_d2_tok_img1024_r4_8b0eca'

def setup_inputs(seed: int=0):
    np.random.seed(seed)
    _w = jnp.asarray

    def _rec_inputs():
        import jax
        import jax.numpy as jnp
        _rk = jax.random.key(seed)
        x = -0.00011082 + 0.999858 * jax.random.normal(jax.random.fold_in(_rk, 1), (2, 5, 128, 128), jnp.float32)
        return x
    x = _rec_inputs()

    def _L0_tok_setup():
        import jax, jax.numpy as jnp
        import numpy as np
        PATCH = 8
        EPS = 1e-05

        def _patchify(x):
            B, C, H, Wd = x.shape
            p = PATCH
            x = x.reshape(B, C, H // p, p, Wd // p, p)
            x = x.transpose(0, 2, 4, 1, 3, 5)
            return x.reshape(B, H // p * (Wd // p), C * p * p)
        key = jax.random.key(seed)
        k1, k2 = jax.random.split(key)
        B, C, H, W_ = (32, 5, 128, 128)
        in_feat, embed_dim = (C * PATCH * PATCH, 256)
        x = jax.random.normal(k1, (B, C, H, W_), dtype=jnp.float32)
        W = jax.random.normal(k2, (in_feat, embed_dim), dtype=jnp.float32) * (1.0 / np.sqrt(in_feat))
        gamma = jnp.ones((embed_dim,), dtype=jnp.float32)
        return {'x': x, 'W': W, 'gamma': gamma}
    _L0_tok_all = _L0_tok_setup()
    _L0_tok_in = {k: v for k, v in _L0_tok_all.items() if k in ('W', 'gamma')}
    del _L0_tok_all

    def _L0_attn_setup():
        import math
        import jax, jax.numpy as jnp
        import numpy as np
        N_HEADS = 16
        D_EMBED = 256
        key = jax.random.key(seed)
        ks = jax.random.split(key, 5)
        b, l, d = (2, 512, D_EMBED)
        return {'x': jax.random.normal(ks[0], (b, l, d), dtype=jnp.float32), 'w_in': jax.random.normal(ks[1], (3 * d, d), dtype=jnp.float32) * 0.02, 'b_in': jax.random.normal(ks[2], (3 * d,), dtype=jnp.float32) * 0.02, 'w_out': jax.random.normal(ks[3], (d, d), dtype=jnp.float32) * 0.02, 'b_out': jax.random.normal(ks[4], (d,), dtype=jnp.float32) * 0.02}
    _L0_attn_all = _L0_attn_setup()
    _L0_attn_in = {k: v for k, v in _L0_attn_all.items() if k in ('w_in', 'b_in', 'w_out', 'b_out')}
    del _L0_attn_all

    def _L0_ffn_setup():
        import jax, jax.numpy as jnp
        import numpy as np
        B, S, D = (1, 512, 256)
        E, K, F = (64, 8, 192)
        SF = 192
        C = 128
        ROUTED_SCALE = 1.0

        def _moe_forward(x, router_w, w_gate, w_up, w_down, ws_gate_up, ws_down):
            T = x.shape[0]
            logits = x.astype(jnp.float32) @ router_w.T
            probs = jax.nn.softmax(logits, axis=-1)
            topk_w, topk_ids = jax.lax.top_k(probs, K)
            topk_w = topk_w / jnp.sum(topk_w, axis=-1, keepdims=True)
            topk_w = topk_w.astype(x.dtype)
            N = T * K
            flat_e = topk_ids.reshape(-1)
            flat_w = topk_w.reshape(-1)
            tok = jnp.arange(N) // K
            onehot = flat_e[:, None] == jnp.arange(E)[None, :]
            pos = jnp.cumsum(onehot, axis=0)[jnp.arange(N), flat_e] - 1
            valid = pos < C
            idx = jnp.where(valid, flat_e * C + pos, E * C)
            x_buf = jnp.zeros((E * C + 1, x.shape[1]), x.dtype).at[idx].set(x[tok])
            xb = x_buf[:E * C].reshape(E, C, -1)
            g = jnp.einsum('ecd,edf->ecf', xb, w_gate)
            u = jnp.einsum('ecd,edf->ecf', xb, w_up)
            h = jax.nn.silu(g) * u
            y = jnp.einsum('ecf,efd->ecd', h, w_down).reshape(E * C, -1)
            safe = jnp.where(valid, idx, 0)
            contrib = y[safe] * (flat_w * valid.astype(flat_w.dtype))[:, None]
            routed = jax.ops.segment_sum(contrib, tok, num_segments=T)
            routed = routed * ROUTED_SCALE
            gu = x @ ws_gate_up
            sg, su = (gu[:, :SF], gu[:, SF:])
            shared = jax.nn.silu(sg) * su @ ws_down
            return routed + shared
        key = jax.random.key(seed)
        ks = jax.random.split(key, 7)
        w = 0.02
        return {'hidden_states': jax.random.normal(ks[0], (B, S, D), jnp.float32), 'router_w': jax.random.normal(ks[1], (E, D), jnp.float32) * w, 'w_gate': jax.random.normal(ks[2], (E, D, F), jnp.float32) * w, 'w_up': jax.random.normal(ks[3], (E, D, F), jnp.float32) * w, 'w_down': jax.random.normal(ks[4], (E, F, D), jnp.float32) * w, 'ws_gate_up': jax.random.normal(ks[5], (D, 2 * SF), jnp.float32) * w, 'ws_down': jax.random.normal(ks[6], (SF, D), jnp.float32) * w}
    _L0_ffn_all = _L0_ffn_setup()
    _L0_ffn_in = {k: v for k, v in _L0_ffn_all.items() if k in ('router_w', 'w_gate', 'w_up', 'w_down', 'ws_gate_up', 'ws_down')}
    del _L0_ffn_all

    def _L1_attn_setup():
        import math
        import jax, jax.numpy as jnp
        import numpy as np
        DIM = 256
        DIM_QK = 128
        DIM_V = 256
        CHUNK = 128
        NUM_BUCKETS = 32
        MAX_DISTANCE = 128

        def _rel_pos_bucket(n_q, n_k):
            q_pos = jnp.arange(n_q, dtype=jnp.int32)
            k_pos = jnp.arange(n_k, dtype=jnp.int32)
            rel = k_pos[None, :] - q_pos[:, None]
            n = jnp.maximum(-rel, 0)
            max_exact = NUM_BUCKETS // 2
            is_small = n < max_exact
            n_f = jnp.maximum(n, 1).astype(jnp.float32)
            val_large = max_exact + jnp.log(n_f / max_exact) / math.log(MAX_DISTANCE / max_exact) * (NUM_BUCKETS - max_exact)
            val_large = jnp.minimum(val_large, NUM_BUCKETS - 1)
            bucket = jnp.where(is_small, n.astype(jnp.float32), val_large)
            return bucket.astype(jnp.int32)
        key = jax.random.key(seed)
        ks = jax.random.split(key, 6)
        b, s = (8, 1024)
        x = jax.random.normal(ks[0], (b, s, DIM), dtype=jnp.float32)
        Wqk = jax.random.normal(ks[1], (DIM, DIM_QK), dtype=jnp.float32) * (1.0 / math.sqrt(DIM))
        bqk = jnp.zeros((DIM_QK,), dtype=jnp.float32)
        Wv = jax.random.normal(ks[2], (DIM, DIM_V), dtype=jnp.float32) * (1.0 / math.sqrt(DIM))
        bv = jnp.zeros((DIM_V,), dtype=jnp.float32)
        gamma = jax.random.normal(ks[3], (2, DIM_QK), dtype=jnp.float32) * 0.02
        beta = jnp.zeros((2, DIM_QK), dtype=jnp.float32)
        rel_emb = jax.random.normal(ks[4], (NUM_BUCKETS, 1), dtype=jnp.float32) * 0.05
        return {'x': x, 'Wqk': Wqk, 'bqk': bqk, 'Wv': Wv, 'bv': bv, 'gamma': gamma, 'beta': beta, 'rel_emb': rel_emb}
    _L1_attn_all = _L1_attn_setup()
    _L1_attn_in = {k: v for k, v in _L1_attn_all.items() if k in ('Wqk', 'bqk', 'Wv', 'bv', 'gamma', 'beta', 'rel_emb')}
    del _L1_attn_all

    def _L1_ffn_setup():
        import jax, jax.numpy as jnp
        import numpy as np
        TOP_K = 2
        key = jax.random.key(seed)
        ks = jax.random.split(key, 6)
        B, T, H, E, F = (2, 512, 256, 8, 1024)
        s = 0.02
        return {'hidden_states': jax.random.normal(ks[0], (B, T, H), dtype=jnp.float32), 'router_w': jax.random.normal(ks[1], (E, H), dtype=jnp.float32) * s, 'w1': jax.random.normal(ks[2], (E, F, H), dtype=jnp.float32) * s, 'b1': jax.random.normal(ks[3], (E, F), dtype=jnp.float32) * s, 'w2': jax.random.normal(ks[4], (E, H, F), dtype=jnp.float32) * s, 'b2': jax.random.normal(ks[5], (E, H), dtype=jnp.float32) * s}
    _L1_ffn_all = _L1_ffn_setup()
    _L1_ffn_in = {k: v for k, v in _L1_ffn_all.items() if k in ('router_w', 'w1', 'b1', 'w2', 'b2')}
    del _L1_ffn_all
    return {'x': x, 'L0_tok_W': _L0_tok_in['W'], 'L0_tok_gamma': _L0_tok_in['gamma'], 'L0_attn_w_in': _L0_attn_in['w_in'], 'L0_attn_b_in': _L0_attn_in['b_in'], 'L0_attn_w_out': _L0_attn_in['w_out'], 'L0_attn_b_out': _L0_attn_in['b_out'], 'L0_ffn_router_w': _L0_ffn_in['router_w'], 'L0_ffn_w_gate': _L0_ffn_in['w_gate'], 'L0_ffn_w_up': _L0_ffn_in['w_up'], 'L0_ffn_w_down': _L0_ffn_in['w_down'], 'L0_ffn_ws_gate_up': _L0_ffn_in['ws_gate_up'], 'L0_ffn_ws_down': _L0_ffn_in['ws_down'], 'L1_attn_Wqk': _L1_attn_in['Wqk'], 'L1_attn_bqk': _L1_attn_in['bqk'], 'L1_attn_Wv': _L1_attn_in['Wv'], 'L1_attn_bv': _L1_attn_in['bv'], 'L1_attn_gamma': _L1_attn_in['gamma'], 'L1_attn_beta': _L1_attn_in['beta'], 'L1_attn_rel_emb': _L1_attn_in['rel_emb'], 'L1_ffn_router_w': _L1_ffn_in['router_w'], 'L1_ffn_w1': _L1_ffn_in['w1'], 'L1_ffn_b1': _L1_ffn_in['b1'], 'L1_ffn_w2': _L1_ffn_in['w2'], 'L1_ffn_b2': _L1_ffn_in['b2']}

def reference(x, L0_tok_W, L0_tok_gamma, L0_attn_w_in, L0_attn_b_in, L0_attn_w_out, L0_attn_b_out, L0_ffn_router_w, L0_ffn_w_gate, L0_ffn_w_up, L0_ffn_w_down, L0_ffn_ws_gate_up, L0_ffn_ws_down, L1_attn_Wqk, L1_attn_bqk, L1_attn_Wv, L1_attn_bv, L1_attn_gamma, L1_attn_beta, L1_attn_rel_emb, L1_ffn_router_w, L1_ffn_w1, L1_ffn_b1, L1_ffn_w2, L1_ffn_b2):
    import jax
    import jax.numpy as jnp

    def _L0_tok_ref(x, W, gamma):
        import jax, jax.numpy as jnp
        import numpy as np
        PATCH = 8
        EPS = 1e-05

        def _patchify(x):
            B, C, H, Wd = x.shape
            p = PATCH
            x = x.reshape(B, C, H // p, p, Wd // p, p)
            x = x.transpose(0, 2, 4, 1, 3, 5)
            return x.reshape(B, H // p * (Wd // p), C * p * p)
        tokens = _patchify(x)
        h = jnp.einsum('bnf,fd->bnd', tokens, W)
        mu = jnp.mean(h, axis=-1, keepdims=True)
        var = jnp.mean(jnp.square(h - mu), axis=-1, keepdims=True)
        out = (h - mu) * jax.lax.rsqrt(var + EPS) * gamma
        return out

    def _L0_attn_ref(x, w_in, b_in, w_out, b_out):
        import math
        import jax, jax.numpy as jnp
        import numpy as np
        N_HEADS = 16
        D_EMBED = 256
        b, l, d = x.shape
        h = N_HEADS
        scale = 1.0 / math.sqrt(d // h)
        x_proj = (x @ w_in.T + b_in).reshape(b, l, h, -1)
        q, k, v = jnp.split(x_proj, 3, axis=-1)
        att = jnp.einsum('blhd,bmhd->blmh', q, k) * scale
        att = jax.nn.softmax(att, axis=2)
        opt = jnp.einsum('blmh,blhd->blhd', att, v).reshape(b, l, d)
        return opt @ w_out.T + b_out

    def _L0_ffn_ref(hidden_states, router_w, w_gate, w_up, w_down, ws_gate_up, ws_down):
        import jax, jax.numpy as jnp
        import numpy as np
        B, S, D = (1, 512, 256)
        E, K, F = (64, 8, 192)
        SF = 192
        C = 128
        ROUTED_SCALE = 1.0

        def _moe_forward(x, router_w, w_gate, w_up, w_down, ws_gate_up, ws_down):
            T = x.shape[0]
            logits = x.astype(jnp.float32) @ router_w.T
            probs = jax.nn.softmax(logits, axis=-1)
            topk_w, topk_ids = jax.lax.top_k(probs, K)
            topk_w = topk_w / jnp.sum(topk_w, axis=-1, keepdims=True)
            topk_w = topk_w.astype(x.dtype)
            N = T * K
            flat_e = topk_ids.reshape(-1)
            flat_w = topk_w.reshape(-1)
            tok = jnp.arange(N) // K
            onehot = flat_e[:, None] == jnp.arange(E)[None, :]
            pos = jnp.cumsum(onehot, axis=0)[jnp.arange(N), flat_e] - 1
            valid = pos < C
            idx = jnp.where(valid, flat_e * C + pos, E * C)
            x_buf = jnp.zeros((E * C + 1, x.shape[1]), x.dtype).at[idx].set(x[tok])
            xb = x_buf[:E * C].reshape(E, C, -1)
            g = jnp.einsum('ecd,edf->ecf', xb, w_gate)
            u = jnp.einsum('ecd,edf->ecf', xb, w_up)
            h = jax.nn.silu(g) * u
            y = jnp.einsum('ecf,efd->ecd', h, w_down).reshape(E * C, -1)
            safe = jnp.where(valid, idx, 0)
            contrib = y[safe] * (flat_w * valid.astype(flat_w.dtype))[:, None]
            routed = jax.ops.segment_sum(contrib, tok, num_segments=T)
            routed = routed * ROUTED_SCALE
            gu = x @ ws_gate_up
            sg, su = (gu[:, :SF], gu[:, SF:])
            shared = jax.nn.silu(sg) * su @ ws_down
            return routed + shared
        b, s, d = hidden_states.shape
        x = hidden_states.reshape(-1, d)
        out = _moe_forward(x, router_w, w_gate, w_up, w_down, ws_gate_up, ws_down)
        return out.reshape(b, s, d)

    def _L1_attn_ref(x, Wqk, bqk, Wv, bv, gamma, beta, rel_emb):
        import math
        import jax, jax.numpy as jnp
        import numpy as np
        DIM = 256
        DIM_QK = 128
        DIM_V = 256
        CHUNK = 128
        NUM_BUCKETS = 32
        MAX_DISTANCE = 128

        def _rel_pos_bucket(n_q, n_k):
            q_pos = jnp.arange(n_q, dtype=jnp.int32)
            k_pos = jnp.arange(n_k, dtype=jnp.int32)
            rel = k_pos[None, :] - q_pos[:, None]
            n = jnp.maximum(-rel, 0)
            max_exact = NUM_BUCKETS // 2
            is_small = n < max_exact
            n_f = jnp.maximum(n, 1).astype(jnp.float32)
            val_large = max_exact + jnp.log(n_f / max_exact) / math.log(MAX_DISTANCE / max_exact) * (NUM_BUCKETS - max_exact)
            val_large = jnp.minimum(val_large, NUM_BUCKETS - 1)
            bucket = jnp.where(is_small, n.astype(jnp.float32), val_large)
            return bucket.astype(jnp.int32)
        b, s, dim = x.shape
        qk = jax.nn.swish(x @ Wqk + bqk)
        v = jax.nn.swish(x @ Wv + bv)
        os = qk[..., None, :] * gamma + beta
        q, k = (os[..., 0, :], os[..., 1, :])
        c = CHUNK
        nk = s // c
        q = q.reshape(b, nk, c, DIM_QK)
        k = k.reshape(b, nk, c, DIM_QK)
        vc = v.reshape(b, nk, c, DIM_V)
        scale = dim ** (-0.5)
        sim = jnp.einsum('bkiz,bkjz->bkij', q, k) * scale
        bucket = _rel_pos_bucket(c, c)
        bias = rel_emb[bucket, 0] * DIM_QK ** 0.5
        sim = sim + bias
        future = jnp.triu(jnp.ones((c, c), dtype=bool), k=1)
        sim = jnp.where(future, -jnp.inf, sim)
        attn = jax.nn.softmax(sim, axis=-1)
        out = jnp.einsum('bkij,bkjz->bkiz', attn, vc)
        return out.reshape(b, s, DIM_V)

    def _L1_ffn_ref(hidden_states, router_w, w1, b1, w2, b2):
        import jax, jax.numpy as jnp
        import numpy as np
        TOP_K = 2
        x = hidden_states
        router_logits = jnp.einsum('bth,eh->bte', x, router_w)
        topk_values, topk_indices = jax.lax.top_k(router_logits, TOP_K)
        topk_weights = jax.nn.softmax(topk_values.astype(jnp.float32), axis=-1).astype(x.dtype)
        h1 = jnp.einsum('bth,efh->btef', x, w1) + b1
        h1 = jax.nn.gelu(h1, approximate=False)
        expert_outputs = jnp.einsum('btef,ehf->bteh', h1, w2) + b2
        gather_idx = topk_indices[..., None]
        topk_expert_outputs = jnp.take_along_axis(expert_outputs, gather_idx, axis=2)
        mixed_output = jnp.sum(topk_expert_outputs * topk_weights[..., None], axis=2)
        return mixed_output
    h = _L0_tok_ref(x, L0_tok_W, L0_tok_gamma)
    h = h + _L0_attn_ref(_layernorm(h, axis=-1), L0_attn_w_in, L0_attn_b_in, L0_attn_w_out, L0_attn_b_out)
    h = h + _L0_ffn_ref(_layernorm(h, axis=-1), L0_ffn_router_w, L0_ffn_w_gate, L0_ffn_w_up, L0_ffn_w_down, L0_ffn_ws_gate_up, L0_ffn_ws_down)
    h = h + _L1_attn_ref(_layernorm(h, axis=-1), L1_attn_Wqk, L1_attn_bqk, L1_attn_Wv, L1_attn_bv, L1_attn_gamma, L1_attn_beta, L1_attn_rel_emb)
    h = h + _L1_ffn_ref(_layernorm(h, axis=-1), L1_ffn_router_w, L1_ffn_w1, L1_ffn_b1, L1_ffn_w2, L1_ffn_b2)
    return h

_drawn_inputs = setup_inputs


def setup_inputs(seed=0):
    import zlib

    import numpy as np

    out = dict(_drawn_inputs(seed))
    spreads = {'L0_tok_gamma': (1.0, 0.2),
     'L1_attn_bqk': (0.0, 2.0),
     'L1_attn_bv': (0.0, 0.8),
     'L1_attn_beta': (0.0, 2.0)}
    factors = {'L0_attn_b_in': 5.19,
     'L0_ffn_router_w': 8.0,
     'L0_ffn_w_gate': 7.75,
     'L0_ffn_w_up': 7.556,
     'L0_ffn_w_down': 8.0,
     'L0_ffn_ws_gate_up': 3.479,
     'L0_ffn_ws_down': 3.482,
     'L1_attn_Wqk': 50.697,
     'L1_attn_gamma': 46.052,
     'L1_ffn_b1': 64.0,
     'L1_ffn_b2': 22.928,
     'L1_attn_rel_emb': 17.966,
     'L1_ffn_router_w': 3.697,
     'L1_ffn_w1': 4.313,
     'L1_ffn_w2': 3.799}
    for name, (base, spread) in spreads.items():
        noise = np.random.default_rng([zlib.crc32(name.encode()), seed]).standard_normal(out[name].shape)
        drawn = base * np.exp(spread * noise) if base else spread * noise
        out[name] = jnp.asarray(drawn.astype(out[name].dtype))
    for name, factor in factors.items():
        out[name] = (out[name] * factor).astype(out[name].dtype)
    return out
```

```python
from contextlib import ExitStack

import numpy as np

import concourse.bass as bass
from concourse import mybir

F32 = mybir.dt.float32
I32 = mybir.dt.int32
U32 = mybir.dt.uint32
ALU = mybir.AluOpType
ACT = mybir.ActivationFunctionType
AX_X = mybir.AxisListType.X

P = 128
D = 256
KD = D // P
T = 512
NT = T // P
PATCH = 8
FEAT = 5 * PATCH * PATCH
EPS = 1e-5

HEADS, HD = 16, 16
SEQ = 256
PAIRS = HEADS // 2
ATT_SCALE = 1.0 / HD ** 0.5

E0, K0, F0, CAP = 64, 8, 192, 128
FH = F0 // 2
GU = KD * 2 * F0
DN = 2 * D
RING = 4
DROPPED = E0 * CAP
BA, BB = 16, 8

ZQK = 128
L1_SCALE = D ** -0.5
BUCKETS, MAX_DISTANCE = 32, 128

E1, K1, F1 = 8, 2, 1024
KF = F1 // P
TILES1 = (K1 * T + E1 * (P - 1)) // P
CB = 16
FAR = 1023.0
NEG = -1e30

C_IDENT, C_UPPER, C_ONES, C_EXP0, C_EXP1, C_ROW128 = (i * P for i in range(6))
C_DIAG = 6 * P
C_LOW0 = C_DIAG + 64
C_IOTA16 = C_LOW0 + BB
C_TOK = C_IOTA16 + 16
C_BASE = C_TOK + NT
C_TILE = C_BASE + E0
C_LOW1 = C_TILE + 16
C_PAIR = C_LOW1 + CB
C_128J = C_PAIR + 2
C_ALL = C_128J + 16


def constants():
    c = np.zeros((P, C_ALL), np.float32)
    p = np.arange(P)[:, None]
    s = np.arange(P)[None, :]
    c[:, C_IDENT:C_IDENT + P] = p == s
    c[:, C_UPPER:C_UPPER + P] = p < s
    c[:, C_ONES:C_ONES + P] = 1
    c[:, C_EXP0:C_EXP0 + P] = p % BA == s // BB
    c[:, C_EXP1:C_EXP1 + P] = p % 8 == s // CB
    c[:, C_ROW128:C_ROW128 + P] = s
    c[:, C_DIAG:C_DIAG + 64] = p // BA == np.arange(64)[None, :] // BB
    c[:, C_LOW0:C_LOW0 + BB] = np.arange(BB)[None, :] == p % BB
    c[:, C_IOTA16:C_IOTA16 + 16] = np.arange(16)
    c[:, C_TOK:C_TOK + NT] = p + P * np.arange(NT)[None, :]
    c[:, C_BASE:C_BASE + E0] = CAP * np.arange(E0)
    c[:, C_TILE:C_TILE + 16] = p // 8 == np.arange(16)[None, :]
    c[:, C_LOW1:C_LOW1 + CB] = np.arange(CB)[None, :] == p % CB
    c[:, C_PAIR:C_PAIR + 2] = (p // HD) % 2 == np.arange(2)[None, :]
    c[:, C_128J:C_128J + 16] = P * np.arange(16)
    return c


def bucket_rows():
    out = np.zeros((BUCKETS + 1, 2 * P), np.float32)
    n = np.arange(P)
    exact = BUCKETS // 2
    far = exact + (np.log((np.maximum(n, 1).astype(np.float32) / np.float32(exact)))
                   / np.float32(np.log(MAX_DISTANCE / exact)) * np.float32(BUCKETS - exact))
    far = np.minimum(far, BUCKETS - 1)
    b = np.where(n < exact, n.astype(np.float32), far).astype(np.int32)
    out[b, P - 1 - n] = 1
    out[BUCKETS, P:] = NEG
    return out


def vit_tower(nc, x_in, tok_w, gamma, consts, buckets, w_in, bq_in, bk_in, bv_in, w_out, b_out,
              router0, gate_up, down, shared_gu, shared_dn, wqk, bqk, wv, bv1, gam1, bet1, rel,
              router1, w1, w2, b1, b2, out):
    rows0 = nc.dram_tensor("rows0", (T, D), F32).ap()
    rows1 = nc.dram_tensor("rows1", (T, D), F32).ap()
    y0 = nc.dram_tensor("y0", (E0 * CAP + 1, D), F32).ap()
    y1 = nc.dram_tensor("y1", (TILES1 * P, D), F32).ap()
    bias_rows = nc.dram_tensor("bias_rows", (P, 2 * P), F32).ap()

    with ExitStack() as ctx:
        def sb(name, shape, dt=F32):
            return ctx.enter_context(nc.sbuf_tensor(name, shape, dt))

        def sem(name):
            return ctx.enter_context(nc.semaphore(name))

        ps = [ctx.enter_context(nc.psum_tensor(f"bank{i}", [P, 512], F32)) for i in range(8)]

        w1_sb = sb("w1_sb", [P, E1 * KD * F1])
        w2_sb = sb("w2_sb", [P, E1 * KF * D])
        ring_gu = [sb(f"ring_gu{u}", [P, GU]) for u in range(RING)]
        ring_dn = [sb(f"ring_dn{u}", [FH, DN]) for u in range(RING)]
        con = sb("con", [P, C_ALL])
        gamma_bc = sb("gamma_bc", [P, D])
        wout_sb = sb("wout_sb", [P, KD * D])
        r0_sb = sb("r0_sb", [P, KD * E0])
        bqk0 = sb("bqk0", [P, 4])
        wqk_sb = sb("wqk_sb", [P, KD * ZQK])
        wv_sb = sb("wv_sb", [P, KD * D])
        bv1_bc = sb("bv1_bc", [P, D])
        r1_sb = sb("r1_sb", [P, KD * E1])
        z_cols = sb("z_cols", [P, 5])
        b1_sb = sb("b1_sb", [P, E1 * KF])
        bias1 = sb("bias1", [P, P])
        h = sb("h", [P, NT, D])
        a = sb("a", [P, NT, D])
        aT = sb("aT", [P, KD, T])
        stats = sb("stats", [P, NT, 6])
        mv = sb("mv", [P, NT, 2])
        std = sb("std", [P, NT])
        rstd = sb("rstd", [P, NT])
        pool = sb("pool", [P, 8192])

        hidT_bvec = sb("hidT_bvec", [P, 2 * D])

        def at(start, *dims, parts=P):
            n = int(np.prod(dims))
            v = pool[0:parts, start:start + n]
            if len(dims) == 1:
                return v
            names = "abcd"[:len(dims)]
            return v.rearrange(f"p ({' '.join(names)}) -> p {' '.join(names)}",
                               **{k: d for k, d in zip(names[1:], dims[1:])})

        ident = con[:, C_IDENT:C_IDENT + P]
        upper = con[:, C_UPPER:C_UPPER + P]
        ones = con[:, C_ONES:C_ONES + P]

        bvec_bc = hidT_bvec
        small = at(7936, 2 * P)
        xa = at(0, KD, T)
        xb = at(1024, T, parts=FEAT - KD * P)
        wa = at(1536, KD, D)
        wb = at(2048, D, parts=FEAT - KD * P)
        win = at(2304, KD, 3 * D)
        qT = at(3840, KD, T)
        kT = at(4864, 2, KD, T)
        v0 = at(6912, NT, D)
        prob = at(0, 4, D)
        mx, nmx, esum, erec = (at(1024 + 64 * n, NT * HEADS) for n in range(4))
        opt = at(1536, NT, D)
        optT = at(2560, KD, T)

        lg = at(0, NT, E0)
        rp = at(256, NT, E0)
        mask = at(512, NT, E0)
        pr = at(768, NT, E0)
        wt = at(1024, NT, E0)
        kept = at(1280, NT, E0)
        t1 = at(1536, NT, E0)
        key = at(1792, NT, E0)
        digit_a = at(2048, NT, E0)
        digit_b = at(2304, NT, E0)
        top8 = sb("top8", [P, NT, 8])
        r_small = sb("r_small", [P, 6 * NT])
        slot_i = at(7936, NT * E0).bitcast(I32)
        dig_i = at(0, NT * E0).bitcast(I32)
        take0 = sb("take0", [P, NT * K0], I32)
        oneA = at(2560, 2, E0, BA)
        oneB = at(4608, E0, BB)
        rhsB = at(5120, 2, 8, 2, 64)
        mid = at(2560, 2, 512)
        sel = at(4608, 2, 64, BB)
        picked = at(3584, 8, 2, 8)
        tok0 = sb("tok0", [P, E0], I32)
        wsl0 = sb("wsl0", [P, E0])

        sil = at(7168, 2, F0)
        hid = at(7552, 2, F0)
        hidT = hidT_bvec[0:FH, :].rearrange("p (a b) -> p a b", a=2)
        xg = at(0, 4, D)
        xTs = at(1024, 2, KD, P)
        yb = at(1536, 4, D)
        acc_in = at(0, 8, D)
        idx_ring = sb("idx_ring", [P, 4], I32)

        z = at(2048, NT, P)
        qz = at(2560, NT, P)
        kz = at(3072, NT, P)
        v1 = at(3584, NT, D)
        sc = at(4608, NT, P)
        pT = at(5120, NT, P)
        m1 = sb("m1", [P, NT])
        s1 = sb("s1", [P, NT])
        i1 = sb("i1", [P, NT])
        lg1 = at(4608, NT, E1)
        mask1 = at(4640, NT, E1)
        pos1 = at(4672, NT, E1)
        addr1 = at(4704, NT, E1)
        tmp1 = at(4736, NT, E1)
        cnt = at(4768, 4, E1)
        start1 = at(4800, 3, E1)
        hot = at(4832, NT, K1, E1)
        ad = at(4896, NT, K1)
        ww = at(4904, NT, 4)
        oneA1 = at(0, NT, K1, P)
        rhsB1 = at(1024, NT, K1, 2, CB)
        mid1 = at(1280, 2, 16, CB)
        sel1 = at(4928, 2, 16, CB)
        picked1 = at(5440, 2, 16)
        tend = at(5472, 16, E1)
        ecol = at(5600, 16)
        idx8 = sb("idx8", [P, NT, 8], U32)
        adr_i = sb("adr_i", [P, NT * K1], I32)
        dga = sb("dga", [P, NT * K1], I32)
        tok1 = sb("tok1", [P, 16], I32)
        wsl1 = sb("wsl1", [P, 16])
        tile_e = sb("tile_e", [P, 16], I32)
        b2_bc = at(6144, E1 * D)
        b1j = sb("b1j", [P, 2, KF])
        xg1 = at(0, 2, D)
        xT1 = at(512, 2, KD, P)
        h1s = at(1024, F1)
        hT1 = at(2048, KF, P)
        y_t = at(3072, D)
        yb1 = at(3328, 2, D)
        acc_in1 = at(4096, 8, D)

        buck_sb = at(3840, 2 * P, parts=BUCKETS + 1)
        rel_sb = sb("rel_sb", [BUCKETS + 1, 1])

        names = """tok_in con_in attn_in late_in b2_in ffn_in rows0_out zero_set zero_out rows1_out
            bias_mm bias_sb bias_out bias_in fin_out
            tok_mm var_ready std_ready rows_ready T_mm T_sb q_mm k_mm v_mm q_ready kcol_ready k_ready v_ready
            score_mm max_done exp_done hb_ready proj_mm h1_ready
            log0_mm nmax_ready soft_done mask_ready pos_mm digits_ready disp_mm mid_ready
            slot_mm slots_ready s_gu s_silu s_hid s_hT s_hTs s_dn s_res
            xT_mm xT_sb gu_mm silu_done hid_done hT_mm hT_sb y_mm y_sb idx_ready gathers
            h2_ready z_mm z_ready qk1_ready v1_mm vb_ready v1_ready sim_mm nm_ready p_done p_T
            pT_ready o_mm h3_ready
            log1_mm nm1_ready ex1_done mask1_ready pos1_mm hot1_ready disp1_mm mid1_ready slot1_mm
            slots1_ready g_xT g_xTs g_h1 g_h1s g_hT g_gelu g_y g_yt g_ysb g_b1 g_idx final_ready
            dve_chain""".split()
        s = {n: sem(n) for n in names}
        (tok_in, con_in, attn_in, late_in, b2_in, ffn_in, rows0_out, zero_set, zero_out, rows1_out,
         bias_mm, bias_sb, bias_out, bias_in, fin_out,
         tok_mm, var_ready, std_ready, rows_ready, T_mm, T_sb, q_mm, k_mm, v_mm, q_ready, kcol_ready, k_ready, v_ready,
         score_mm, max_done, exp_done, hb_ready, proj_mm, h1_ready,
         log0_mm, nmax_ready, soft_done, mask_ready, pos_mm, digits_ready, disp_mm, mid_ready,
         slot_mm, slots_ready, s_gu, s_silu, s_hid, s_hT, s_hTs, s_dn, s_res,
         xT_mm, xT_sb, gu_mm, silu_done, hid_done, hT_mm, hT_sb, y_mm, y_sb, idx_ready, gathers,
         h2_ready, z_mm, z_ready, qk1_ready, v1_mm, vb_ready, v1_ready, sim_mm, nm_ready, p_done, p_T,
         pT_ready, o_mm, h3_ready,
         log1_mm, nm1_ready, ex1_done, mask1_ready, pos1_mm, hot1_ready, disp1_mm, mid1_ready, slot1_mm,
         slots1_ready, g_xT, g_xTs, g_h1, g_h1s, g_hT, g_gelu, g_y, g_yt, g_ysb, g_b1, g_idx, final_ready,
         dve_chain) = s.values()
        ring_in = [sem(f"ring_in{u}") for u in range(RING)]
        xg_in = [sem(f"xg_in{u}") for u in range(4)]
        y_out = [sem(f"y_out{u}") for u in range(4)]
        take_in = [sem(f"take_in{u}") for u in range(8)]
        g_in = [sem(f"g_in{u}") for u in range(2)]
        g_out = [sem(f"g_out{u}") for u in range(2)]
        take1_in = [sem(f"take1_in{u}") for u in range(8)]

        def tile(i):
            return slice(i * P, (i + 1) * P)

        def spread(ap, axis, n):
            v = ap.unsqueeze(axis)
            shape = list(v.shape)
            shape[axis] = n
            return v.broadcast_to(shape)

        def ptr(tensor, start, size=1):
            return tensor[:, bass.ds(start, size)]

        block = ctx.enter_context(nc.Block())

        @block.sync
        def _(sp):
            sp.dma_start(xa, x_in[0:KD * P, :].rearrange("(k p) t -> p k t", p=P)).then_inc(tok_in, 16)
            sp.dma_start(wa, tok_w[0:KD * P, :].rearrange("(k p) d -> p k d", p=P)).then_inc(tok_in, 16)
            sp.dma_start(xb, x_in[KD * P:FEAT, :]).then_inc(tok_in, 16)
            sp.dma_start(wb, tok_w[KD * P:FEAT, :]).then_inc(tok_in, 16)
            sp.dma_start(win, w_in).then_inc(attn_in, 16)
            sp.dma_start(wout_sb[:, :], w_out).then_inc(attn_in, 16)
            sp.dma_start(r0_sb[:, :], router0).then_inc(attn_in, 16)

            def load_expert(e, u):
                sp.dma_start(ring_gu[u][:, :], gate_up[bass.ds(e, 1), :, :].squeeze(0)).then_inc(ring_in[u], 16)
                sp.dma_start(ring_dn[u][:, :], down[bass.ds(e, 1), :, :].squeeze(0)).then_inc(ring_in[u], 16)

            sp.dma_start(ring_gu[RING - 1][:, :], shared_gu).then_inc(ring_in[RING - 1], 16)
            sp.dma_start(ring_dn[RING - 1][:, :], shared_dn).then_inc(ring_in[RING - 1], 16)
            for e in range(RING - 1):
                load_expert(e, e)
            for e in range(E1):
                sp.dma_start(w1_sb[:, e * KD * F1:(e + 1) * KD * F1], w1[e]).then_inc(ffn_in, 16)
                sp.dma_start(w2_sb[:, e * KF * D:(e + 1) * KF * D], w2[e]).then_inc(ffn_in, 16)
            sp.wait_ge(s_dn, NT)
            load_expert(RING - 1, RING - 1)

            def store_y(e, u):
                sp.wait_ge(y_sb, e + 3)
                sp.dma_start(y0[bass.ds(e * CAP, CAP), :], yb[:, u, :]).then_inc(y_out[u], 16)

            with sp.Fori(0, E0 // RING - 1) as it:
                for u in range(RING):
                    e = sp.snap(it * RING + u)
                    store_y(e, u)
                    sp.wait_ge(y_mm, e + 3)
                    load_expert(e + RING, u)
            for u in range(RING):
                store_y(E0 - RING + u, u)

            def store_y1(j):
                sp.wait_ge(g_ysb, j + 3)
                sp.dma_start(y1[j * P:(j + 1) * P, :], yb1[:, j % 2, :]).then_inc(g_out[j % 2], 16)

            for j in range(TILES1):
                store_y1(j)
            for i in range(NT):
                sp.wait_ge(final_ready, K1 * (i + 1))
                sp.dma_start(out[tile(i), :], h[:, i, :]).then_inc(fin_out, 16)
            sp.wait_ge(fin_out, 16 * NT)

        @block.gpsimd
        def _(pool_e):
            pool_e.wait_ge(rows_ready, NT)
            pool_e.wait_ge(con_in, 16 * 6)
            nc.gpsimd.tensor_tensor(h[:, :, :], h[:, :, :], spread(bvec_bc[:, D:2 * D], 1, NT),
                                    ALU.add).then_inc(hb_ready, 1)

            def gather(e, u, value):
                nc.gpsimd.tensor_copy(idx_ring[:, u:u + 1], ptr(tok0, e)).then_inc(idx_ready, 1)
                pool_e.wait_ge(idx_ready, value)
                pool_e.sem_inc(gathers, 1)
                pool_e.indirect_dma_start(xg[:, u, :], None, rows0, bass.IndirectOffsetOnAxis(idx_ring[:, u:u + 1], 0),
                                          bounds_check=T - 1, oob_is_err=False).then_inc(xg_in[u], 16)

            pool_e.wait_ge(slots_ready, 1)
            pool_e.wait_ge(rows0_out, 16)
            pool_e.sem_inc(idx_ready, 1)
            for u in range(4):
                gather(u, u, u + 2)
            with pool_e.Fori(1, E0 // 4) as it:
                for u in range(4):
                    e = pool_e.snap(it * 4 + u)
                    pool_e.wait_ge(xT_mm, e + 1)
                    gather(e, u, e + 2)
            for u in range(4):
                pool_e.wait_ge(y_out[u], 16 * (E0 // 4 + 1))
            pool_e.wait_ge(zero_out, 16)
            for i in range(NT):
                for k in range(K0):
                    if i:
                        pool_e.wait_ge(h2_ready, K0 * (i - 1) + k + 1)
                    n = i * K0 + k
                    pool_e.indirect_dma_start(acc_in[:, k, :], None, y0, bass.IndirectOffsetOnAxis(take0[:, n:n + 1], 0),
                                              bounds_check=DROPPED, oob_is_err=False).then_inc(take_in[k], 16)

            def gather1(j, u, value):
                nc.gpsimd.tensor_copy(idx_ring[:, u:u + 1], ptr(tok1, j)).then_inc(g_idx, 1)
                pool_e.wait_ge(g_idx, value)
                pool_e.indirect_dma_start(xg1[:, u, :], None, rows1, bass.IndirectOffsetOnAxis(idx_ring[:, u:u + 1], 0),
                                          bounds_check=T - 1, oob_is_err=False).then_inc(g_in[u], 16)

            pool_e.wait_ge(slots1_ready, 1)
            pool_e.wait_ge(rows1_out, 16)
            for j in range(TILES1):
                if j >= 2:
                    pool_e.wait_ge(g_xT, j + 1)
                gather1(j, j % 2, j + 1)
            for u in range(2):
                pool_e.wait_ge(g_out[u], 16 * ((TILES1 + 1 - u) // 2 + 1))
            for n in range(NT * K1):
                pool_e.indirect_dma_start(acc_in1[:, n, :], None, y1, bass.IndirectOffsetOnAxis(adr_i[:, n:n + 1], 0),
                                          bounds_check=TILES1 * P - 1, oob_is_err=False).then_inc(take1_in[n], 16)

        @block.scalar
        def _(act):
            act.dma_start(con[:, :], consts).then_inc(con_in, 16)
            act.dma_start(gamma_bc[:, :], gamma.partition_broadcast(P)).then_inc(con_in, 16)
            act.dma_start(bvec_bc[:, 0:D], bv_in.partition_broadcast(P)).then_inc(con_in, 16)
            act.dma_start(bvec_bc[:, D:2 * D], b_out.partition_broadcast(P)).then_inc(con_in, 16)
            act.dma_start(bqk0[:, 0:2], bq_in).then_inc(attn_in, 16)
            act.dma_start(bqk0[:, 2:4], bk_in).then_inc(attn_in, 16)
            for dst, src in ((buck_sb[:, :], buckets), (rel_sb[0:BUCKETS, :], rel)):
                act.dma_start(dst, src).then_inc(con_in, 16)
            for dst, src in ((wqk_sb[:, :], wqk), (wv_sb[:, :], wv),
                             (bv1_bc[:, :], bv1.partition_broadcast(P)), (r1_sb[:, :], router1),
                             (z_cols[:, 0:1], bqk), (z_cols[:, 1:3], gam1), (z_cols[:, 3:5], bet1),
                             (b1_sb[:, :], b1)):
                act.dma_start(dst, src).then_inc(late_in, 16)
            act.wait_ge(zero_set, 1)
            act.dma_start(y0[DROPPED:DROPPED + 1, :], small[0:1, 0:D]).then_inc(zero_out, 16)

            def roots(layer, tiles):
                for i in tiles:
                    act.wait_ge(var_ready, layer * NT + i + 1)
                    nc.scalar.activation(std[:, i:i + 1], mv[:, i, 1:2], ACT.Sqrt).then_inc(std_ready, 1)

            roots(0, range(NT))
            act.wait_ge(bias_sb, 1)
            act.dma_start(bias_rows, small[:, 0:2 * P]).then_inc(bias_out, 16)
            roots(1, range(NT))
            act.wait_ge(bias_out, 16)
            act.dma_start(bias1[:, :], bass.AP(bias_rows.tensor, P - 1, [[2 * P - 1, P], [1, P]])).then_inc(bias_in, 16)
            act.wait_ge(kcol_ready, 1)
            for c in range(KD):
                act.wait_ge(k_mm, c + 1)
                for par in range(2):
                    nc.scalar.activation(kT[:, par, c, :], ps[2 + c][:, :], ACT.Identity,
                                         scale=con[:, C_PAIR + par:C_PAIR + par + 1],
                                         bias=small[:, 2 * par + c:2 * par + c + 1]).then_inc(k_ready, 1)
            for u in range(NT * PAIRS):
                act.wait_ge(max_done, u + 1)
                if u >= 2:
                    act.wait_ge(exp_done, 2 * u - 2)
                for par in range(2):
                    n = 2 * u + par
                    nc.scalar.activation(prob[:, n % 4, :], ps[u % 8][:, par * SEQ:(par + 1) * SEQ], ACT.Exp,
                                         scale=ATT_SCALE, bias=nmx[:, n:n + 1],
                                         accum_out=esum[:, n:n + 1]).then_inc(exp_done, 1)
            roots(2, range(NT))
            act.wait_ge(rows_ready, 3 * NT)
            act.dma_start(rows0.rearrange("(i p) d -> p i d", p=P), a[:, :, :]).then_inc(rows0_out, 16)
            for i in range(NT):
                act.wait_ge(nmax_ready, i + 1)
                nc.scalar.activation(pr[:, i, :], lg[:, i, :], ACT.Exp, bias=r_small[:, i:i + 1],
                                     accum_out=r_small[:, NT + i:NT + i + 1]).then_inc(soft_done, 1)

            for i in range(NT):
                act.wait_ge(s_gu, i + 1)
                if i >= 2:
                    act.wait_ge(s_hid, i - 1)
                nc.scalar.activation(sil[:, i % 2, :], ps[i % 2][:, 0:F0], ACT.Silu).then_inc(s_silu, 1)
                act.wait_ge(s_hT, i + 1)
                if i >= 2:
                    act.wait_ge(s_dn, i - 1)
                nc.scalar.activation(hidT[:, i % 2, :], ps[2 + i % 2][0:FH, 0:D],
                                     ACT.Copy).then_inc(s_hTs, 1)

            act.sem_inc(hT_sb, 2)

            def silu(e, par):
                act.wait_ge(gu_mm, e + 3)
                act.wait_ge(hid_done, e + 1)
                nc.scalar.activation(sil[:, par, :], ps[par][:, 0:F0], ACT.Silu).then_inc(silu_done, 1)

            def turned(e, par):
                act.wait_ge(hT_mm, e + 3)
                act.wait_ge(y_mm, e + 1)
                nc.scalar.activation(hidT[:, par, :], ps[2 + par][0:FH, 0:D], ACT.Copy).then_inc(hT_sb, 1)

            silu(0, 0)
            with act.Fori(0, E0 // 4 - 1) as it:
                for u in range(4):
                    e = act.snap(it * 4 + u + 1)
                    turned(e - 1, u % 2)
                    silu(e, (u + 1) % 2)
            for e in range(E0 - 3, E0):
                turned(e - 1, (e - 1) % 2)
                silu(e, e % 2)
            turned(E0 - 1, (E0 - 1) % 2)

            act.dma_start(b2_bc, b2.partition_broadcast(P)).then_inc(b2_in, 16)

            for i in range(NT):
                roots(3, [i])
                act.wait_ge(z_mm, i + 1)
                nc.scalar.activation(z[:, i, :], ps[4 + i][:, 0:P], ACT.Silu, bias=z_cols[:, 0:1]).then_inc(z_ready, 1)
                act.wait_ge(vb_ready, i + 1)
                nc.scalar.activation(v1[:, i, :], v1[:, i, :], ACT.Silu).then_inc(v1_ready, 1)
            for i in range(NT):
                act.wait_ge(nm_ready, i + 1)
                nc.scalar.activation(sc[:, i, :], sc[:, i, :], ACT.Exp, bias=m1[:, i:i + 1],
                                     accum_out=s1[:, i:i + 1]).then_inc(p_done, 1)
            roots(4, range(NT))
            act.wait_ge(rows_ready, 5 * NT)
            act.dma_start(rows1.rearrange("(i p) d -> p i d", p=P), a[:, :, :]).then_inc(rows1_out, 16)
            for i in range(NT):
                act.wait_ge(nm1_ready, i + 1)
                nc.scalar.activation(ww[:, i, 0:K1], top8[:, i, 0:K1], ACT.Exp, bias=m1[:, i:i + 1],
                                     accum_out=ww[:, i, K1:K1 + 1]).then_inc(ex1_done, 1)

            act.sem_inc(g_gelu, 2)

            def gelu(j, par):
                act.wait_ge(g_b1, j + 1)
                act.wait_ge(g_y, j + 1)
                for n in range(2):
                    act.wait_ge(g_hT, 2 * j + n + 3)
                    for q in range(KF // 2):
                        f = n * (KF // 2) + q
                        ins = nc.scalar.activation(hT1[:, f, :], ps[2 + n][:, tile(q)], ACT.Gelu,
                                                   bias=b1j[:, par, f:f + 1])
                    ins.then_inc(g_gelu, 1)

            gelu(0, 0)
            with act.Fori(0, (TILES1 - 3) // 2) as it:
                for u in range(2):
                    gelu(act.snap(it * 2 + u + 1), (u + 1) % 2)
            for j in range(TILES1 - 2, TILES1):
                gelu(j, j % 2)

        @block.tensor
        def _(pe):
            def turn(stage, i, bank, src):
                pe.wait_ge(rows_ready, stage * NT + i + 1)
                for k in range(KD):
                    ins = nc.tensor.transpose(ps[bank][:, tile(k)], src[:, i, tile(k)], ident)
                ins.then_inc(T_mm, 1)

            pe.wait_ge(tok_in, 16 * 4)
            for i in range(NT):
                for k in range(KD):
                    nc.tensor.matmul(ps[i][:, 0:D], xa[:, k, tile(i)], wa[:, k, :], start=(k == 0), stop=False)
                nc.tensor.matmul(ps[i][:, 0:D], xb[:, tile(i)], wb, start=False, stop=True).then_inc(tok_mm, 1)
            pe.wait_ge(con_in, 16 * 6)
            pe.wait_ge(zero_set, 2)
            nc.tensor.matmul(ps[7][:, 0:2 * P], rel_sb[:, :].broadcast_to([BUCKETS + 1, P]), buck_sb[:, :], start=True, stop=True).then_inc(bias_mm, 1)
            pe.wait_ge(bias_sb, 1)
            for i in range(NT):
                turn(0, i, 4 + i, a)
            pe.wait_ge(T_sb, NT)
            pe.wait_ge(attn_in, 16 * 5)
            for which, done in ((0, q_mm), (1, k_mm)):
                for c in range(KD):
                    for k in range(KD):
                        lo = which * D + c * P
                        ins = nc.tensor.matmul(ps[2 * which + c][:, :], win[:, k, lo:lo + P], aT[:, k, :],
                                               start=(k == 0), stop=(k == KD - 1))
                    ins.then_inc(done, 1)
            for i in range(NT):
                for k in range(KD):
                    ins = nc.tensor.matmul(ps[4 + i][:, 0:D], aT[:, k, tile(i)], win[:, k, 2 * D:3 * D],
                                           start=(k == 0), stop=(k == KD - 1))
                ins.then_inc(v_mm, 1)

            pe.wait_ge(q_ready, KD)
            pe.wait_ge(k_ready, 2 * KD)
            pe.wait_ge(v_ready, NT)
            for u in range(NT * PAIRS):
                i, g = divmod(u, PAIRS)
                c, lo = g // 4, 32 * (g % 4)
                keys = slice((i // 2) * SEQ, (i // 2 + 1) * SEQ)
                if u >= 8:
                    pe.wait_ge(exp_done, 2 * (u - 8) + 2)
                for par in range(2):
                    ins = nc.tensor.matmul(ps[u % 8][:, par * SEQ:(par + 1) * SEQ], qT[lo:lo + 32, c, tile(i)],
                                           kT[lo:lo + 32, par, c, keys], start=True, stop=True)
                ins.then_inc(score_mm, 1)

            pe.wait_ge(exp_done, 2 * NT * PAIRS)
            for i in range(NT):
                turn(1, i, i, opt)
            for i in range(NT):
                pe.wait_ge(T_sb, NT + i + 1)
                for k in range(KD):
                    ins = nc.tensor.matmul(ps[4 + i][:, 0:D], optT[:, k, tile(i)], wout_sb[:, k * D:(k + 1) * D],
                                           start=(k == 0), stop=(k == KD - 1))
                ins.then_inc(proj_mm, 1)
            for i in range(NT):
                turn(2, i, i, a)
            for i in range(NT):
                pe.wait_ge(T_sb, 2 * NT + i + 1)
                for k in range(KD):
                    ins = nc.tensor.matmul(ps[4 + i][:, 0:E0], aT[:, k, tile(i)],
                                           r0_sb[:, k * E0:(k + 1) * E0], start=(k == 0), stop=(k == KD - 1))
                ins.then_inc(log0_mm, 1)

            def shared(i):
                u = RING - 1
                pe.wait_ge(ring_in[u], 32)
                if i >= 2:
                    pe.wait_ge(s_hid, i - 1)
                for k in range(KD):
                    ins = nc.tensor.matmul(ps[i % 2][:, 0:2 * F0], aT[:, k, tile(i)],
                                           ring_gu[u][:, k * 2 * F0:(k + 1) * 2 * F0], start=(k == 0), stop=(k == KD - 1))
                ins.then_inc(s_gu, 1)

            def shared_down(i):
                par, u = i % 2, RING - 1
                pe.wait_ge(s_hid, i + 1)
                for k in range(2):
                    ins = nc.tensor.transpose(ps[2 + par][0:FH, tile(k)],
                                              hid[:, par, k * FH:(k + 1) * FH], ident)
                ins.then_inc(s_hT, 1)
                pe.wait_ge(s_hTs, i + 1)
                if i >= 2:
                    pe.wait_ge(s_res, i - 1)
                for k in range(2):
                    ins = nc.tensor.matmul(ps[4 + par][:, 0:D], hidT[:, par, tile(k)],
                                           ring_dn[u][:, k * D:(k + 1) * D], start=(k == 0), stop=(k == 1))
                ins.then_inc(s_dn, 1)

            def positions(bank, m, width, done, wanted):
                pe.wait_ge(wanted, 1)
                for i in range(NT):
                    for b in range(i + 1):
                        ins = nc.tensor.matmul(ps[bank][:, i * width:(i + 1) * width], upper if b == i else ones,
                                               m[:, b, :], start=(b == 0), stop=(b == i))
                ins.then_inc(done, 1)

            for i in range(NT):
                shared(i)
                shared_down(i)
            positions(6, mask, E0, pos_mm, mask_ready)
            for i in range(NT):
                pe.wait_ge(digits_ready, i + 1)
                for g in range(8):
                    ins = nc.tensor.matmul(ps[4 + g // 4][:, tile(g % 4)],
                                           oneA[:, i % 2, 8 * g:8 * g + 8, :].rearrange("p a b -> p (a b)"),
                                           rhsB[:, i % 2, g, :, :].rearrange("p a b -> p (a b)"),
                                           start=(i == 0 and g % 4 == 0), stop=(i == NT - 1),
                                           skip_group_check=True)
                ins.then_inc(disp_mm, 1)
            pe.wait_ge(mid_ready, 1)
            for n in range(2):
                ins = nc.tensor.matmul(ps[6 + n][:, :], con[:, C_EXP0:C_EXP0 + P], mid[:, n, :], start=True, stop=True)
            ins.then_inc(slot_mm, 1)

            pe.wait_ge(s_res, NT)
            for done, credit in ((xT_mm, 4), (gu_mm, 2), (hT_mm, 2), (y_mm, 2)):
                pe.sem_inc(done, credit)

            def turn_x(e, u, turn_no):
                pe.wait_ge(xg_in[u], 16 * turn_no)
                pe.wait_ge(xT_sb, e + 1)
                for k in range(KD):
                    ins = nc.tensor.transpose(ps[6 + u % 2][:, tile(k)], xg[:, u, tile(k)], ident)
                ins.then_inc(xT_mm, 1)

            def gate_up_mm(e, u, turn_no):
                pe.wait_ge(ring_in[u], 32 * (turn_no + (1 if u == RING - 1 else 0)))
                pe.wait_ge(xT_sb, e + 3)
                pe.wait_ge(hid_done, e + 1)
                for k in range(KD):
                    ins = nc.tensor.matmul(ps[u % 2][:, 0:2 * F0], xTs[:, u % 2, k, :],
                                           ring_gu[u][:, k * 2 * F0:(k + 1) * 2 * F0], start=(k == 0), stop=(k == KD - 1))
                ins.then_inc(gu_mm, 1)

            def turn_h(e, u):
                pe.wait_ge(hid_done, e + 3)
                pe.wait_ge(hT_sb, e + 1)
                for k in range(2):
                    ins = nc.tensor.transpose(ps[2 + u % 2][0:FH, tile(k)], hid[:, u % 2, k * FH:(k + 1) * FH], ident)
                ins.then_inc(hT_mm, 1)

            def down_mm(e, u):
                pe.wait_ge(hT_sb, e + 3)
                pe.wait_ge(y_sb, e + 1)
                for k in range(2):
                    ins = nc.tensor.matmul(ps[4 + u % 2][:, 0:D], hidT[:, u % 2, tile(k)],
                                           ring_dn[u][:, k * D:(k + 1) * D], start=(k == 0), stop=(k == 1))
                ins.then_inc(y_mm, 1)

            turn_x(0, 0, 1)
            turn_x(1, 1, 1)
            gate_up_mm(0, 0, 1)
            with pe.Fori(0, E0 // 4 - 1) as it:
                for v in range(4):
                    e = pe.snap(it * 4 + v + 1)
                    turn_h(e - 1, v)
                    turn_x(e + 1, (v + 2) % 4, it + (v + 2) // 4 + 1)
                    gate_up_mm(e, (v + 1) % 4, it + (v + 1) // 4 + 1)
                    down_mm(e - 1, v)
            for e in range(E0 - 3, E0):
                turn_h(e - 1, (e - 1) % 4)
                if e + 1 < E0:
                    turn_x(e + 1, (e + 1) % 4, (e + 1) // 4 + 1)
                gate_up_mm(e, e % 4, e // 4 + 1)
                down_mm(e - 1, (e - 1) % 4)
            turn_h(E0 - 1, 3)
            down_mm(E0 - 1, 3)

            for i in range(NT):
                turn(3, i, i, a)
                pe.wait_ge(T_sb, 3 * NT + i + 1)
                for k in range(KD):
                    ins = nc.tensor.matmul(ps[4 + i][:, 0:P], wqk_sb[:, tile(k)], aT[:, k, tile(i)],
                                           start=(k == 0), stop=(k == KD - 1))
                ins.then_inc(z_mm, 1)
                for k in range(KD):
                    ins = nc.tensor.matmul(ps[i][:, 0:D], aT[:, k, tile(i)], wv_sb[:, k * D:(k + 1) * D],
                                           start=(k == 0), stop=(k == KD - 1))
                ins.then_inc(v1_mm, 1)
            for i in range(NT):
                pe.wait_ge(qk1_ready, 2 * (i + 1))
                nc.tensor.matmul(ps[4 + i][:, 0:P], qz[:, i, :], kz[:, i, :], start=True, stop=True).then_inc(sim_mm, 1)
            for i in range(NT):
                pe.wait_ge(p_done, i + 1)
                nc.tensor.transpose(ps[i][:, D:D + P], sc[:, i, :], ident).then_inc(p_T, 1)
                pe.wait_ge(pT_ready, i + 1)
                pe.wait_ge(v1_ready, i + 1)
                nc.tensor.matmul(ps[i][:, 0:D], pT[:, i, :], v1[:, i, :], start=True, stop=True).then_inc(o_mm, 1)
            for i in range(NT):
                turn(4, i, i, a)
            for i in range(NT):
                pe.wait_ge(T_sb, 4 * NT + i + 1)
                for k in range(KD):
                    ins = nc.tensor.matmul(ps[4 + i][:, 0:E1], aT[:, k, tile(i)],
                                           r1_sb[:, k * E1:(k + 1) * E1], start=(k == 0), stop=(k == KD - 1))
                ins.then_inc(log1_mm, 1)
            pe.wait_ge(mask1_ready, 1)
            for b in range(NT):
                nc.tensor.matmul(ps[5][:, NT * E1:(NT + 1) * E1], ones, mask1[:, b, :], start=(b == 0), stop=(b == NT - 1))
            positions(5, mask1, E1, pos1_mm, mask1_ready)
            pe.wait_ge(hot1_ready, 1)
            for n in range(NT * K1):
                i, k = divmod(n, K1)
                ins = nc.tensor.matmul(ps[6][:, 0:2 * CB], oneA1[:, i, k, :],
                                       rhsB1[:, i, k, :, :].rearrange("p a b -> p (a b)"),
                                       start=(n == 0), stop=(n == NT * K1 - 1))
            ins.then_inc(disp1_mm, 1)
            pe.wait_ge(mid1_ready, 1)
            nc.tensor.matmul(ps[7][:, :], con[:, C_EXP1:C_EXP1 + P], mid1.rearrange("p a b c -> p (a b c)"),
                             start=True, stop=True).then_inc(slot1_mm, 1)

            pe.wait_ge(slots1_ready, 1)
            pe.wait_ge(ffn_in, 16 * 2 * E1)
            for done, credit in ((g_xT, 2), (g_h1, 4), (g_hT, 2), (g_y, 1)):
                pe.sem_inc(done, credit)

            def turn_x1(j, par, turn_no):
                pe.wait_ge(g_in[par], 16 * turn_no)
                pe.wait_ge(g_xTs, j + 1)
                for k in range(KD):
                    ins = nc.tensor.transpose(ps[6 + par][:, tile(k)], xg1[:, par, tile(k)], ident)
                ins.then_inc(g_xT, 1)

            def expert_of(j):
                return pe.value_load(tile_e[0:1, bass.ds(j, 1)], min_val=0, max_val=E1 - 1)

            def first_mm(j, par):
                e = expert_of(j)
                pe.wait_ge(g_xTs, j + 3)
                for n in range(2):
                    pe.wait_ge(g_h1s, 2 * j + n + 1)
                    for k in range(KD):
                        ins = nc.tensor.matmul(ps[n][:, :], xT1[:, par, k, :],
                                               w1_sb[:, bass.ds(e * (KD * F1) + (k * F1 + n * 512), 512)],
                                               start=(k == 0), stop=(k == KD - 1))
                    ins.then_inc(g_h1, 1)

            def second_mm(j, par):
                e = expert_of(j)
                pe.wait_ge(g_gelu, 2 * j + 4)
                pe.wait_ge(g_ysb, j + 1)
                for f in range(KF):
                    ins = nc.tensor.matmul(ps[4 + par][:, 0:D], hT1[:, f, :],
                                           w2_sb[:, bass.ds(e * (KF * D) + f * D, D)], start=(f == 0), stop=(f == KF - 1))
                ins.then_inc(g_y, 1)

            def turn_h1(j):
                for n in range(2):
                    pe.wait_ge(g_h1s, 2 * j + n + 3)
                    pe.wait_ge(g_gelu, 2 * j + n + 1)
                    for q in range(KF // 2):
                        f = n * (KF // 2) + q
                        ins = nc.tensor.transpose(ps[2 + n][:, tile(q)], h1s[:, tile(f)], ident)
                    ins.then_inc(g_hT, 1)

            turn_x1(0, 0, 1)
            turn_x1(1, 1, 1)
            first_mm(0, 0)
            turn_h1(0)
            with pe.Fori(0, (TILES1 - 3) // 2) as it:
                for v in range(2):
                    j = pe.snap(it * 2 + v + 1)
                    turn_x1(j + 1, v, it + 2)
                    first_mm(j, (v + 1) % 2)
                    second_mm(j - 1, v)
                    turn_h1(j)
            for j in range(TILES1 - 2, TILES1):
                if j + 1 < TILES1:
                    turn_x1(j + 1, (j + 1) % 2, (j + 1) // 2 + 1)
                first_mm(j, j % 2)
                second_mm(j - 1, (j - 1) % 2)
                turn_h1(j)
            second_mm(TILES1 - 1, (TILES1 - 1) % 2)

        @block.vector
        def _(dve):
            count = [0]

            def link(ins):
                count[0] += 1
                ins.then_inc(dve_chain, 1)
                dve.wait_ge(dve_chain, count[0])

            V = nc.vector
            V.memset(small[:, :], 0.0).then_inc(zero_set, 1)
            V.memset(rel_sb[BUCKETS:BUCKETS + 1, :], 1.0).then_inc(zero_set, 1)

            def moments(layer, i, src):
                link(V.bn_stats(stats[:, i, :], src))
                link(V.bn_aggr(mv[:, i, :], stats[:, i, :]))
                V.tensor_scalar(mv[:, i, 1:2], mv[:, i, 1:2], EPS, None, ALU.add).then_inc(var_ready, 1)

            def normed(layer, i):
                dve.wait_ge(std_ready, layer * NT + i + 1)
                link(V.reciprocal(rstd[:, i:i + 1], std[:, i:i + 1]))
                V.tensor_scalar(a[:, i, :], h[:, i, :], mv[:, i, 0:1], rstd[:, i:i + 1],
                                ALU.subtract, ALU.mult).then_inc(rows_ready, 1)

            def turned(stage, i, bank, dst):
                dve.wait_ge(T_mm, stage * NT + i + 1)
                V.tensor_copy(dst[:, :, tile(i)], ps[bank][:, 0:KD * P].rearrange("p (k t) -> p k t", k=KD)).then_inc(T_sb, 1)

            for i in range(NT):
                dve.wait_ge(tok_mm, i + 1)
                moments(0, i, ps[i][:, 0:D])
            dve.wait_ge(con_in, 16 * 6)
            for i in range(NT):
                dve.wait_ge(std_ready, i + 1)
                V.scalar_tensor_tensor(h[:, i, :], ps[i][:, 0:D], mv[:, i, 0:1], gamma_bc[:, :], ALU.subtract, ALU.mult)
                link(V.reciprocal(rstd[:, i:i + 1], std[:, i:i + 1]))
                link(V.tensor_scalar(h[:, i, :], h[:, i, :], rstd[:, i:i + 1], None, ALU.mult))
            dve.wait_ge(bias_mm, 1)
            dve.wait_ge(zero_out, 16)
            V.tensor_scalar(small[:, 0:2 * P], ps[7][:, 0:2 * P], float(ZQK) ** 0.5, None, ALU.mult).then_inc(bias_sb, 1)
            for i in range(NT):
                moments(1, i, h[:, i, :])
            for i in range(NT):
                normed(1, i)
            for i in range(NT):
                turned(0, i, 4 + i, aT)
            dve.wait_ge(attn_in, 16 * 5)
            dve.wait_ge(bias_out, 16)
            for par in range(2):
                ins = V.tensor_scalar(small[:, 2 * par:2 * par + 2], bqk0[:, 2:4], con[:, C_PAIR + par:C_PAIR + par + 1], None, ALU.mult)
            ins.then_inc(kcol_ready, 1)
            for c in range(KD):
                dve.wait_ge(q_mm, c + 1)
                V.tensor_scalar(qT[:, c, :], ps[c][:, :], bqk0[:, c:c + 1], None, ALU.add).then_inc(q_ready, 1)
            for i in range(NT):
                dve.wait_ge(v_mm, i + 1)
                V.tensor_tensor(v0[:, i, :], ps[4 + i][:, 0:D], bvec_bc[:, 0:D], ALU.add).then_inc(v_ready, 1)

            def attended(i):
                cols = slice(i * HEADS, (i + 1) * HEADS)
                dve.wait_ge(exp_done, HEADS * (i + 1))
                link(V.reciprocal(erec[:, cols], esum[:, cols]))
                link(V.tensor_tensor(erec[:, cols], erec[:, cols], esum[:, cols], ALU.mult))
                V.tensor_tensor(opt[:, i, :].rearrange("p (h d) -> p h d", h=HEADS),
                                v0[:, i, :].rearrange("p (h d) -> p h d", h=HEADS),
                                spread(erec[:, cols], 2, HD), ALU.mult).then_inc(rows_ready, 1)

            for u in range(NT * PAIRS):
                dve.wait_ge(score_mm, u + 1)
                link(V.tensor_reduce(mx[:, 2 * u:2 * u + 2], ps[u % 8][:, :].rearrange("p (a b) -> p a b", a=2), AX_X, ALU.max))
                V.tensor_scalar(nmx[:, 2 * u:2 * u + 2], mx[:, 2 * u:2 * u + 2], -ATT_SCALE, None, ALU.mult).then_inc(max_done, 1)
                if u >= PAIRS and u % PAIRS == 3:
                    attended(u // PAIRS - 1)
            attended(NT - 1)
            for i in range(NT):
                turned(1, i, i, optT)
            dve.wait_ge(hb_ready, 1)
            for i in range(NT):
                dve.wait_ge(proj_mm, i + 1)
                link(V.tensor_tensor(h[:, i, :], ps[4 + i][:, 0:D], h[:, i, :], ALU.add))
                moments(2, i, h[:, i, :])
            for i in range(NT):
                normed(2, i)
            for i in range(NT):
                turned(2, i, i, aT)

            for i in range(NT):
                dve.wait_ge(log0_mm, i + 1)
                link(V.tensor_copy(lg[:, i, :], ps[4 + i][:, 0:E0]))
                link(V.max(top8[:, i, :], lg[:, i, :]))
                V.tensor_scalar(r_small[:, i:i + 1], top8[:, i, 0:1], -1.0, None, ALU.mult).then_inc(nmax_ready, 1)
                link(V.match_replace(rp[:, i, :], top8[:, i, :], lg[:, i, :], -3e38))
            V.tensor_tensor(mask, rp, lg, ALU.not_equal).then_inc(mask_ready, 1)
            dve.wait_ge(mask_ready, 1)
            dve.wait_ge(soft_done, NT)
            link(V.reciprocal(r_small[:, 2 * NT:3 * NT], r_small[:, NT:2 * NT]))
            for i in range(NT):
                ins = V.scalar_tensor_tensor(wt[:, i, :], pr[:, i, :], r_small[:, 2 * NT + i:2 * NT + i + 1], mask[:, i, :],
                                             ALU.mult, ALU.mult)
            link(ins)
            link(V.tensor_reduce(r_small[:, 3 * NT:4 * NT], wt, AX_X, ALU.add))
            link(V.reciprocal(r_small[:, 4 * NT:5 * NT], r_small[:, 3 * NT:4 * NT]))
            link(V.tensor_tensor(wt, wt, spread(r_small[:, 4 * NT:5 * NT], 2, E0), ALU.mult))
            for i in range(NT):
                dve.wait_ge(s_silu, i + 1)
                if i >= 2:
                    dve.wait_ge(s_hT, i - 1)
                V.tensor_tensor(hid[:, i % 2, :], ps[i % 2][:, F0:2 * F0], sil[:, i % 2, :], ALU.mult).then_inc(s_hid, 1)
                dve.wait_ge(s_dn, i + 1)
                V.tensor_tensor(h[:, i, :], ps[4 + i % 2][:, 0:D], h[:, i, :], ALU.add).then_inc(s_res, 1)
            dve.wait_ge(pos_mm, 1)
            pos = ps[6][:, 0:NT * E0].rearrange("p (i e) -> p i e", i=NT)
            link(V.scalar_tensor_tensor(kept, pos, float(CAP), mask, ALU.is_lt, ALU.mult))
            link(V.scalar_tensor_tensor(t1, pos, FAR, kept, ALU.subtract, ALU.mult))
            link(V.tensor_scalar(slot_i[:, :].rearrange("p (i e) -> p i e", i=NT), t1, FAR, None, ALU.add))
            link(V.tensor_scalar(dig_i[:, :], slot_i[:, :], 3, None, ALU.logical_shift_right))
            link(V.tensor_copy(digit_a, dig_i[:, :].rearrange("p (i e) -> p i e", i=NT)))
            link(V.tensor_scalar(dig_i[:, :], slot_i[:, :], BB - 1, None, ALU.bitwise_and))
            link(V.tensor_copy(digit_b, dig_i[:, :].rearrange("p (i e) -> p i e", i=NT)))
            link(V.tensor_tensor(kept, kept, wt, ALU.mult))
            iota_a = con[:, C_IOTA16:C_IOTA16 + BA]
            iota_b = con[:, C_IOTA16:C_IOTA16 + BB]
            for i in range(NT):
                if i >= 2:
                    dve.wait_ge(disp_mm, i - 1)
                if i:
                    dve.wait_ge(digits_ready, i)
                V.tensor_tensor(oneA[:, i % 2, :, :], spread(iota_a, 1, E0), spread(digit_a[:, i, :], 2, BA), ALU.is_equal)
                link(V.tensor_tensor(oneB, spread(iota_b, 1, E0), spread(digit_b[:, i, :], 2, BB), ALU.is_equal))
                V.tensor_scalar(rhsB[:, i % 2, :, 0, :], oneB.rearrange("p (g e) b -> p g (e b)", g=8),
                                con[:, C_TOK + i:C_TOK + i + 1], None, ALU.mult)
                V.tensor_tensor(rhsB[:, i % 2, :, 1, :].rearrange("p g (e b) -> p g e b", b=BB),
                                oneB.rearrange("p (g e) b -> p g e b", g=8),
                                spread(kept[:, i, :].rearrange("p (g e) -> p g e", g=8), 3, BB),
                                ALU.mult).then_inc(digits_ready, 1)
            link(V.tensor_tensor(t1, pos, spread(con[:, C_BASE:C_BASE + E0], 1, NT), ALU.add))
            link(V.scalar_tensor_tensor(rp, pos, float(CAP), mask, ALU.is_lt, ALU.mult))
            link(V.scalar_tensor_tensor(t1, t1, float(DROPPED), rp, ALU.subtract, ALU.mult))
            link(V.scalar_tensor_tensor(key, mask, float(DROPPED + 1), t1, ALU.mult, ALU.add))
            link(V.tensor_scalar(key, key, -1.0, None, ALU.add))
            for i in range(NT):
                ins = V.max(top8[:, i, :], key[:, i, :])
            link(ins)
            V.tensor_copy(take0[:, :], top8[:, :, :].rearrange("p i k -> p (i k)"))
            dve.wait_ge(disp_mm, NT)
            for n in range(2):
                ins = V.tensor_tensor(mid[:, n, :].rearrange("p (g c) -> p g c", c=64),
                                      ps[4 + n][:, :].rearrange("p (g c) -> p g c", c=64),
                                      spread(con[:, C_DIAG:C_DIAG + 64], 1, 8), ALU.mult)
            ins.then_inc(mid_ready, 1)
            dve.wait_ge(slot_mm, 1)
            for n in range(2):
                ins = V.tensor_tensor(sel[:, n, :, :], ps[6 + n][:, :].rearrange("p (g b) -> p g b", b=BB),
                                      spread(con[:, C_LOW0:C_LOW0 + BB], 1, 64), ALU.mult)
            link(ins)
            link(V.tensor_reduce(picked.rearrange("p a b c -> p (a b c)"), sel.rearrange("p n g b -> p (n g) b"), AX_X, ALU.add))
            V.tensor_copy(wsl0[:, :].rearrange("p (g e) -> p g e", g=8), picked[:, :, 1, :])
            V.tensor_copy(tok0[:, :].rearrange("p (g e) -> p g e", g=8), picked[:, :, 0, :]).then_inc(slots_ready, 1)

            dve.sem_inc(xT_sb, 2)
            dve.sem_inc(hid_done, 2)
            dve.sem_inc(y_sb, 2)
            for u in range(4):
                dve.sem_inc(y_out[u], 16)

            def copy_x(e, par):
                dve.wait_ge(xT_mm, e + 5)
                dve.wait_ge(gu_mm, e + 1)
                V.tensor_copy(xTs[:, par, :, :].rearrange("p a b -> p (a b)"), ps[6 + par][:, 0:D]).then_inc(xT_sb, 1)

            def hidden(e, par):
                dve.wait_ge(silu_done, e + 1)
                dve.wait_ge(hT_mm, e + 1)
                V.tensor_tensor(hid[:, par, :], ps[par][:, F0:2 * F0], sil[:, par, :], ALU.mult).then_inc(hid_done, 1)

            def weigh(e, u, turn_no):
                dve.wait_ge(y_mm, e + 3)
                dve.wait_ge(y_out[u], 16 * turn_no)
                V.tensor_scalar(yb[:, u, :], ps[4 + u % 2][:, 0:D], ptr(wsl0, e), None, ALU.mult).then_inc(y_sb, 1)

            copy_x(0, 0)
            copy_x(1, 1)
            hidden(0, 0)
            with dve.Fori(0, E0 // 4 - 1) as it:
                for v in range(4):
                    e = dve.snap(it * 4 + v + 1)
                    copy_x(e + 1, v % 2)
                    hidden(e, (v + 1) % 2)
                    weigh(e - 1, v, it + 1)
            for e in range(E0 - 3, E0):
                if e + 1 < E0:
                    copy_x(e + 1, (e + 1) % 2)
                hidden(e, e % 2)
                weigh(e - 1, (e - 1) % 4, (e - 1) // 4 + 1)
            weigh(E0 - 1, 3, E0 // 4)

            dve.wait_ge(late_in, 16 * 8)
            for i in range(NT):
                for k in range(K0):
                    n = i * K0 + k
                    dve.wait_ge(take_in[k], 16 * (i + 1))
                    V.tensor_tensor(h[:, i, :], h[:, i, :], acc_in[:, k, :], ALU.add).then_inc(h2_ready, 1)
                    dve.wait_ge(h2_ready, n + 1)
                moments(3, i, h[:, i, :])
                normed(3, i)
                turned(3, i, i, aT)
                dve.wait_ge(z_ready, i + 1)
                for n, dst in enumerate((qz, kz)):
                    V.tensor_scalar(dst[:, i, :], z[:, i, :], z_cols[:, 1 + n:2 + n], z_cols[:, 3 + n:4 + n],
                                    ALU.mult, ALU.add).then_inc(qk1_ready, 1)
                dve.wait_ge(v1_mm, i + 1)
                V.tensor_tensor(v1[:, i, :], ps[i][:, 0:D], bv1_bc[:, :], ALU.add).then_inc(vb_ready, 1)
            dve.wait_ge(bias_in, 16)
            for i in range(NT):
                dve.wait_ge(sim_mm, i + 1)
                link(V.scalar_tensor_tensor(sc[:, i, :], ps[4 + i][:, 0:P], L1_SCALE, bias1[:, :], ALU.mult, ALU.add))
                link(V.tensor_reduce(s1[:, i:i + 1], sc[:, i, :], AX_X, ALU.max))
                V.tensor_scalar(m1[:, i:i + 1], s1[:, i:i + 1], -1.0, None, ALU.mult).then_inc(nm_ready, 1)
            for i in range(NT):
                dve.wait_ge(p_done, i + 1)
                V.reciprocal(i1[:, i:i + 1], s1[:, i:i + 1])
                dve.wait_ge(p_T, i + 1)
                V.tensor_copy(pT[:, i, :], ps[i][:, D:D + P]).then_inc(pT_ready, 1)
                dve.wait_ge(pT_ready, i + 1)
                dve.wait_ge(o_mm, i + 1)
                link(V.scalar_tensor_tensor(h[:, i, :], ps[i][:, 0:D], i1[:, i:i + 1], h[:, i, :], ALU.mult, ALU.add))
                moments(4, i, h[:, i, :])
            for i in range(NT):
                normed(4, i)
            for i in range(NT):
                turned(4, i, i, aT)

            for i in range(NT):
                dve.wait_ge(log1_mm, i + 1)
                link(V.tensor_copy(lg1[:, i, :], ps[4 + i][:, 0:E1]))
                link(V.max(top8[:, i, :], lg1[:, i, :]))
                V.tensor_scalar(m1[:, i:i + 1], top8[:, i, 0:1], -1.0, None, ALU.mult).then_inc(nm1_ready, 1)
                link(V.max_index(idx8[:, i, :], top8[:, i, :], lg1[:, i, :]))
            link(V.tensor_copy(ad, idx8[:, :, 0:K1]))
            link(V.tensor_tensor(hot.rearrange("p i k e -> p (i k) e"), spread(con[:, C_IOTA16:C_IOTA16 + E1], 1, NT * K1),
                                 spread(ad.rearrange("p i k -> p (i k)"), 2, E1), ALU.is_equal))
            V.tensor_tensor(mask1, hot[:, :, 0, :], hot[:, :, 1, :], ALU.add).then_inc(mask1_ready, 1)
            dve.wait_ge(ex1_done, NT)
            link(V.reciprocal(ww[:, :, 3:4], ww[:, :, K1:K1 + 1]))
            link(V.tensor_tensor(ww[:, :, 0:K1], ww[:, :, 0:K1], ww[:, :, 3:4].broadcast_to([P, NT, K1]), ALU.mult))
            dve.wait_ge(pos1_mm, 1)
            link(V.tensor_copy(cnt[:, 0, :], ps[5][:, NT * E1:(NT + 1) * E1]))
            link(V.tensor_scalar(cnt[:, 1, :], cnt[:, 0, :], 0.0, None, ALU.is_gt))
            for m in range(1, NT):
                link(V.scalar_tensor_tensor(cnt[:, 1, :], cnt[:, 0, :], float(m * P), cnt[:, 1, :], ALU.is_gt, ALU.add))
            link(V.tensor_copy(start1[:, 0, :], cnt[:, 1, :]))
            for n, step in enumerate((1, 2, 4)):
                src, dst = start1[:, n % 2, :], start1[:, (n + 1) % 2, :]
                V.tensor_copy(dst[:, 0:step], src[:, 0:step])
                link(V.tensor_tensor(dst[:, step:E1], src[:, step:E1], src[:, 0:E1 - step], ALU.add))
            last = start1[:, 1, :]
            link(V.tensor_scalar(last, last, float(P), None, ALU.mult))
            link(V.scalar_tensor_tensor(start1[:, 2, :], cnt[:, 1, :], -float(P), last, ALU.mult, ALU.add))
            pos_1 = ps[5][:, 0:NT * E1].rearrange("p (i e) -> p i e", i=NT)
            link(V.tensor_tensor(addr1, pos_1, spread(start1[:, 2, :], 1, NT), ALU.add))
            for k in range(K1):
                link(V.tensor_tensor(tmp1, hot[:, :, k, :], addr1, ALU.mult))
                link(V.tensor_reduce(ad[:, :, k], tmp1, AX_X, ALU.add))
            link(V.tensor_copy(adr_i[:, :].rearrange("p (i k) -> p i k", k=K1), ad))
            link(V.tensor_scalar(dga[:, :], adr_i[:, :], 4, None, ALU.logical_shift_right))
            link(V.tensor_copy(ad, dga[:, :].rearrange("p (i k) -> p i k", k=K1)))
            link(V.tensor_tensor(oneA1.rearrange("p i k s -> p (i k) s"), spread(con[:, C_ROW128:C_ROW128 + P], 1, NT * K1),
                                 spread(ad.rearrange("p i k -> p (i k)"), 2, P), ALU.is_equal))
            link(V.tensor_scalar(dga[:, :], adr_i[:, :], CB - 1, None, ALU.bitwise_and))
            link(V.tensor_copy(ad, dga[:, :].rearrange("p (i k) -> p i k", k=K1)))
            for k in range(K1):
                link(V.tensor_tensor(rhsB1[:, :, k, 1, :], spread(con[:, C_IOTA16:C_IOTA16 + CB], 1, NT),
                                     spread(ad[:, :, k], 2, CB), ALU.is_equal))
                V.tensor_tensor(rhsB1[:, :, k, 0, :], rhsB1[:, :, k, 1, :], spread(con[:, C_TOK:C_TOK + NT], 2, CB), ALU.mult)
                ins = V.tensor_tensor(rhsB1[:, :, k, 1, :], rhsB1[:, :, k, 1, :], ww[:, :, k:k + 1].broadcast_to([P, NT, CB]), ALU.mult)
            ins.then_inc(hot1_ready, 1)
            link(V.tensor_tensor(tend, spread(last, 1, 16), spread(con[:, C_128J:C_128J + 16], 2, E1), ALU.is_le))
            link(V.tensor_reduce(ecol, tend, AX_X, ALU.add))
            link(V.tensor_scalar(tile_e[:, :], ecol, float(E1 - 1), None, ALU.min))
            dve.wait_ge(disp1_mm, 1)
            for n in range(2):
                ins = V.tensor_tensor(mid1[:, n, :, :], spread(ps[6][:, n * CB:(n + 1) * CB], 1, 16),
                                      spread(con[:, C_TILE:C_TILE + 16], 2, CB), ALU.mult)
            ins.then_inc(mid1_ready, 1)
            dve.wait_ge(slot1_mm, 1)
            link(V.tensor_tensor(sel1.rearrange("p a b c -> p (a b) c"), ps[7][:, :].rearrange("p (g b) -> p g b", b=CB),
                                 spread(con[:, C_LOW1:C_LOW1 + CB], 1, 32), ALU.mult))
            link(V.tensor_reduce(picked1.rearrange("p a b -> p (a b)"), sel1.rearrange("p a b c -> p (a b) c"), AX_X, ALU.add))
            V.tensor_copy(wsl1[:, :], picked1[:, 1, :])
            V.tensor_copy(tok1[:, :], picked1[:, 0, :]).then_inc(slots1_ready, 1)

            dve.wait_ge(slots1_ready, 1)
            dve.wait_ge(b2_in, 16)
            for done, credit in ((g_xTs, 2), (g_h1s, 2), (g_ysb, 2), (g_out[0], 16), (g_out[1], 16)):
                dve.sem_inc(done, credit)

            def expert_of(j):
                return dve.value_load(tile_e[0:1, bass.ds(j, 1)], min_val=0, max_val=E1 - 1)

            def copy_x1(j, par):
                dve.wait_ge(g_xT, j + 3)
                dve.wait_ge(g_h1, 2 * j + 2)
                V.tensor_copy(xT1[:, par, :, :].rearrange("p a b -> p (a b)"), ps[6 + par][:, 0:D]).then_inc(g_xTs, 1)

            def hidden1(j, par, first=False):
                e = expert_of(j)
                if not first:
                    dve.wait_ge(g_gelu, 2 * j)
                V.tensor_scalar(b1j[:, par, :], ptr(b1_sb, e * KF, KF), 1.0, None, ALU.mult).then_inc(g_b1, 1)
                for n in range(2):
                    dve.wait_ge(g_h1, 2 * j + n + 5)
                    dve.wait_ge(g_hT, 2 * j + n + 1)
                    V.tensor_copy(h1s[:, n * 512:(n + 1) * 512], ps[n][:, :]).then_inc(g_h1s, 1)

            def weigh1(j, par, turn_no):
                e = expert_of(j)
                dve.wait_ge(g_y, j + 2)
                dve.wait_ge(g_ysb, j + 2)
                V.scalar_tensor_tensor(y_t, ps[4 + par][:, 0:D], 1.0, ptr(b2_bc, e * D, D),
                                       ALU.mult, ALU.add).then_inc(g_yt, 1)
                dve.wait_ge(g_yt, j + 1)
                dve.wait_ge(g_out[par], 16 * turn_no)
                V.tensor_scalar(yb1[:, par, :], y_t, ptr(wsl1, j), None, ALU.mult).then_inc(g_ysb, 1)

            copy_x1(0, 0)
            copy_x1(1, 1)
            hidden1(0, 0, first=True)
            with dve.Fori(0, (TILES1 - 3) // 2) as it:
                for v in range(2):
                    j = dve.snap(it * 2 + v + 1)
                    copy_x1(j + 1, v)
                    hidden1(j, (v + 1) % 2)
                    weigh1(j - 1, v, it + 1)
            for j in range(TILES1 - 2, TILES1):
                if j + 1 < TILES1:
                    copy_x1(j + 1, (j + 1) % 2)
                hidden1(j, j % 2)
                weigh1(j - 1, (j - 1) % 2, (j - 1) // 2 + 1)
            weigh1(TILES1 - 1, (TILES1 - 1) % 2, (TILES1 - 1) // 2 + 1)
            for n in range(NT * K1):
                dve.wait_ge(take1_in[n], 16)
                V.tensor_tensor(h[:, n // K1, :], h[:, n // K1, :], acc_in1[:, n, :], ALU.add).then_inc(final_ready, 1)
                dve.wait_ge(final_ready, n + 1)


def laid_out(v):
    c = np.ascontiguousarray

    def blocks(m):
        return c(m.reshape(-1, P, m.shape[-1]).transpose(1, 0, 2).reshape(P, -1))

    x = v["x"].reshape(2, 5, 16, PATCH, 16, PATCH).transpose(1, 3, 5, 0, 2, 4).reshape(FEAT, T)
    w_in = v["L0_attn_w_in"].reshape(HEADS, 3, HD, D).transpose(1, 0, 2, 3).reshape(3 * D, D)
    b_in = v["L0_attn_b_in"].reshape(HEADS, 3, HD).transpose(1, 0, 2).reshape(3, D)
    gu = np.concatenate([v["L0_ffn_w_gate"], v["L0_ffn_w_up"]], axis=-1)
    return {
        "x_in": c(x), "tok_w": c(v["L0_tok_W"]), "gamma": v["L0_tok_gamma"], "consts": constants(), "buckets": bucket_rows(),
        "w_in": c(w_in.T.reshape(KD, P, 3 * D).transpose(1, 0, 2)),
        "bq_in": c(b_in[0].reshape(KD, P).T), "bk_in": c(b_in[1].reshape(KD, P).T), "bv_in": c(b_in[2]),
        "w_out": blocks(v["L0_attn_w_out"].T), "b_out": v["L0_attn_b_out"], "router0": blocks(v["L0_ffn_router_w"].T),
        "gate_up": c(gu.reshape(E0, KD, P, 2 * F0).transpose(0, 2, 1, 3).reshape(E0, P, GU)),
        "down": c(v["L0_ffn_w_down"].reshape(E0, 2, FH, D).transpose(0, 2, 1, 3).reshape(E0, FH, DN)),
        "shared_gu": blocks(v["L0_ffn_ws_gate_up"]),
        "shared_dn": c(v["L0_ffn_ws_down"].reshape(2, FH, D).transpose(1, 0, 2).reshape(FH, DN)),
        "wqk": blocks(v["L1_attn_Wqk"]), "bqk": c(v["L1_attn_bqk"].reshape(P, 1)), "wv": blocks(v["L1_attn_Wv"]),
        "bv1": v["L1_attn_bv"], "gam1": c(v["L1_attn_gamma"].T), "bet1": c(v["L1_attn_beta"].T), "rel": v["L1_attn_rel_emb"],
        "router1": blocks(v["L1_ffn_router_w"].T),
        "w1": c(v["L1_ffn_w1"].transpose(0, 2, 1).reshape(E1, KD, P, F1).transpose(0, 2, 1, 3).reshape(E1, P, KD * F1)),
        "w2": c(v["L1_ffn_w2"].transpose(0, 2, 1).reshape(E1, KF, P, D).transpose(0, 2, 1, 3).reshape(E1, P, KF * D)),
        "b1": c(v["L1_ffn_b1"].reshape(E1, KF, P).transpose(2, 0, 1).reshape(P, E1 * KF)),
        "b2": c(v["L1_ffn_b2"].reshape(-1)),
    }


def kernel(**inputs):
    import concourse.bacc as bacc
    from concourse.bass_utils import run_bass_kernel_spmd as run

    nc = bacc.Bacc("TRN2", target_bir_lowering=False, num_devices=1)
    arrays = laid_out({k: np.asarray(v) for k, v in inputs.items()})
    args = {k: nc.dram_tensor(k, a.shape, mybir.dt.from_np(a.dtype), kind="ExternalInput").ap() for k, a in arrays.items()}
    out = nc.dram_tensor("out", (T, D), F32, kind="ExternalOutput").ap()
    vit_tower(nc, out=out, **args)
    r = run(nc, [arrays], core_ids=[0])
    return r.results[0]["out"].reshape(2, SEQ, D)
```

```python
from contextlib import ExitStack

import numpy as np

import concourse.bass as bass
from concourse import mybir

F32 = mybir.dt.float32
I32 = mybir.dt.int32
U32 = mybir.dt.uint32
ALU = mybir.AluOpType
ACT = mybir.ActivationFunctionType
AX_X = mybir.AxisListType.X

P = 128
D = 256
KD = D // P
T = 512
NT = T // P
PATCH = 8
FEAT = 5 * PATCH * PATCH
EPS = 1e-5

HEADS, HD = 16, 16
SEQ = 256
PAIRS = HEADS // 2
ATT_SCALE = 1.0 / HD ** 0.5

E0, K0, F0, CAP = 64, 8, 192, 128
FH = F0 // 2
GU = KD * 2 * F0
DN = 2 * D
RING = 4
DROPPED = E0 * CAP
BA, BB = 16, 8

ZQK = 128
L1_SCALE = D ** -0.5
BUCKETS, MAX_DISTANCE = 32, 128

E1, K1, F1 = 8, 2, 1024
KF = F1 // P
TILES1 = (K1 * T + E1 * (P - 1)) // P
CB = 16
FAR = 1023.0
NEG = -1e30

C_IDENT, C_UPPER, C_ONES, C_EXP0, C_EXP1, C_ROW128 = (i * P for i in range(6))
C_DIAG = 6 * P
C_LOW0 = C_DIAG + 64
C_IOTA16 = C_LOW0 + BB
C_TOK = C_IOTA16 + 16
C_BASE = C_TOK + NT
C_TILE = C_BASE + E0
C_LOW1 = C_TILE + 16
C_HEAD = C_LOW1 + CB
C_128J = C_HEAD + 8
C_ALL = C_128J + 16


def constants():
    c = np.zeros((P, C_ALL), np.float32)
    p = np.arange(P)[:, None]
    s = np.arange(P)[None, :]
    c[:, C_IDENT:C_IDENT + P] = p == s
    c[:, C_UPPER:C_UPPER + P] = p < s
    c[:, C_ONES:C_ONES + P] = 1
    c[:, C_EXP0:C_EXP0 + P] = p % BA == s // BB
    c[:, C_EXP1:C_EXP1 + P] = p % 8 == s // CB
    c[:, C_ROW128:C_ROW128 + P] = s
    c[:, C_DIAG:C_DIAG + 64] = p // BA == np.arange(64)[None, :] // BB
    c[:, C_LOW0:C_LOW0 + BB] = np.arange(BB)[None, :] == p % BB
    c[:, C_IOTA16:C_IOTA16 + 16] = np.arange(16)
    c[:, C_TOK:C_TOK + NT] = p + P * np.arange(NT)[None, :]
    c[:, C_BASE:C_BASE + E0] = CAP * np.arange(E0) + FAR - DROPPED
    c[:, C_TILE:C_TILE + 16] = p // 8 == np.arange(16)[None, :]
    c[:, C_LOW1:C_LOW1 + CB] = np.arange(CB)[None, :] == p % CB
    c[:, C_HEAD:C_HEAD + 8] = p // HD == np.arange(8)[None, :]
    c[:, C_128J:C_128J + 16] = P * np.arange(16)
    return c


def bucket_rows():
    out = np.zeros((BUCKETS + 1, 2 * P), np.float32)
    n = np.arange(P)
    exact = BUCKETS // 2
    far = exact + (np.log((np.maximum(n, 1).astype(np.float32) / np.float32(exact)))
                   / np.float32(np.log(MAX_DISTANCE / exact)) * np.float32(BUCKETS - exact))
    far = np.minimum(far, BUCKETS - 1)
    b = np.where(n < exact, n.astype(np.float32), far).astype(np.int32)
    out[b, P - 1 - n] = 1
    out[BUCKETS, P:] = NEG
    return out


def vit_tower(nc, x_in, tok_w, gamma, consts, buckets, w_in, bq_in, bk_in, bv_in, w_out, b_out,
              router0, gate_up, down, shared_gu, shared_dn, wqk, bqk, wv, bv1, gam1, bet1, rel,
              router1, w1, w2, b1, b2, out):
    rows0 = nc.dram_tensor("rows0", (T, D), F32).ap()
    rows1 = nc.dram_tensor("rows1", (T, D), F32).ap()
    y0 = nc.dram_tensor("y0", (E0 * CAP + 1, D), F32).ap()
    y1 = nc.dram_tensor("y1", (TILES1 * P, D), F32).ap()
    bias_rows = nc.dram_tensor("bias_rows", (P, 2 * P), F32).ap()

    with ExitStack() as ctx:
        def sb(name, shape, dt=F32):
            return ctx.enter_context(nc.sbuf_tensor(name, shape, dt))

        def sem(name):
            return ctx.enter_context(nc.semaphore(name))

        ps = [ctx.enter_context(nc.psum_tensor(f"bank{i}", [P, 512], F32)) for i in range(8)]

        w1_sb = sb("w1_sb", [P, E1 * KD * F1])
        w2_sb = sb("w2_sb", [P, E1 * KF * D])
        ring_gu = [sb(f"ring_gu{u}", [P, GU]) for u in range(RING)]
        ring_dn = [sb(f"ring_dn{u}", [FH, DN]) for u in range(RING)]
        con = sb("con", [P, C_ALL])
        gamma_bc = sb("gamma_bc", [P, D])
        wout_sb = sb("wout_sb", [P, KD * D])
        r0_sb = sb("r0_sb", [P, KD * E0])
        bqk0 = sb("bqk0", [P, 4])
        bq_one = sb("bq_one", [P, KD, 8])
        wqk_sb = sb("wqk_sb", [P, KD * ZQK])
        wv_sb = sb("wv_sb", [P, KD * D])
        bv1_bc = sb("bv1_bc", [P, D])
        r1_sb = sb("r1_sb", [P, KD * E1])
        z_cols = sb("z_cols", [P, 5])
        b1_sb = sb("b1_sb", [P, E1 * KF])
        bias1 = sb("bias1", [P, P])
        h = sb("h", [P, NT, D])
        a = sb("a", [P, NT, D])
        aT = sb("aT", [P, KD, T])
        stats = sb("stats", [P, NT, 6])
        mv = sb("mv", [P, NT, 2])
        std = sb("std", [P, NT])
        rstd = sb("rstd", [P, NT])
        pool = sb("pool", [P, 8192])

        hidT_bvec = sb("hidT_bvec", [P, 2 * D])

        def at(start, *dims, parts=P):
            n = int(np.prod(dims))
            v = pool[0:parts, start:start + n]
            if len(dims) == 1:
                return v
            names = "abcd"[:len(dims)]
            return v.rearrange(f"p ({' '.join(names)}) -> p {' '.join(names)}",
                               **{k: d for k, d in zip(names[1:], dims[1:])})

        ident = con[:, C_IDENT:C_IDENT + P]
        upper = con[:, C_UPPER:C_UPPER + P]
        ones = con[:, C_ONES:C_ONES + P]

        bvec_bc = hidT_bvec
        small = at(7936, 2 * P)
        xa = at(0, KD, T)
        xb = at(1024, T, parts=FEAT - KD * P)
        wa = at(1536, KD, D)
        wb = at(2048, D, parts=FEAT - KD * P)
        win = at(2304, KD, 3 * D)
        q_one = w2_sb[:, E1 * KF * D // 2:].rearrange("p (h t) -> p h t", h=HEADS)
        kT = at(4864, KD, T)
        zero_row = at(6912, D, parts=1)
        v0 = at(6912, NT, D)
        mx, nmx, esum, erec = (at(1024 + 64 * n, NT * HEADS) for n in range(4))
        opt = at(1536, NT, D)
        optT = at(2560, KD, T)

        lg = at(0, NT, E0)
        rp = at(256, NT, E0)
        mask = at(512, NT, E0)
        pr = at(768, NT, E0)
        kept = at(1280, NT, E0)
        t1 = at(1536, NT, E0)
        key = at(5632, NT, E0)
        hot8 = at(5888, K0, E0)
        top8 = sb("top8", [P, NT, 8])
        r_small = sb("r_small", [P, 4 * NT])
        wt8 = sb("wt8", [P, NT, K0])
        id8 = sb("id8", [P, NT, K0], U32)
        slot_i = at(7936, NT * E0).bitcast(I32)
        dig_a = at(2048, NT * E0).bitcast(I32)
        dig_b = at(2304, NT * E0).bitcast(I32)
        take0 = sb("take0", [P, NT * K0], I32)
        oneA = at(2560, 2, E0, BA)
        oneB = at(4608, E0, BB)
        rhsB = at(6144, 2, 8, 64)
        mid = at(2560, 512)
        tok_f = at(6400, E0)
        sel = at(4608, E0, BB)
        tok0 = sb("tok0", [P, E0], I32)

        sil = at(7168, 2, F0)
        hid = at(7552, 2, F0)
        hidT = hidT_bvec[0:FH, :].rearrange("p (a b) -> p a b", a=2)
        xg = at(0, 4, D)
        xTs = at(1024, 2, KD, P)
        yb = at(1536, 4, D)
        acc_in = at(0, 8, D)
        idx_ring = sb("idx_ring", [P, 4], I32)

        z = at(2048, NT, P)
        qz = at(2560, NT, P)
        kz = at(3072, NT, P)
        v1 = at(3584, NT, D)
        sc = at(5632, NT, P)
        pT = at(5120, NT, P)
        m1 = sb("m1", [P, NT])
        s1 = sb("s1", [P, NT])
        i1 = sb("i1", [P, NT])
        lg1 = at(4608, NT, E1)
        mask1 = at(4640, NT, E1)
        pos1 = at(4672, NT, E1)
        addr1 = at(4704, NT, E1)
        tmp1 = at(4736, NT, E1)
        cnt = at(4768, 4, E1)
        start1 = at(4800, 3, E1)
        hot = at(4832, NT, K1, E1)
        ad = at(4896, NT, K1)
        ww = at(4904, NT, 4)
        oneA1 = at(0, NT, K1, P)
        rhsB1 = at(1024, NT, K1, CB)
        mid1 = at(1280, 16, CB)
        sel1 = at(4928, 16, CB)
        tend = at(5472, 16, E1)
        ecol = at(5600, 16)
        idx8 = sb("idx8", [P, NT, 8], U32)
        adr_i = sb("adr_i", [P, NT * K1], I32)
        dga = sb("dga", [P, NT * K1], I32)
        tok1 = sb("tok1", [P, 16], I32)
        tile_e = sb("tile_e", [P, 16], I32)
        b2_bc = at(6144, E1 * D)
        b1j = sb("b1j", [P, 2, KF])
        xg1 = at(0, 2, D)
        xT1 = at(512, 2, KD, P)
        h1s = at(1024, F1)
        hT1 = at(2048, KF, P)
        yb1 = at(3328, 2, D)
        acc_in1 = at(0, 8, D)

        buck_sb = at(3840, 2 * P, parts=BUCKETS + 1)
        rel_sb = sb("rel_sb", [BUCKETS + 1, 1])

        names = """tok_in con_in bvec_in attn_in late_in b2_in ffn_in rows0_out zero_set zero_out rows1_out
            bias_mm bias_sb bias_out bias_in fin_out
            tok_mm var_ready std_ready rows_ready T_mm T_sb q_mm k_mm v_mm qcol_ready q0_ready q1_ready k_ready v_ready
            score_mm max_done exp_done hb_ready proj_mm
            log0_mm nmax_ready soft_done mask_ready pos_mm digits_ready disp_mm mid_ready
            slot_mm slots_ready take_ready s_gu s_silu s_hid s_hT s_hTs s_dn s_res
            xT_mm xT_sb gu_mm silu_done hid_done hT_mm hT_sb y_mm y_sb idx_ready gathers
            h2_ready z_mm z_ready qk1_ready v1_mm vb_ready v1_ready sim_mm nm_ready p_done p_T
            pT_ready o_mm
            log1_mm nm1_ready ex1_done mask1_ready pos1_mm hot1_ready disp1_mm mid1_ready slot1_mm
            slots1_ready g_xT g_xTs g_h1 g_h1s g_hT g_gelu g_y g_ysb g_b1 g_idx final_ready
            dve_chain""".split()
        s = {n: sem(n) for n in names}
        (tok_in, con_in, bvec_in, attn_in, late_in, b2_in, ffn_in, rows0_out, zero_set, zero_out, rows1_out,
         bias_mm, bias_sb, bias_out, bias_in, fin_out,
         tok_mm, var_ready, std_ready, rows_ready, T_mm, T_sb, q_mm, k_mm, v_mm, qcol_ready, q0_ready, q1_ready, k_ready, v_ready,
         score_mm, max_done, exp_done, hb_ready, proj_mm,
         log0_mm, nmax_ready, soft_done, mask_ready, pos_mm, digits_ready, disp_mm, mid_ready,
         slot_mm, slots_ready, take_ready, s_gu, s_silu, s_hid, s_hT, s_hTs, s_dn, s_res,
         xT_mm, xT_sb, gu_mm, silu_done, hid_done, hT_mm, hT_sb, y_mm, y_sb, idx_ready, gathers,
         h2_ready, z_mm, z_ready, qk1_ready, v1_mm, vb_ready, v1_ready, sim_mm, nm_ready, p_done, p_T,
         pT_ready, o_mm,
         log1_mm, nm1_ready, ex1_done, mask1_ready, pos1_mm, hot1_ready, disp1_mm, mid1_ready, slot1_mm,
         slots1_ready, g_xT, g_xTs, g_h1, g_h1s, g_hT, g_gelu, g_y, g_ysb, g_b1, g_idx, final_ready,
         dve_chain) = s.values()
        ring_in = [sem(f"ring_in{u}") for u in range(RING)]
        xg_in = [sem(f"xg_in{u}") for u in range(4)]
        y_out = [sem(f"y_out{u}") for u in range(4)]
        take_in = [sem(f"take_in{u}") for u in range(8)]
        g_in = [sem(f"g_in{u}") for u in range(2)]
        g_out = [sem(f"g_out{u}") for u in range(2)]
        take1_in = [sem(f"take1_in{u}") for u in range(8)]

        def tile(i):
            return slice(i * P, (i + 1) * P)

        def spread(ap, axis, n):
            v = ap.unsqueeze(axis)
            shape = list(v.shape)
            shape[axis] = n
            return v.broadcast_to(shape)

        def ptr(tensor, start, size=1):
            return tensor[:, bass.ds(start, size)]

        def head_pair(u):
            i, g = divmod(u, PAIRS)
            return i, g % 2, 2 * (g // 2), (u + 2) % 8

        block = ctx.enter_context(nc.Block())

        @block.sync
        def _(sp):
            sp.dma_start(xa, x_in[0:KD * P, :].rearrange("(k p) t -> p k t", p=P)).then_inc(tok_in, 16)
            sp.dma_start(wa, tok_w[0:KD * P, :].rearrange("(k p) d -> p k d", p=P)).then_inc(tok_in, 16)
            sp.dma_start(xb, x_in[KD * P:FEAT, :]).then_inc(tok_in, 16)
            sp.dma_start(wb, tok_w[KD * P:FEAT, :]).then_inc(tok_in, 16)
            sp.dma_start(win, w_in).then_inc(attn_in, 16)
            sp.dma_start(bvec_bc[:, 0:D], bv_in.partition_broadcast(P)).then_inc(bvec_in, 16)
            sp.dma_start(bvec_bc[:, D:2 * D], b_out.partition_broadcast(P)).then_inc(bvec_in, 16)
            sp.dma_start(wout_sb[:, :], w_out).then_inc(attn_in, 16)
            sp.dma_start(r0_sb[:, :], router0).then_inc(attn_in, 16)

            def load_expert(e, u):
                sp.dma_start(ring_gu[u][:, :], gate_up[bass.ds(e, 1), :, :].squeeze(0)).then_inc(ring_in[u], 16)
                sp.dma_start(ring_dn[u][:, :], down[bass.ds(e, 1), :, :].squeeze(0)).then_inc(ring_in[u], 16)

            sp.dma_start(ring_gu[RING - 1][:, :], shared_gu).then_inc(ring_in[RING - 1], 16)
            sp.dma_start(ring_dn[RING - 1][:, :], shared_dn).then_inc(ring_in[RING - 1], 16)
            for e in range(RING - 1):
                load_expert(e, e)
            def load_w2(e):
                sp.dma_start(w2_sb[:, e * KF * D:(e + 1) * KF * D], w2[e]).then_inc(ffn_in, 16)

            for e in range(E1):
                sp.dma_start(w1_sb[:, e * KD * F1:(e + 1) * KD * F1], w1[e]).then_inc(ffn_in, 16)
            for e in range(E1 // 2):
                load_w2(e)
            sp.wait_ge(exp_done, HEADS * NT)
            for e in range(E1 // 2, E1):
                load_w2(e)
            sp.wait_ge(s_dn, NT)
            load_expert(RING - 1, RING - 1)

            def store_y(e, u):
                sp.wait_ge(y_sb, e + 3)
                sp.dma_start(y0[bass.ds(e * CAP, CAP), :], yb[:, u, :]).then_inc(y_out[u], 16)

            with sp.Fori(0, E0 // RING - 1) as it:
                for u in range(RING):
                    e = sp.snap(it * RING + u)
                    store_y(e, u)
                    sp.wait_ge(y_mm, e + 3)
                    load_expert(e + RING, u)
            for u in range(RING):
                store_y(E0 - RING + u, u)

            def store_y1(j):
                sp.wait_ge(g_ysb, j + 3)
                sp.dma_start(y1[j * P:(j + 1) * P, :], yb1[:, j % 2, :]).then_inc(g_out[j % 2], 16)

            for j in range(TILES1):
                store_y1(j)
            for i in range(NT):
                sp.wait_ge(final_ready, K1 * (i + 1))
                sp.dma_start(out[tile(i), :], h[:, i, :]).then_inc(fin_out, 16)
            sp.wait_ge(fin_out, 16 * NT)

        @block.gpsimd
        def _(pool_e):
            for dst, src in ((wqk_sb[:, :], wqk), (wv_sb[:, :], wv),
                             (bv1_bc[:, :], bv1.partition_broadcast(P)), (r1_sb[:, :], router1),
                             (z_cols[:, 0:1], bqk), (z_cols[:, 1:3], gam1), (z_cols[:, 3:5], bet1),
                             (b1_sb[:, :], b1)):
                pool_e.dma_start(dst, src).then_inc(late_in, 16)
            pool_e.wait_ge(rows_ready, NT)
            pool_e.wait_ge(bvec_in, 16 * 2)
            nc.gpsimd.tensor_tensor(h[:, :, :], h[:, :, :], spread(bvec_bc[:, D:2 * D], 1, NT),
                                    ALU.add).then_inc(hb_ready, 1)

            def gather(e, u, value):
                nc.gpsimd.tensor_copy(idx_ring[:, u:u + 1], ptr(tok0, e)).then_inc(idx_ready, 1)
                pool_e.wait_ge(idx_ready, value)
                pool_e.sem_inc(gathers, 1)
                pool_e.indirect_dma_start(xg[:, u, :], None, rows0, bass.IndirectOffsetOnAxis(idx_ring[:, u:u + 1], 0),
                                          bounds_check=T - 1, oob_is_err=False).then_inc(xg_in[u], 16)

            pool_e.wait_ge(slots_ready, 1)
            pool_e.wait_ge(rows0_out, 16)
            pool_e.sem_inc(idx_ready, 1)
            for u in range(4):
                gather(u, u, u + 2)
            with pool_e.Fori(1, E0 // 4) as it:
                for u in range(4):
                    e = pool_e.snap(it * 4 + u)
                    pool_e.wait_ge(xT_mm, e + 1)
                    gather(e, u, e + 2)
            for u in range(4):
                pool_e.wait_ge(y_out[u], 16 * (E0 // 4 + 1))
            pool_e.wait_ge(zero_out, 16)
            for i in range(NT):
                pool_e.wait_ge(take_ready, i + 1)
                for k in range(K0):
                    if i:
                        pool_e.wait_ge(h2_ready, K0 * (i - 1) + k + 1)
                    n = i * K0 + k
                    pool_e.indirect_dma_start(acc_in[:, k, :], None, y0, bass.IndirectOffsetOnAxis(take0[:, n:n + 1], 0),
                                              bounds_check=DROPPED, oob_is_err=False).then_inc(take_in[k], 16)

            def gather1(j, u, value):
                nc.gpsimd.tensor_copy(idx_ring[:, u:u + 1], ptr(tok1, j)).then_inc(g_idx, 1)
                pool_e.wait_ge(g_idx, value)
                pool_e.indirect_dma_start(xg1[:, u, :], None, rows1, bass.IndirectOffsetOnAxis(idx_ring[:, u:u + 1], 0),
                                          bounds_check=T - 1, oob_is_err=False).then_inc(g_in[u], 16)

            pool_e.wait_ge(slots1_ready, 1)
            pool_e.wait_ge(rows1_out, 16)
            for j in range(TILES1):
                if j >= 2:
                    pool_e.wait_ge(g_xT, j + 1)
                gather1(j, j % 2, j + 1)
            for u in range(2):
                pool_e.wait_ge(g_out[u], 16 * ((TILES1 + 1 - u) // 2 + 1))
            for n in range(NT * K1):
                pool_e.indirect_dma_start(acc_in1[:, n, :], None, y1, bass.IndirectOffsetOnAxis(adr_i[:, n:n + 1], 0),
                                          bounds_check=TILES1 * P - 1, oob_is_err=False).then_inc(take1_in[n], 16)

        @block.scalar
        def _(act):
            act.dma_start(con[:, :], consts).then_inc(con_in, 16)
            act.dma_start(gamma_bc[:, :], gamma.partition_broadcast(P)).then_inc(con_in, 16)
            for dst, src in ((buck_sb[:, :], buckets), (rel_sb[0:BUCKETS, :], rel)):
                act.dma_start(dst, src).then_inc(con_in, 16)
            act.dma_start(bqk0[:, 0:2], bq_in).then_inc(attn_in, 16)
            act.dma_start(bqk0[:, 2:4], bk_in).then_inc(attn_in, 16)
            act.wait_ge(zero_set, 1)
            act.dma_start(y0[DROPPED:DROPPED + 1, :], zero_row).then_inc(zero_out, 16)

            def roots(count, tiles):
                act.wait_ge(var_ready, count)
                nc.scalar.activation(std[:, tiles], mv[:, tiles, 1], ACT.Sqrt).then_inc(std_ready, 1)

            all_tiles = slice(0, NT)
            roots(1, all_tiles)
            act.wait_ge(bias_sb, 1)
            act.dma_start(bias_rows, small[:, 0:2 * P]).then_inc(bias_out, 16)
            roots(2, all_tiles)
            act.wait_ge(attn_in, 16 * 5)
            for c in range(KD):
                act.wait_ge(k_mm, c + 1)
                nc.scalar.activation(kT[:, c, :], ps[2 + c][:, :], ACT.Identity, bias=bqk0[:, 2 + c:3 + c]).then_inc(k_ready, 1)
            act.wait_ge(q_mm, 2)
            act.wait_ge(qcol_ready, 1)
            for hd in range(8):
                nc.scalar.activation(q_one[:, 8 + hd, :], ps[1][:, :], ACT.Identity,
                                     scale=con[:, C_HEAD + hd:C_HEAD + hd + 1],
                                     bias=bq_one[:, 1, hd:hd + 1]).then_inc(q1_ready, 1)
            for u in range(NT * PAIRS):
                i, c, hd, bank = head_pair(u)
                act.wait_ge(max_done, u + 1)
                for par in range(2):
                    n = i * HEADS + 8 * c + hd + par
                    scores = ps[bank][:, par * SEQ:(par + 1) * SEQ]
                    nc.scalar.activation(scores, scores, ACT.Exp, scale=ATT_SCALE, bias=nmx[:, n:n + 1],
                                         accum_out=esum[:, n:n + 1]).then_inc(exp_done, 1)
            act.wait_ge(bias_out, 16)
            act.dma_start(bias1[:, :], bass.AP(bias_rows.tensor, P - 1, [[2 * P - 1, P], [1, P]])).then_inc(bias_in, 16)
            roots(3, all_tiles)
            act.wait_ge(rows_ready, 3 * NT)
            act.dma_start(rows0.rearrange("(i p) d -> p i d", p=P), a[:, :, :]).then_inc(rows0_out, 16)
            act.wait_ge(nmax_ready, 1)
            for i in range(NT):
                nc.scalar.activation(pr[:, i, :], lg[:, i, :], ACT.Exp, bias=r_small[:, i:i + 1],
                                     accum_out=r_small[:, NT + i:NT + i + 1]).then_inc(soft_done, 1)
                nc.scalar.activation(wt8[:, i, :], top8[:, i, :], ACT.Exp, bias=r_small[:, i:i + 1]).then_inc(soft_done, 1)

            for i in range(NT):
                act.wait_ge(s_gu, i + 1)
                if i >= 2:
                    act.wait_ge(s_hid, i - 1)
                nc.scalar.activation(sil[:, i % 2, :], ps[i % 2][:, 0:F0], ACT.Silu).then_inc(s_silu, 1)
                act.wait_ge(s_hT, i + 1)
                if i >= 2:
                    act.wait_ge(s_dn, i - 1)
                nc.scalar.activation(hidT[:, i % 2, :], ps[2 + i % 2][0:FH, 0:D],
                                     ACT.Copy).then_inc(s_hTs, 1)

            act.sem_inc(hT_sb, 2)

            def silu(e, par):
                act.wait_ge(gu_mm, e + 3)
                act.wait_ge(hid_done, e + 1)
                nc.scalar.activation(sil[:, par, :], ps[par][:, 0:F0], ACT.Silu).then_inc(silu_done, 1)

            def turned(e, par):
                act.wait_ge(hT_mm, e + 3)
                act.wait_ge(y_mm, e + 1)
                nc.scalar.activation(hidT[:, par, :], ps[2 + par][0:FH, 0:D], ACT.Copy).then_inc(hT_sb, 1)

            silu(0, 0)
            with act.Fori(0, E0 // 4 - 1) as it:
                for u in range(4):
                    e = act.snap(it * 4 + u + 1)
                    turned(e - 1, u % 2)
                    silu(e, (u + 1) % 2)
            for e in range(E0 - 3, E0):
                turned(e - 1, (e - 1) % 2)
                silu(e, e % 2)
            turned(E0 - 1, (E0 - 1) % 2)

            for i in range(NT):
                roots(4 + 2 * i, slice(i, i + 1))
                act.wait_ge(z_mm, i + 1)
                nc.scalar.activation(z[:, i, :], ps[4][:, 0:P], ACT.Silu, bias=z_cols[:, 0:1]).then_inc(z_ready, 1)
                act.wait_ge(vb_ready, i + 1)
                nc.scalar.activation(v1[:, i, :], v1[:, i, :], ACT.Silu).then_inc(v1_ready, 1)
                act.wait_ge(nm_ready, i + 1)
                nc.scalar.activation(sc[:, i, :], sc[:, i, :], ACT.Exp, bias=m1[:, i:i + 1],
                                     accum_out=s1[:, i:i + 1]).then_inc(p_done, 1)
                roots(5 + 2 * i, slice(i, i + 1))
                act.wait_ge(nm1_ready, i + 1)
                nc.scalar.activation(ww[:, i, 0:K1], top8[:, i, 0:K1], ACT.Exp, bias=m1[:, i:i + 1],
                                     accum_out=ww[:, i, K1:K1 + 1]).then_inc(ex1_done, 1)
                if i == 0:
                    act.wait_ge(take_ready, NT)
                    act.dma_start(b2_bc, b2.partition_broadcast(P)).then_inc(b2_in, 16)
            act.wait_ge(rows_ready, 5 * NT)
            act.dma_start(rows1.rearrange("(i p) d -> p i d", p=P), a[:, :, :]).then_inc(rows1_out, 16)

            act.sem_inc(g_gelu, 2)

            def gelu(j, par):
                act.wait_ge(g_b1, j + 1)
                act.wait_ge(g_y, j + 1)
                for n in range(2):
                    act.wait_ge(g_hT, 2 * j + n + 3)
                    for q in range(KF // 2):
                        f = n * (KF // 2) + q
                        ins = nc.scalar.activation(hT1[:, f, :], ps[2 + n][:, tile(q)], ACT.Gelu,
                                                   bias=b1j[:, par, f:f + 1])
                    ins.then_inc(g_gelu, 1)

            gelu(0, 0)
            with act.Fori(0, (TILES1 - 3) // 2) as it:
                for u in range(2):
                    gelu(act.snap(it * 2 + u + 1), (u + 1) % 2)
            for j in range(TILES1 - 2, TILES1):
                gelu(j, j % 2)

        @block.tensor
        def _(pe):
            def turn(stage, i, bank, src):
                pe.wait_ge(rows_ready, stage * NT + i + 1 if stage < 3 else 3 * NT + 2 * i + stage - 2)
                for k in range(KD):
                    ins = nc.tensor.transpose(ps[bank][:, tile(k)], src[:, i, tile(k)], ident)
                ins.then_inc(T_mm, 1)

            pe.wait_ge(tok_in, 16 * 4)
            for i in range(NT):
                for k in range(KD):
                    nc.tensor.matmul(ps[i][:, 0:D], xa[:, k, tile(i)], wa[:, k, :], start=(k == 0), stop=False)
                nc.tensor.matmul(ps[i][:, 0:D], xb[:, tile(i)], wb, start=False, stop=True).then_inc(tok_mm, 1)
            pe.wait_ge(con_in, 16 * 4)
            pe.wait_ge(zero_set, 2)
            nc.tensor.matmul(ps[7][:, 0:2 * P], rel_sb[:, :].broadcast_to([BUCKETS + 1, P]), buck_sb[:, :], start=True, stop=True).then_inc(bias_mm, 1)
            pe.wait_ge(bias_sb, 1)
            for i in range(NT):
                turn(0, i, 4 + i, a)
            pe.wait_ge(T_sb, NT)
            pe.wait_ge(attn_in, 16 * 5)
            for c in range(KD):
                for which, done in ((0, q_mm), (1, k_mm)):
                    for k in range(KD):
                        lo = which * D + c * P
                        ins = nc.tensor.matmul(ps[2 * which + c][:, :], win[:, k, lo:lo + P], aT[:, k, :],
                                               start=(k == 0), stop=(k == KD - 1))
                    ins.then_inc(done, 1)
            for i in range(NT):
                for k in range(KD):
                    ins = nc.tensor.matmul(ps[4 + i][:, 0:D], aT[:, k, tile(i)], win[:, k, 2 * D:3 * D],
                                           start=(k == 0), stop=(k == KD - 1))
                ins.then_inc(v_mm, 1)

            pe.wait_ge(k_ready, KD)
            for u in range(NT * PAIRS):
                i, c, hd, bank = head_pair(u)
                keys = slice((i // 2) * SEQ, (i // 2 + 1) * SEQ)
                if u < PAIRS:
                    pe.wait_ge((q0_ready, q1_ready)[c], hd + 2)
                    if bank >= 4:
                        pe.wait_ge(v_ready, bank - 3)
                    elif bank < 2:
                        pe.wait_ge((q0_ready, q1_ready)[bank], 8)
                else:
                    pe.wait_ge(exp_done, 2 * (u - 8) + 2)
                for par in range(2):
                    ins = nc.tensor.matmul(ps[bank][:, par * SEQ:(par + 1) * SEQ], q_one[:, 8 * c + hd + par, tile(i)],
                                           kT[:, c, keys], start=True, stop=True)
                ins.then_inc(score_mm, 1)

            pe.wait_ge(exp_done, 2 * NT * PAIRS)
            for i in range(NT):
                turn(1, i, i, opt)
            for i in range(NT):
                pe.wait_ge(T_sb, NT + i + 1)
                for k in range(KD):
                    ins = nc.tensor.matmul(ps[4 + i][:, 0:D], optT[:, k, tile(i)], wout_sb[:, k * D:(k + 1) * D],
                                           start=(k == 0), stop=(k == KD - 1))
                ins.then_inc(proj_mm, 1)
            for i in range(NT):
                turn(2, i, i, a)
            for i in range(NT):
                pe.wait_ge(T_sb, 2 * NT + i + 1)
                for k in range(KD):
                    ins = nc.tensor.matmul(ps[4 + i][:, 0:E0], aT[:, k, tile(i)],
                                           r0_sb[:, k * E0:(k + 1) * E0], start=(k == 0), stop=(k == KD - 1))
                ins.then_inc(log0_mm, 1)

            def shared(i):
                u = RING - 1
                pe.wait_ge(ring_in[u], 32)
                if i >= 2:
                    pe.wait_ge(s_hid, i - 1)
                for k in range(KD):
                    ins = nc.tensor.matmul(ps[i % 2][:, 0:2 * F0], aT[:, k, tile(i)],
                                           ring_gu[u][:, k * 2 * F0:(k + 1) * 2 * F0], start=(k == 0), stop=(k == KD - 1))
                ins.then_inc(s_gu, 1)

            def shared_down(i):
                par, u = i % 2, RING - 1
                pe.wait_ge(s_hid, i + 1)
                for k in range(2):
                    ins = nc.tensor.transpose(ps[2 + par][0:FH, tile(k)],
                                              hid[:, par, k * FH:(k + 1) * FH], ident)
                ins.then_inc(s_hT, 1)
                pe.wait_ge(s_hTs, i + 1)
                if i >= 2:
                    pe.wait_ge(s_res, i - 1)
                for k in range(2):
                    ins = nc.tensor.matmul(ps[4 + par][:, 0:D], hidT[:, par, tile(k)],
                                           ring_dn[u][:, k * D:(k + 1) * D], start=(k == 0), stop=(k == 1))
                ins.then_inc(s_dn, 1)

            def positions(bank, m, width, done, wanted):
                pe.wait_ge(wanted, 1)
                for i in range(NT):
                    for b in range(i + 1):
                        ins = nc.tensor.matmul(ps[bank][:, i * width:(i + 1) * width], upper if b == i else ones,
                                               m[:, b, :], start=(b == 0), stop=(b == i))
                ins.then_inc(done, 1)

            def dispatch(i):
                pe.wait_ge(digits_ready, i + 1)
                for g in range(8):
                    ins = nc.tensor.matmul(ps[7][:, g * 64:(g + 1) * 64],
                                           oneA[:, i % 2, 8 * g:8 * g + 8, :].rearrange("p a b -> p (a b)"),
                                           rhsB[:, i % 2, g, :],
                                           start=(i == 0 and g == 0), stop=(i == NT - 1),
                                           skip_group_check=True)
                ins.then_inc(disp_mm, 1)

            positions(6, mask, E0, pos_mm, mask_ready)
            shared(0)
            shared(1)
            for i in range(NT):
                dispatch(i)
                if i < NT - 1:
                    shared_down(i)
                if i + 2 < NT:
                    shared(i + 2)
            pe.wait_ge(mid_ready, 1)
            nc.tensor.matmul(ps[6][:, :], con[:, C_EXP0:C_EXP0 + P], mid, start=True, stop=True).then_inc(slot_mm, 1)
            shared_down(NT - 1)

            pe.wait_ge(s_res, NT)
            for done, credit in ((xT_mm, 4), (gu_mm, 2), (hT_mm, 2), (y_mm, 2)):
                pe.sem_inc(done, credit)

            def turn_x(e, u, turn_no):
                pe.wait_ge(xg_in[u], 16 * turn_no)
                pe.wait_ge(xT_sb, e + 1)
                for k in range(KD):
                    ins = nc.tensor.transpose(ps[6 + u % 2][:, tile(k)], xg[:, u, tile(k)], ident)
                ins.then_inc(xT_mm, 1)

            def gate_up_mm(e, u, turn_no):
                pe.wait_ge(ring_in[u], 32 * (turn_no + (1 if u == RING - 1 else 0)))
                pe.wait_ge(xT_sb, e + 3)
                pe.wait_ge(hid_done, e + 1)
                for k in range(KD):
                    ins = nc.tensor.matmul(ps[u % 2][:, 0:2 * F0], xTs[:, u % 2, k, :],
                                           ring_gu[u][:, k * 2 * F0:(k + 1) * 2 * F0], start=(k == 0), stop=(k == KD - 1))
                ins.then_inc(gu_mm, 1)

            def turn_h(e, u):
                pe.wait_ge(hid_done, e + 3)
                pe.wait_ge(hT_sb, e + 1)
                for k in range(2):
                    ins = nc.tensor.transpose(ps[2 + u % 2][0:FH, tile(k)], hid[:, u % 2, k * FH:(k + 1) * FH], ident)
                ins.then_inc(hT_mm, 1)

            def down_mm(e, u):
                pe.wait_ge(hT_sb, e + 3)
                pe.wait_ge(y_sb, e + 1)
                for k in range(2):
                    ins = nc.tensor.matmul(ps[4 + u % 2][:, 0:D], hidT[:, u % 2, tile(k)],
                                           ring_dn[u][:, k * D:(k + 1) * D], start=(k == 0), stop=(k == 1))
                ins.then_inc(y_mm, 1)

            turn_x(0, 0, 1)
            turn_x(1, 1, 1)
            gate_up_mm(0, 0, 1)
            with pe.Fori(0, E0 // 4 - 1) as it:
                for v in range(4):
                    e = pe.snap(it * 4 + v + 1)
                    turn_h(e - 1, v)
                    turn_x(e + 1, (v + 2) % 4, it + (v + 2) // 4 + 1)
                    gate_up_mm(e, (v + 1) % 4, it + (v + 1) // 4 + 1)
                    down_mm(e - 1, v)
            for e in range(E0 - 3, E0):
                turn_h(e - 1, (e - 1) % 4)
                if e + 1 < E0:
                    turn_x(e + 1, (e + 1) % 4, (e + 1) // 4 + 1)
                gate_up_mm(e, e % 4, e // 4 + 1)
                down_mm(e - 1, (e - 1) % 4)
            turn_h(E0 - 1, 3)
            down_mm(E0 - 1, 3)

            for i in range(NT):
                turn(3, i, 0, a)
                pe.wait_ge(T_sb, 3 * NT + 2 * i + 1)
                for k in range(KD):
                    ins = nc.tensor.matmul(ps[4][:, 0:P], wqk_sb[:, tile(k)], aT[:, k, tile(i)],
                                           start=(k == 0), stop=(k == KD - 1))
                ins.then_inc(z_mm, 1)
                for k in range(KD):
                    ins = nc.tensor.matmul(ps[1][:, 0:D], aT[:, k, tile(i)], wv_sb[:, k * D:(k + 1) * D],
                                           start=(k == 0), stop=(k == KD - 1))
                ins.then_inc(v1_mm, 1)
                pe.wait_ge(qk1_ready, 2 * (i + 1))
                nc.tensor.matmul(ps[5][:, 0:P], qz[:, i, :], kz[:, i, :], start=True, stop=True).then_inc(sim_mm, 1)
                pe.wait_ge(p_done, i + 1)
                nc.tensor.transpose(ps[2][:, 0:P], sc[:, i, :], ident).then_inc(p_T, 1)
                pe.wait_ge(pT_ready, i + 1)
                pe.wait_ge(v1_ready, i + 1)
                nc.tensor.matmul(ps[3][:, 0:D], pT[:, i, :], v1[:, i, :], start=True, stop=True).then_inc(o_mm, 1)
                turn(4, i, 6, a)
                pe.wait_ge(T_sb, 3 * NT + 2 * i + 2)
                for k in range(KD):
                    ins = nc.tensor.matmul(ps[7][:, 0:E1], aT[:, k, tile(i)],
                                           r1_sb[:, k * E1:(k + 1) * E1], start=(k == 0), stop=(k == KD - 1))
                ins.then_inc(log1_mm, 1)
            pe.wait_ge(mask1_ready, 1)
            for b in range(NT):
                nc.tensor.matmul(ps[5][:, NT * E1:(NT + 1) * E1], ones, mask1[:, b, :], start=(b == 0), stop=(b == NT - 1))
            positions(5, mask1, E1, pos1_mm, mask1_ready)
            pe.wait_ge(hot1_ready, 1)
            for n in range(NT * K1):
                i, k = divmod(n, K1)
                ins = nc.tensor.matmul(ps[6][:, 0:CB], oneA1[:, i, k, :], rhsB1[:, i, k, :],
                                       start=(n == 0), stop=(n == NT * K1 - 1))
            ins.then_inc(disp1_mm, 1)
            pe.wait_ge(mid1_ready, 1)
            nc.tensor.matmul(ps[7][:, 0:16 * CB], con[:, C_EXP1:C_EXP1 + P], mid1.rearrange("p a b -> p (a b)"),
                             start=True, stop=True).then_inc(slot1_mm, 1)

            pe.wait_ge(slots1_ready, 1)
            pe.wait_ge(ffn_in, 16 * 2 * E1)
            for done, credit in ((g_xT, 2), (g_h1, 4), (g_hT, 2), (g_y, 1)):
                pe.sem_inc(done, credit)

            def turn_x1(j, par, turn_no):
                pe.wait_ge(g_in[par], 16 * turn_no)
                pe.wait_ge(g_xTs, j + 1)
                for k in range(KD):
                    ins = nc.tensor.transpose(ps[6 + par][:, tile(k)], xg1[:, par, tile(k)], ident)
                ins.then_inc(g_xT, 1)

            def expert_of(j):
                return pe.value_load(tile_e[0:1, bass.ds(j, 1)], min_val=0, max_val=E1 - 1)

            def first_mm(j, par):
                e = expert_of(j)
                pe.wait_ge(g_xTs, j + 3)
                for n in range(2):
                    pe.wait_ge(g_h1s, 2 * j + n + 1)
                    for k in range(KD):
                        ins = nc.tensor.matmul(ps[n][:, :], xT1[:, par, k, :],
                                               w1_sb[:, bass.ds(e * (KD * F1) + (k * F1 + n * 512), 512)],
                                               start=(k == 0), stop=(k == KD - 1))
                    ins.then_inc(g_h1, 1)

            def second_mm(j, par):
                e = expert_of(j)
                pe.wait_ge(g_gelu, 2 * j + 4)
                pe.wait_ge(g_ysb, j + 1)
                for f in range(KF):
                    ins = nc.tensor.matmul(ps[4 + par][:, 0:D], hT1[:, f, :],
                                           w2_sb[:, bass.ds(e * (KF * D) + f * D, D)], start=(f == 0), stop=(f == KF - 1))
                ins.then_inc(g_y, 1)

            def turn_h1(j):
                for n in range(2):
                    pe.wait_ge(g_h1s, 2 * j + n + 3)
                    pe.wait_ge(g_gelu, 2 * j + n + 1)
                    for q in range(KF // 2):
                        f = n * (KF // 2) + q
                        ins = nc.tensor.transpose(ps[2 + n][:, tile(q)], h1s[:, tile(f)], ident)
                    ins.then_inc(g_hT, 1)

            turn_x1(0, 0, 1)
            turn_x1(1, 1, 1)
            first_mm(0, 0)
            turn_h1(0)
            with pe.Fori(0, (TILES1 - 3) // 2) as it:
                for v in range(2):
                    j = pe.snap(it * 2 + v + 1)
                    turn_x1(j + 1, v, it + 2)
                    first_mm(j, (v + 1) % 2)
                    second_mm(j - 1, v)
                    turn_h1(j)
            for j in range(TILES1 - 2, TILES1):
                if j + 1 < TILES1:
                    turn_x1(j + 1, (j + 1) % 2, (j + 1) // 2 + 1)
                first_mm(j, j % 2)
                second_mm(j - 1, (j - 1) % 2)
                turn_h1(j)
            second_mm(TILES1 - 1, (TILES1 - 1) % 2)

        @block.vector
        def _(dve):
            count = [0]

            def link(ins):
                count[0] += 1
                ins.then_inc(dve_chain, 1)
                dve.wait_ge(dve_chain, count[0])

            V = nc.vector
            V.memset(zero_row, 0.0).then_inc(zero_set, 1)
            V.memset(rel_sb[BUCKETS:BUCKETS + 1, :], 1.0).then_inc(zero_set, 1)

            def stats_of(i, src):
                return V.bn_stats(stats[:, i, :], src)

            def variances(tiles):
                for i in range(tiles.start, tiles.stop):
                    ins = V.bn_aggr(mv[:, i, :], stats[:, i, :])
                link(ins)
                V.tensor_scalar(mv[:, tiles, 1], mv[:, tiles, 1], EPS, None, ALU.add).then_inc(var_ready, 1)

            def reciprocals(count, tiles):
                dve.wait_ge(std_ready, count)
                link(V.reciprocal(rstd[:, tiles], std[:, tiles]))

            def normed(i):
                V.tensor_scalar(a[:, i, :], h[:, i, :], mv[:, i, 0:1], rstd[:, i:i + 1],
                                ALU.subtract, ALU.mult).then_inc(rows_ready, 1)

            def turned(count, i, bank, dst):
                dve.wait_ge(T_mm, count)
                V.tensor_copy(dst[:, :, tile(i)], ps[bank][:, 0:KD * P].rearrange("p (k t) -> p k t", k=KD)).then_inc(T_sb, 1)

            all_tiles = slice(0, NT)
            for i in range(NT):
                dve.wait_ge(tok_mm, i + 1)
                ins = stats_of(i, ps[i][:, 0:D])
            link(ins)
            variances(all_tiles)
            dve.wait_ge(con_in, 16 * 4)
            for i in range(NT):
                V.scalar_tensor_tensor(h[:, i, :], ps[i][:, 0:D], mv[:, i, 0:1], gamma_bc[:, :], ALU.subtract, ALU.mult)
            reciprocals(1, all_tiles)
            for i in range(NT):
                link(V.tensor_scalar(h[:, i, :], h[:, i, :], rstd[:, i:i + 1], None, ALU.mult))
                ins = stats_of(i, h[:, i, :])
            link(ins)
            variances(all_tiles)
            dve.wait_ge(bias_mm, 1)
            V.tensor_scalar(small[:, 0:2 * P], ps[7][:, 0:2 * P], float(ZQK) ** 0.5, None, ALU.mult).then_inc(bias_sb, 1)
            reciprocals(2, all_tiles)
            for i in range(NT):
                normed(i)
            for i in range(NT):
                turned(i + 1, i, 4 + i, aT)
            dve.wait_ge(attn_in, 16 * 5)
            for c in range(KD):
                ins = V.tensor_scalar(bq_one[:, c, :], con[:, C_HEAD:C_HEAD + 8], bqk0[:, c:c + 1], None, ALU.mult)
            ins.then_inc(qcol_ready, 1)
            dve.wait_ge(qcol_ready, 1)
            dve.wait_ge(q_mm, 1)

            def one_head(hd):
                V.tensor_scalar(q_one[:, hd, :], ps[0][:, :], con[:, C_HEAD + hd:C_HEAD + hd + 1],
                                bq_one[:, 0, hd:hd + 1], ALU.mult, ALU.add).then_inc(q0_ready, 1)

            for hd in range(4):
                one_head(hd)
            dve.wait_ge(bvec_in, 16 * 2)
            dve.wait_ge(zero_out, 16)
            for i in range(NT):
                dve.wait_ge(v_mm, i + 1)
                V.tensor_tensor(v0[:, i, :], ps[4 + i][:, 0:D], bvec_bc[:, 0:D], ALU.add).then_inc(v_ready, 1)
            for hd in range(4, 8):
                one_head(hd)

            def attended(i):
                cols = slice(i * HEADS, (i + 1) * HEADS)
                dve.wait_ge(exp_done, HEADS * (i + 1))
                link(V.reciprocal(erec[:, cols], esum[:, cols]))
                link(V.tensor_tensor(erec[:, cols], erec[:, cols], esum[:, cols], ALU.mult))
                V.tensor_tensor(opt[:, i, :].rearrange("p (h d) -> p h d", h=HEADS),
                                v0[:, i, :].rearrange("p (h d) -> p h d", h=HEADS),
                                spread(erec[:, cols], 2, HD), ALU.mult).then_inc(rows_ready, 1)

            for u in range(NT * PAIRS):
                i, c, hd, bank = head_pair(u)
                n = i * HEADS + 8 * c + hd
                dve.wait_ge(score_mm, u + 1)
                link(V.tensor_reduce(mx[:, n:n + 2], ps[bank][:, :].rearrange("p (a b) -> p a b", a=2), AX_X, ALU.max))
                V.tensor_scalar(nmx[:, n:n + 2], mx[:, n:n + 2], -ATT_SCALE, None, ALU.mult).then_inc(max_done, 1)
                if u >= PAIRS and u % PAIRS == 3:
                    attended(u // PAIRS - 1)
            attended(NT - 1)
            for i in range(NT):
                turned(NT + i + 1, i, i, optT)
            dve.wait_ge(hb_ready, 1)
            for i in range(NT):
                dve.wait_ge(proj_mm, i + 1)
                link(V.tensor_tensor(h[:, i, :], ps[4 + i][:, 0:D], h[:, i, :], ALU.add))
                ins = stats_of(i, h[:, i, :])
            link(ins)
            variances(all_tiles)
            reciprocals(3, all_tiles)
            for i in range(NT):
                normed(i)
            for i in range(NT):
                turned(2 * NT + i + 1, i, i, aT)

            for i in range(NT):
                dve.wait_ge(log0_mm, i + 1)
                ins = V.tensor_copy(lg[:, i, :], ps[4 + i][:, 0:E0])
            link(ins)
            for i in range(NT):
                ins = V.max(top8[:, i, :], lg[:, i, :])
            link(ins)
            for i in range(NT):
                ins = V.match_replace(rp[:, i, :], top8[:, i, :], lg[:, i, :], -3e38)
            link(ins)
            V.tensor_tensor(mask, rp, lg, ALU.not_equal).then_inc(mask_ready, 1)
            V.tensor_scalar(r_small[:, 0:NT], top8[:, :, 0], -1.0, None, ALU.mult).then_inc(nmax_ready, 1)
            for i in range(NT):
                V.max_index(id8[:, i, :], top8[:, i, :], lg[:, i, :])
            dve.wait_ge(mask_ready, 1)
            dve.wait_ge(bias_out, 16)
            dve.wait_ge(pos_mm, 1)
            pos = ps[6][:, 0:NT * E0].rearrange("p (i e) -> p i e", i=NT)
            link(V.scalar_tensor_tensor(kept, pos, float(CAP), mask, ALU.is_lt, ALU.mult))
            link(V.scalar_tensor_tensor(t1, pos, FAR, kept, ALU.subtract, ALU.mult))
            link(V.tensor_scalar(slot_i[:, :].rearrange("p (i e) -> p i e", i=NT), t1, FAR, None, ALU.add))
            V.tensor_scalar(dig_a[:, :], slot_i[:, :], 3, None, ALU.logical_shift_right)
            link(V.tensor_scalar(dig_b[:, :], slot_i[:, :], BB - 1, None, ALU.bitwise_and))
            iota_a = con[:, C_IOTA16:C_IOTA16 + BA]
            iota_b = con[:, C_IOTA16:C_IOTA16 + BB]

            def digits(i):
                if i >= 2:
                    dve.wait_ge(disp_mm, i - 1)
                if i:
                    dve.wait_ge(digits_ready, i)
                V.tensor_tensor(oneA[:, i % 2, :, :], spread(iota_a, 1, E0), spread(dig_a[:, i * E0:(i + 1) * E0], 2, BA),
                                ALU.is_equal)
                link(V.tensor_tensor(oneB, spread(iota_b, 1, E0), spread(dig_b[:, i * E0:(i + 1) * E0], 2, BB), ALU.is_equal))
                V.tensor_scalar(rhsB[:, i % 2, :, :], oneB.rearrange("p (g e) b -> p g (e b)", g=8),
                                con[:, C_TOK + i:C_TOK + i + 1], None, ALU.mult).then_inc(digits_ready, 1)

            def shared_hidden(i):
                dve.wait_ge(s_silu, i + 1)
                if i >= 2:
                    dve.wait_ge(s_hT, i - 1)
                V.tensor_tensor(hid[:, i % 2, :], ps[i % 2][:, F0:2 * F0], sil[:, i % 2, :], ALU.mult).then_inc(s_hid, 1)

            def shared_sum(i):
                dve.wait_ge(s_dn, i + 1)
                V.tensor_tensor(h[:, i, :], ps[4 + i % 2][:, 0:D], h[:, i, :], ALU.add).then_inc(s_res, 1)

            for i in range(NT):
                digits(i)
                shared_hidden(i)
                if i:
                    shared_sum(i - 1)
            dve.wait_ge(disp_mm, NT)
            V.tensor_tensor(mid.rearrange("p (g c) -> p g c", g=8), ps[7][:, :].rearrange("p (g c) -> p g c", g=8),
                            spread(con[:, C_DIAG:C_DIAG + 64], 1, 8), ALU.mult).then_inc(mid_ready, 1)
            V.tensor_tensor(rp, kept, spread(con[:, C_BASE:C_BASE + E0], 1, NT), ALU.mult)
            link(V.scalar_tensor_tensor(key, mask, float(DROPPED), t1, ALU.mult, ALU.add))
            link(V.tensor_tensor(key, key, rp, ALU.add))
            dve.wait_ge(slot_mm, 1)
            link(V.tensor_tensor(sel, ps[6][:, :].rearrange("p (e b) -> p e b", b=BB),
                                 spread(con[:, C_LOW0:C_LOW0 + BB], 1, E0), ALU.mult))
            link(V.tensor_reduce(tok_f[:, 0:E0], sel, AX_X, ALU.add))
            V.tensor_copy(tok0[:, :], tok_f[:, 0:E0]).then_inc(slots_ready, 1)
            shared_sum(NT - 1)
            dve.wait_ge(soft_done, 2 * NT)
            link(V.reciprocal(r_small[:, 2 * NT:3 * NT], r_small[:, NT:2 * NT]))
            link(V.tensor_tensor(wt8[:, :, :], wt8[:, :, :], spread(r_small[:, 2 * NT:3 * NT], 2, K0), ALU.mult))
            link(V.tensor_reduce(r_small[:, 3 * NT:4 * NT], wt8[:, :, :], AX_X, ALU.add))
            link(V.reciprocal(r_small[:, 2 * NT:3 * NT], r_small[:, 3 * NT:4 * NT]))
            link(V.tensor_tensor(wt8[:, :, :], wt8[:, :, :], spread(r_small[:, 2 * NT:3 * NT], 2, K0), ALU.mult))

            def choices(i):
                link(V.tensor_tensor(hot8, spread(con[:, C_ROW128:C_ROW128 + E0], 1, K0), spread(id8[:, i, :], 2, E0), ALU.is_equal))
                link(V.tensor_tensor(hot8, hot8, spread(key[:, i, :], 1, K0), ALU.mult))
                link(V.tensor_reduce(tok_f[:, 0:K0], hot8, AX_X, ALU.add))
                link(V.tensor_copy(take0[:, i * K0:(i + 1) * K0], tok_f[:, 0:K0]))
                dve.sem_inc(take_ready, 1)

            for i in range(2):
                choices(i)

            dve.sem_inc(xT_sb, 2)
            dve.sem_inc(hid_done, 2)
            dve.sem_inc(y_sb, 2)
            for u in range(4):
                dve.sem_inc(y_out[u], 16)

            def copy_x(e, par):
                dve.wait_ge(xT_mm, e + 5)
                dve.wait_ge(gu_mm, e + 1)
                V.tensor_copy(xTs[:, par, :, :].rearrange("p a b -> p (a b)"), ps[6 + par][:, 0:D]).then_inc(xT_sb, 1)

            def hidden(e, par):
                dve.wait_ge(silu_done, e + 1)
                dve.wait_ge(hT_mm, e + 1)
                V.tensor_tensor(hid[:, par, :], ps[par][:, F0:2 * F0], sil[:, par, :], ALU.mult).then_inc(hid_done, 1)

            def copy_y(e, u, turn_no):
                dve.wait_ge(y_mm, e + 3)
                dve.wait_ge(y_out[u], 16 * turn_no)
                V.tensor_copy(yb[:, u, :], ps[4 + u % 2][:, 0:D]).then_inc(y_sb, 1)

            copy_x(0, 0)
            copy_x(1, 1)
            hidden(0, 0)
            with dve.Fori(0, E0 // 4 - 1) as it:
                for v in range(4):
                    e = dve.snap(it * 4 + v + 1)
                    copy_x(e + 1, v % 2)
                    hidden(e, (v + 1) % 2)
                    copy_y(e - 1, v, it + 1)
            for e in range(E0 - 3, E0):
                if e + 1 < E0:
                    copy_x(e + 1, (e + 1) % 2)
                hidden(e, e % 2)
                copy_y(e - 1, (e - 1) % 4, (e - 1) // 4 + 1)
            copy_y(E0 - 1, 3, E0 // 4)

            for i in range(2, NT):
                choices(i)
            dve.wait_ge(late_in, 16 * 8)
            dve.wait_ge(bias_in, 16)

            def add_choice(i, k):
                n = i * K0 + k
                dve.wait_ge(take_in[k], 16 * (i + 1))
                if k:
                    dve.wait_ge(h2_ready, n)
                V.scalar_tensor_tensor(h[:, i, :], acc_in[:, k, :], wt8[:, i, k:k + 1], h[:, i, :],
                                       ALU.mult, ALU.add).then_inc(h2_ready, 1)

            def step(i, n):
                one = slice(i, i + 1)
                if n == 0:
                    dve.wait_ge(h2_ready, K0 * (i + 1))
                    link(stats_of(i, h[:, i, :]))
                    variances(one)
                elif n == 1:
                    reciprocals(4 + 2 * i, one)
                    normed(i)
                elif n == 2:
                    turned(3 * NT + 2 * i + 1, i, 0, aT)
                elif n == 3:
                    dve.wait_ge(z_ready, i + 1)
                    for m, dst in enumerate((qz, kz)):
                        V.tensor_scalar(dst[:, i, :], z[:, i, :], z_cols[:, 1 + m:2 + m], z_cols[:, 3 + m:4 + m],
                                        ALU.mult, ALU.add).then_inc(qk1_ready, 1)
                    dve.wait_ge(v1_mm, i + 1)
                    V.tensor_tensor(v1[:, i, :], ps[1][:, 0:D], bv1_bc[:, :], ALU.add).then_inc(vb_ready, 1)
                elif n == 4:
                    dve.wait_ge(sim_mm, i + 1)
                    link(V.scalar_tensor_tensor(sc[:, i, :], ps[5][:, 0:P], L1_SCALE, bias1[:, :], ALU.mult, ALU.add))
                    link(V.tensor_reduce(s1[:, one], sc[:, i, :], AX_X, ALU.max))
                    V.tensor_scalar(m1[:, one], s1[:, one], -1.0, None, ALU.mult).then_inc(nm_ready, 1)
                elif n == 5:
                    dve.wait_ge(p_done, i + 1)
                    V.reciprocal(i1[:, one], s1[:, one])
                    dve.wait_ge(p_T, i + 1)
                    V.tensor_copy(pT[:, i, :], ps[2][:, 0:P]).then_inc(pT_ready, 1)
                elif n == 6:
                    dve.wait_ge(pT_ready, i + 1)
                    dve.wait_ge(o_mm, i + 1)
                    link(V.scalar_tensor_tensor(h[:, i, :], ps[3][:, 0:D], i1[:, one], h[:, i, :], ALU.mult, ALU.add))
                    link(stats_of(i, h[:, i, :]))
                    variances(one)
                elif n == 7:
                    reciprocals(5 + 2 * i, one)
                    normed(i)
                elif n == 8:
                    turned(3 * NT + 2 * i + 2, i, 6, aT)
                elif n == 9:
                    dve.wait_ge(log1_mm, i + 1)
                    link(V.tensor_copy(lg1[:, i, :], ps[7][:, 0:E1]))
                    link(V.max(top8[:, i, :], lg1[:, i, :]))
                    V.tensor_scalar(m1[:, one], top8[:, i, 0:1], -1.0, None, ALU.mult).then_inc(nm1_ready, 1)
                    link(V.max_index(idx8[:, i, :], top8[:, i, :], lg1[:, i, :]))

            for i in range(NT):
                for k in range(K0):
                    add_choice(i, k)
                    if i:
                        step(i - 1, k)
                if i:
                    step(i - 1, 8)
                    step(i - 1, 9)
            for n in range(10):
                step(NT - 1, n)

            link(V.tensor_copy(ad, idx8[:, :, 0:K1]))
            link(V.tensor_tensor(hot.rearrange("p i k e -> p (i k) e"), spread(con[:, C_IOTA16:C_IOTA16 + E1], 1, NT * K1),
                                 spread(ad.rearrange("p i k -> p (i k)"), 2, E1), ALU.is_equal))
            V.tensor_tensor(mask1, hot[:, :, 0, :], hot[:, :, 1, :], ALU.add).then_inc(mask1_ready, 1)
            dve.wait_ge(ex1_done, NT)
            link(V.reciprocal(ww[:, :, 3:4], ww[:, :, K1:K1 + 1]))
            link(V.tensor_tensor(ww[:, :, 0:K1], ww[:, :, 0:K1], ww[:, :, 3:4].broadcast_to([P, NT, K1]), ALU.mult))
            dve.wait_ge(pos1_mm, 1)
            link(V.tensor_copy(cnt[:, 0, :], ps[5][:, NT * E1:(NT + 1) * E1]))
            link(V.tensor_scalar(cnt[:, 1, :], cnt[:, 0, :], 0.0, None, ALU.is_gt))
            for m in range(1, NT):
                link(V.scalar_tensor_tensor(cnt[:, 1, :], cnt[:, 0, :], float(m * P), cnt[:, 1, :], ALU.is_gt, ALU.add))
            link(V.tensor_copy(start1[:, 0, :], cnt[:, 1, :]))
            for n, step in enumerate((1, 2, 4)):
                src, dst = start1[:, n % 2, :], start1[:, (n + 1) % 2, :]
                V.tensor_copy(dst[:, 0:step], src[:, 0:step])
                link(V.tensor_tensor(dst[:, step:E1], src[:, step:E1], src[:, 0:E1 - step], ALU.add))
            last = start1[:, 1, :]
            link(V.tensor_scalar(last, last, float(P), None, ALU.mult))
            link(V.scalar_tensor_tensor(start1[:, 2, :], cnt[:, 1, :], -float(P), last, ALU.mult, ALU.add))
            pos_1 = ps[5][:, 0:NT * E1].rearrange("p (i e) -> p i e", i=NT)
            link(V.tensor_tensor(addr1, pos_1, spread(start1[:, 2, :], 1, NT), ALU.add))
            for k in range(K1):
                link(V.tensor_tensor(tmp1, hot[:, :, k, :], addr1, ALU.mult))
                link(V.tensor_reduce(ad[:, :, k], tmp1, AX_X, ALU.add))
            link(V.tensor_copy(adr_i[:, :].rearrange("p (i k) -> p i k", k=K1), ad))
            link(V.tensor_scalar(dga[:, :], adr_i[:, :], 4, None, ALU.logical_shift_right))
            link(V.tensor_copy(ad, dga[:, :].rearrange("p (i k) -> p i k", k=K1)))
            link(V.tensor_tensor(oneA1.rearrange("p i k s -> p (i k) s"), spread(con[:, C_ROW128:C_ROW128 + P], 1, NT * K1),
                                 spread(ad.rearrange("p i k -> p (i k)"), 2, P), ALU.is_equal))
            link(V.tensor_scalar(dga[:, :], adr_i[:, :], CB - 1, None, ALU.bitwise_and))
            link(V.tensor_copy(ad, dga[:, :].rearrange("p (i k) -> p i k", k=K1)))
            link(V.tensor_tensor(rhsB1.rearrange("p i k s -> p (i k) s"), spread(con[:, C_IOTA16:C_IOTA16 + CB], 1, NT * K1),
                                 spread(ad.rearrange("p i k -> p (i k)"), 2, CB), ALU.is_equal))
            for k in range(K1):
                ins = V.tensor_tensor(rhsB1[:, :, k, :], rhsB1[:, :, k, :], spread(con[:, C_TOK:C_TOK + NT], 2, CB), ALU.mult)
            ins.then_inc(hot1_ready, 1)
            link(V.tensor_tensor(tend, spread(last, 1, 16), spread(con[:, C_128J:C_128J + 16], 2, E1), ALU.is_le))
            link(V.tensor_reduce(ecol, tend, AX_X, ALU.add))
            link(V.tensor_scalar(tile_e[:, :], ecol, float(E1 - 1), None, ALU.min))
            dve.wait_ge(disp1_mm, 1)
            V.tensor_tensor(mid1, spread(ps[6][:, 0:CB], 1, 16), spread(con[:, C_TILE:C_TILE + 16], 2, CB),
                            ALU.mult).then_inc(mid1_ready, 1)
            dve.wait_ge(slot1_mm, 1)
            link(V.tensor_tensor(sel1, ps[7][:, 0:16 * CB].rearrange("p (g b) -> p g b", b=CB),
                                 spread(con[:, C_LOW1:C_LOW1 + CB], 1, 16), ALU.mult))
            link(V.tensor_reduce(ecol, sel1, AX_X, ALU.add))
            V.tensor_copy(tok1[:, :], ecol).then_inc(slots1_ready, 1)

            dve.wait_ge(slots1_ready, 1)
            dve.wait_ge(b2_in, 16)
            for done, credit in ((g_xTs, 2), (g_h1s, 2), (g_ysb, 2), (g_out[0], 16), (g_out[1], 16)):
                dve.sem_inc(done, credit)

            def expert_of(j):
                return dve.value_load(tile_e[0:1, bass.ds(j, 1)], min_val=0, max_val=E1 - 1)

            def copy_x1(j, par):
                dve.wait_ge(g_xT, j + 3)
                dve.wait_ge(g_h1, 2 * j + 2)
                V.tensor_copy(xT1[:, par, :, :].rearrange("p a b -> p (a b)"), ps[6 + par][:, 0:D]).then_inc(g_xTs, 1)

            def hidden1(j, par, first=False):
                e = expert_of(j)
                if not first:
                    dve.wait_ge(g_gelu, 2 * j)
                V.tensor_scalar(b1j[:, par, :], ptr(b1_sb, e * KF, KF), 1.0, None, ALU.mult).then_inc(g_b1, 1)
                for n in range(2):
                    dve.wait_ge(g_h1, 2 * j + n + 5)
                    dve.wait_ge(g_hT, 2 * j + n + 1)
                    V.tensor_copy(h1s[:, n * 512:(n + 1) * 512], ps[n][:, :]).then_inc(g_h1s, 1)

            def copy_y1(j, par, turn_no):
                e = expert_of(j)
                dve.wait_ge(g_y, j + 2)
                dve.wait_ge(g_out[par], 16 * turn_no)
                V.scalar_tensor_tensor(yb1[:, par, :], ps[4 + par][:, 0:D], 1.0, ptr(b2_bc, e * D, D),
                                       ALU.mult, ALU.add).then_inc(g_ysb, 1)

            copy_x1(0, 0)
            copy_x1(1, 1)
            hidden1(0, 0, first=True)
            with dve.Fori(0, (TILES1 - 3) // 2) as it:
                for v in range(2):
                    j = dve.snap(it * 2 + v + 1)
                    copy_x1(j + 1, v)
                    hidden1(j, (v + 1) % 2)
                    copy_y1(j - 1, v, it + 1)
            for j in range(TILES1 - 2, TILES1):
                if j + 1 < TILES1:
                    copy_x1(j + 1, (j + 1) % 2)
                hidden1(j, j % 2)
                copy_y1(j - 1, (j - 1) % 2, (j - 1) // 2 + 1)
            copy_y1(TILES1 - 1, (TILES1 - 1) % 2, (TILES1 - 1) // 2 + 1)
            for n in range(NT * K1):
                dve.wait_ge(take1_in[n], 16)
                V.scalar_tensor_tensor(h[:, n // K1, :], acc_in1[:, n, :], ww[:, n // K1, n % K1:n % K1 + 1], h[:, n // K1, :],
                                       ALU.mult, ALU.add).then_inc(final_ready, 1)
                dve.wait_ge(final_ready, n + 1)


def laid_out(v):
    c = np.ascontiguousarray

    def blocks(m):
        return c(m.reshape(-1, P, m.shape[-1]).transpose(1, 0, 2).reshape(P, -1))

    x = v["x"].reshape(2, 5, 16, PATCH, 16, PATCH).transpose(1, 3, 5, 0, 2, 4).reshape(FEAT, T)
    w_in = v["L0_attn_w_in"].reshape(HEADS, 3, HD, D).transpose(1, 0, 2, 3).reshape(3 * D, D)
    b_in = v["L0_attn_b_in"].reshape(HEADS, 3, HD).transpose(1, 0, 2).reshape(3, D)
    gu = np.concatenate([v["L0_ffn_w_gate"], v["L0_ffn_w_up"]], axis=-1)
    return {
        "x_in": c(x), "tok_w": c(v["L0_tok_W"]), "gamma": v["L0_tok_gamma"], "consts": constants(), "buckets": bucket_rows(),
        "w_in": c(w_in.T.reshape(KD, P, 3 * D).transpose(1, 0, 2)),
        "bq_in": c(b_in[0].reshape(KD, P).T), "bk_in": c(b_in[1].reshape(KD, P).T), "bv_in": c(b_in[2]),
        "w_out": blocks(v["L0_attn_w_out"].T), "b_out": v["L0_attn_b_out"], "router0": blocks(v["L0_ffn_router_w"].T),
        "gate_up": c(gu.reshape(E0, KD, P, 2 * F0).transpose(0, 2, 1, 3).reshape(E0, P, GU)),
        "down": c(v["L0_ffn_w_down"].reshape(E0, 2, FH, D).transpose(0, 2, 1, 3).reshape(E0, FH, DN)),
        "shared_gu": blocks(v["L0_ffn_ws_gate_up"]),
        "shared_dn": c(v["L0_ffn_ws_down"].reshape(2, FH, D).transpose(1, 0, 2).reshape(FH, DN)),
        "wqk": blocks(v["L1_attn_Wqk"]), "bqk": c(v["L1_attn_bqk"].reshape(P, 1)), "wv": blocks(v["L1_attn_Wv"]),
        "bv1": v["L1_attn_bv"], "gam1": c(v["L1_attn_gamma"].T), "bet1": c(v["L1_attn_beta"].T), "rel": v["L1_attn_rel_emb"],
        "router1": blocks(v["L1_ffn_router_w"].T),
        "w1": c(v["L1_ffn_w1"].transpose(0, 2, 1).reshape(E1, KD, P, F1).transpose(0, 2, 1, 3).reshape(E1, P, KD * F1)),
        "w2": c(v["L1_ffn_w2"].transpose(0, 2, 1).reshape(E1, KF, P, D).transpose(0, 2, 1, 3).reshape(E1, P, KF * D)),
        "b1": c(v["L1_ffn_b1"].reshape(E1, KF, P).transpose(2, 0, 1).reshape(P, E1 * KF)),
        "b2": c(v["L1_ffn_b2"].reshape(-1)),
    }


def kernel(**inputs):
    import concourse.bacc as bacc
    from concourse.bass_utils import run_bass_kernel_spmd as run

    nc = bacc.Bacc("TRN2", target_bir_lowering=False, num_devices=1)
    arrays = laid_out({k: np.asarray(v) for k, v in inputs.items()})
    args = {k: nc.dram_tensor(k, a.shape, mybir.dt.from_np(a.dtype), kind="ExternalInput").ap() for k, a in arrays.items()}
    out = nc.dram_tensor("out", (T, D), F32, kind="ExternalOutput").ap()
    vit_tower(nc, out=out, **args)
    r = run(nc, [arrays], core_ids=[0])
    return r.results[0]["out"].reshape(2, SEQ, D)
```

```python
from contextlib import ExitStack

import numpy as np

import concourse.bass as bass
from concourse import mybir

F32 = mybir.dt.float32
BF16 = mybir.dt.bfloat16
I32 = mybir.dt.int32
U32 = mybir.dt.uint32
ALU = mybir.AluOpType
ACT = mybir.ActivationFunctionType
AX_X = mybir.AxisListType.X

P = 128
D = 256
KD = D // P
T = 512
NT = T // P
PATCH = 8
FEAT = 5 * PATCH * PATCH
FB = (FEAT - P) // 2
EPS = 1e-5

HEADS, HD = 16, 16
SEQ = 256
PAIRS = HEADS // 2
SCORE_BANKS = 6
ATT_SCALE = 1.0 / HD ** 0.5

E0, K0, F0, CAP = 64, 8, 192, 128
FH = F0 // 2
GU = KD * 2 * F0
DN = 2 * D
RING = 4
BA, BB = 16, 8

ZQK = 128
L1_SCALE = D ** -0.5
BUCKETS, MAX_DISTANCE = 32, 128
LAG = 6

E1, K1, F1 = 8, 2, 1024
KF = F1 // P
TILES1 = (K1 * T + E1 * (P - 1)) // P
CB = 16
FAR = 1023.0
NOWHERE = 8192.0
NEG = -1e30

C_IDENT, C_EXP0, C_EXP1, C_ROW128 = (i * P for i in range(4))
C_DIAG = 4 * P
C_LOW0 = C_DIAG + 64
C_IOTA16 = C_LOW0 + BB
C_LOW_ROW = C_IOTA16 + 16
C_HIGH_ROW = C_LOW_ROW + 1
C_ROW1 = C_HIGH_ROW + NT
C_TILE1 = C_ROW1 + K1
C_TILE = C_TILE1 + NT
C_LOW1 = C_TILE + 16
C_HEAD = C_LOW1 + CB
C_128J = C_HEAD + 8
C_ENDS = C_128J + 16
C_ALL = C_ENDS + E1 * E1


def constants():
    c = np.zeros((P, C_ALL), np.float32)
    p = np.arange(P)[:, None]
    s = np.arange(P)[None, :]
    c[:, C_IDENT:C_IDENT + P] = p == s
    c[:, C_EXP0:C_EXP0 + P] = p % BA == s // BB
    c[:, C_EXP1:C_EXP1 + P] = p % 8 == s // CB
    c[:, C_ROW128:C_ROW128 + P] = s
    c[:, C_DIAG:C_DIAG + 64] = p // BA == np.arange(64)[None, :] // BB
    c[:, C_LOW0:C_LOW0 + BB] = np.arange(BB)[None, :] == p % BB
    c[:, C_IOTA16:C_IOTA16 + 16] = np.arange(16)
    c[:, C_LOW_ROW:C_LOW_ROW + 1] = 1 + K0 * p % P
    c[:, C_HIGH_ROW:C_HIGH_ROW + NT] = K0 * (p + P * np.arange(NT)[None, :]) // P * P
    c[:, C_ROW1:C_ROW1 + K1] = 1 + K1 * p + np.arange(K1)[None, :]
    c[:, C_TILE1:C_TILE1 + NT] = K1 * P * np.arange(NT)
    c[:, C_TILE:C_TILE + 16] = p // 8 == np.arange(16)[None, :]
    c[:, C_LOW1:C_LOW1 + CB] = np.arange(CB)[None, :] == p % CB
    c[:, C_HEAD:C_HEAD + 8] = p // HD == np.arange(8)[None, :]
    c[:, C_128J:C_128J + 16] = P * np.arange(16)
    c[:, C_ENDS:C_ENDS + E1 * E1] = P * np.tril(np.ones((E1, E1))).reshape(-1)
    return c


def counting():
    p = np.arange(P)
    return np.concatenate([p[:, None] < p[None, :], np.ones((P, P)), np.eye(P)], axis=1).astype(np.float32)


def bucket_rows():
    out = np.zeros((BUCKETS + 1, 2 * P), np.float32)
    n = np.arange(P)
    exact = BUCKETS // 2
    far = exact + (np.log((np.maximum(n, 1).astype(np.float32) / np.float32(exact)))
                   / np.float32(np.log(MAX_DISTANCE / exact)) * np.float32(BUCKETS - exact))
    far = np.minimum(far, BUCKETS - 1)
    b = np.where(n < exact, n.astype(np.float32), far).astype(np.int32)
    out[b, P - 1 - n] = 1
    out[BUCKETS, P:] = NEG
    return out


def vit_tower(nc, x_in, tok_w, gamma, consts, counters, buckets, w_in, bq_in, bk_in, bv_in, w_out, b_out,
              router0, gate_up, down, shared_gu, shared_dn, wqk, bqk, wv, bv1, gam1, bet1, rel,
              router1, w1, w2, b1, b2, out):
    rows0 = nc.dram_tensor("rows0", (T, D), F32).ap()
    rows1 = nc.dram_tensor("rows1", (T, D), F32).ap()
    y0 = nc.dram_tensor("y0", (T * K0, D), F32).ap()
    y1 = nc.dram_tensor("y1", (T * K1, D), F32).ap()
    bias_rows = nc.dram_tensor("bias_rows", (P, 2 * P), F32).ap()

    with ExitStack() as ctx:
        def sb(name, shape, dt=F32):
            return ctx.enter_context(nc.sbuf_tensor(name, shape, dt))

        def sem(name):
            return ctx.enter_context(nc.semaphore(name))

        ps = [ctx.enter_context(nc.psum_tensor(f"bank{i}", [P, 512], F32)) for i in range(8)]

        w1_sb = sb("w1_sb", [P, E1 * KD * F1])
        w2_sb = sb("w2_sb", [P, E1 * KF * D])
        ring_gu_all = sb("ring_gu_all", [P, RING * GU])
        ring_gu = [ring_gu_all[:, u * GU:(u + 1) * GU] for u in range(RING)]
        ring_dn = [sb(f"ring_dn{u}", [FH, DN]) for u in range(RING)]
        con = sb("con", [P, C_ALL])
        counts = sb("counts", [P, 3 * P], BF16)
        gamma_bc = sb("gamma_bc", [P, D])
        wout_sb = sb("wout_sb", [P, KD * D])
        r0_sb = sb("r0_sb", [P, KD * E0])
        bqk0 = sb("bqk0", [P, 4])
        bq_one = sb("bq_one", [P, KD, 8])
        wqk_sb = sb("wqk_sb", [P, KD * ZQK])
        wv_sb = sb("wv_sb", [P, KD * D])
        bv1_bc = sb("bv1_bc", [P, D])
        r1_sb = sb("r1_sb", [P, KD * E1])
        z_cols = sb("z_cols", [P, 5])
        b1_sb = sb("b1_sb", [P, E1 * KF])
        bias1 = sb("bias1", [P, P])
        h = sb("h", [P, NT, D])
        a = sb("a", [P, NT, D])
        aT = sb("aT", [P, KD, T])
        stats = sb("stats", [P, NT, 6])
        mv = sb("mv", [P, NT, 2])
        std = sb("std", [P, NT])
        rstd = sb("rstd", [P, NT])
        pool = sb("pool", [P, 8192])

        hidT_bvec = sb("hidT_bvec", [P, 2 * D])

        def at(start, *dims, parts=P):
            n = int(np.prod(dims))
            v = pool[0:parts, start:start + n]
            if len(dims) == 1:
                return v
            names = "abcd"[:len(dims)]
            return v.rearrange(f"p ({' '.join(names)}) -> p {' '.join(names)}",
                               **{k: d for k, d in zip(names[1:], dims[1:])})

        ident = con[:, C_IDENT:C_IDENT + P]
        upper = counts[:, 0:P]
        ones = counts[:, P:2 * P]
        ident_b = counts[:, 2 * P:3 * P]

        bvec_bc = hidT_bvec
        small = at(7936, 2 * P)
        counts_f = at(7168, 3 * P)
        xa = at(0, T)
        xb = at(512, 2, T, parts=FB)
        wa = at(1536, D)
        wb = at(1792, 2, D, parts=FB)
        win = at(2304, KD, 3 * D)
        q_one = w2_sb[:, E1 * KF * D // 2:].rearrange("p (h t) -> p h t", h=HEADS)
        kT = at(4864, KD, T)
        zeros = at(5888, D)
        v0 = at(6912, NT, D)
        mx, nmx, esum, erec = (at(1024 + 64 * n, NT * HEADS) for n in range(4))
        opt = at(1536, NT, D)
        optT = at(2560, KD, T)

        lg = at(0, NT, E0)
        rp = at(256, NT, E0)
        mask = at(512, NT * E0 // 2).bitcast(BF16).rearrange("p (i e) -> p i e", i=NT)
        pr = at(6144, NT, E0)
        kept = at(1280, NT, E0)
        t1 = at(1536, NT, E0)
        rank = at(5632, NT, E0)
        wt = at(6400, NT, E0)
        hot8 = at(5888, K0, E0)
        top8 = sb("top8", [P, NT, 8])
        r_small = sb("r_small", [P, 4 * NT])
        wt8 = sb("wt8", [P, NT, K0])
        maskT = at(768, T // 2, parts=E0).bitcast(BF16)
        slot_i = at(7936, NT * E0).bitcast(I32)
        dig_a = at(2048, NT * E0).bitcast(I32)
        dig_b = at(2304, NT * E0).bitcast(I32)
        oneA = at(2560, E0 * BA).bitcast(BF16).rearrange("p (t e a) -> p t e a", t=2, e=E0)
        oneB = at(4608, 2, E0, BB)
        rhsB = at(3584, 2 * E0 * BB).bitcast(BF16).rearrange("p (t n g c) -> p t n g c", t=2, n=2, g=8)
        mid = at(2560, 512)
        row_f, row_g = at(6656, E0), at(6720, E0)
        sel = at(4608, E0, BB)
        tok0 = sb("tok0", [P, E0], I32)
        row0 = sb("row0", [P, E0], I32)

        sil = at(7168, 2, F0)
        hid = at(7552, 2, F0)
        hidT = hidT_bvec[0:FH, :].rearrange("p (a b) -> p a b", a=2)
        xg = at(0, 4, D)
        xTs = at(1024, 2, KD, P)
        yb = at(1536, 4, D)
        acc_in = [at(0, K0, D), ring_gu_all[:, 0:K0 * D].rearrange("p (k d) -> p k d", k=K0), at(2048, K0, D), at(4096, K0, D)]
        idx_ring = sb("idx_ring", [P, 4], I32)
        out_ring = sb("out_ring", [P, 4], I32)

        z = at(2048, NT, P)
        qz = at(2560, NT, P)
        kz = at(3072, NT, P)
        v1 = at(3584, NT, D)
        sc = at(5632, NT, P)
        pT = at(5120, NT, P)
        m1 = sb("m1", [P, NT])
        s1 = sb("s1", [P, NT])
        i1 = sb("i1", [P, NT])
        lg1 = at(4608, NT, E1)
        mask1 = at(4640, NT * E1 // 2).bitcast(BF16).rearrange("p (i e) -> p i e", i=NT)
        addr1 = at(4704, NT, E1)
        over = at(4768, E1, NT)
        tiles, ends, starts = (at(4800 + n * E1, E1) for n in range(3))
        running = at(4928, E1, E1)
        picked = at(4992, NT, K1, E1)
        hot = at(4832, NT, K1, E1)
        ad = at(4896, NT, K1)
        ww = at(4904, NT, 4)
        oneA1 = at(0, NT * K1 * P // 2).bitcast(BF16).rearrange("p (i k s) -> p i k s", i=NT, k=K1)
        rhsB1 = at(1024, NT * K1 * CB).bitcast(BF16).rearrange("p (n i k s) -> p n i k s", n=2, i=NT, k=K1)
        oneB1 = at(1152, NT, K1, CB)
        mid1 = at(1280, 16, CB)
        sel1 = at(4928, 16, CB)
        tend = at(5472, 16, E1)
        ecol = at(5600, 16)
        idx8 = sb("idx8", [P, NT, 8], U32)
        adr_i = sb("adr_i", [P, NT * K1], I32)
        low_digit = sb("low_digit", [P, NT * K1], I32)
        high_digit = sb("high_digit", [P, NT * K1], I32)
        tok1 = sb("tok1", [P, 16], I32)
        row1 = sb("row1", [P, 16], I32)
        row1_f, row1_g = at(5616, 16), at(5632, 16)
        tile_e = sb("tile_e", [P, 16], I32)
        b2_bc = at(6144, E1 * D)
        b1j = sb("b1j", [P, 2, KF])
        xg1 = at(0, 2, D)
        xT1 = at(512, 2, KD, P)
        h1s = at(1024, F1)
        hT1 = at(2048, KF, P)
        yb1 = at(3328, 2, D)
        acc_in1 = at(0, NT, K1, D)

        buck_sb = at(3840, 2 * P, parts=BUCKETS + 1)
        rel_sb = sb("rel_sb", [BUCKETS + 1, 1])

        names = """tok_in tokb_in con_in bvec_in attn_in late_in b2_in ffn_in rows0_out zero_set zero_out rows1_out
            bias_mm bias_sb bias_out bias_in fin_out
            tok_mm emb_ready var_ready std_ready rows_ready T_mm T_sb q_mm k_mm v_mm qcol_ready q0_ready q1_ready k_ready v_ready
            score_mm max_done exp_done hb_ready proj_mm
            log0_mm nmax_ready soft_done mask_ready pos_mm maskT_mm maskT_sb rank_mm digits_ready rhs_ready low_ready disp_mm mid_ready
            slot_mm slots_ready rows_to_ready wt_ready s_gu s_silu s_hid s_hT s_hTs s_dn s_res
            xT_mm xT_sb gu_mm silu_done hid_done hT_mm hT_sb y_mm y_sb idx_ready gathers out_ready scatters
            h2_ready scored o_added z_mm z_ready qk1_ready v1_mm vb_ready v1_ready sim_mm nm_ready p_done p_T
            pT_ready o_mm
            log1_mm nm1_ready ex1_done mask1_ready pos1_mm hot1_ready disp1_mm mid1_ready slot1_mm
            slots1_ready rows1_to_ready g_xT g_xTs g_h1 g_h1s g_hT g_gelu g_y g_ysb g_b1 final_ready
            dve_chain""".split()
        s = {n: sem(n) for n in names}
        (tok_in, tokb_in, con_in, bvec_in, attn_in, late_in, b2_in, ffn_in, rows0_out, zero_set, zero_out, rows1_out,
         bias_mm, bias_sb, bias_out, bias_in, fin_out,
         tok_mm, emb_ready, var_ready, std_ready, rows_ready, T_mm, T_sb, q_mm, k_mm, v_mm, qcol_ready, q0_ready, q1_ready, k_ready, v_ready,
         score_mm, max_done, exp_done, hb_ready, proj_mm,
         log0_mm, nmax_ready, soft_done, mask_ready, pos_mm, maskT_mm, maskT_sb, rank_mm, digits_ready, rhs_ready, low_ready, disp_mm, mid_ready,
         slot_mm, slots_ready, rows_to_ready, wt_ready, s_gu, s_silu, s_hid, s_hT, s_hTs, s_dn, s_res,
         xT_mm, xT_sb, gu_mm, silu_done, hid_done, hT_mm, hT_sb, y_mm, y_sb, idx_ready, gathers, out_ready, scatters,
         h2_ready, scored, o_added, z_mm, z_ready, qk1_ready, v1_mm, vb_ready, v1_ready, sim_mm, nm_ready, p_done, p_T,
         pT_ready, o_mm,
         log1_mm, nm1_ready, ex1_done, mask1_ready, pos1_mm, hot1_ready, disp1_mm, mid1_ready, slot1_mm,
         slots1_ready, rows1_to_ready, g_xT, g_xTs, g_h1, g_h1s, g_hT, g_gelu, g_y, g_ysb, g_b1, final_ready,
         dve_chain) = s.values()
        ring_in = [sem(f"ring_in{u}") for u in range(RING)]
        xg_in = [sem(f"xg_in{u}") for u in range(4)]
        y_out = [sem(f"y_out{u}") for u in range(4)]
        take_in = [sem(f"take_in{u}") for u in range(NT)]
        take_half_in = sem("take_half_in")
        g_in = [sem(f"g_in{u}") for u in range(2)]
        g_out = [sem(f"g_out{u}") for u in range(2)]
        take1_in = [sem(f"take1_in{u}") for u in range(NT)]

        def tile(i):
            return slice(i * P, (i + 1) * P)

        def spread(ap, axis, n):
            v = ap.unsqueeze(axis)
            shape = list(v.shape)
            shape[axis] = n
            return v.broadcast_to(shape)

        def ptr(tensor, start, size=1):
            return tensor[:, bass.ds(start, size)]

        def head_pair(u):
            i, g = divmod(u, PAIRS)
            return i, g % 2, 2 * (g // 2), 2 + u % SCORE_BANKS

        adds = [(i, k) for _, i, k in sorted((K0 // 2 * i + k, i, k) for i in range(NT) for k in range(K0))]

        finals = [(i + m, k) for i in range(0, NT, 2) for k in range(K1) for m in range(2)]

        def added(i, k):
            return 1 + adds.index((i, k))

        block = ctx.enter_context(nc.Block())

        @block.sync
        def _(sp):
            sp.dma_start(xa, x_in[0:P, :]).then_inc(tok_in, 16)
            sp.dma_start(wa, tok_w[0:P, :]).then_inc(tok_in, 16)
            sp.dma_start(xb, x_in[P:FEAT, :].rearrange("(k p) t -> p k t", p=FB)).then_inc(tokb_in, 16)
            sp.dma_start(wb, tok_w[P:FEAT, :].rearrange("(k p) d -> p k d", p=FB)).then_inc(tokb_in, 16)
            sp.dma_start(win, w_in).then_inc(attn_in, 16)
            sp.dma_start(bvec_bc[:, 0:D], bv_in.partition_broadcast(P)).then_inc(bvec_in, 16)
            sp.dma_start(bvec_bc[:, D:2 * D], b_out.partition_broadcast(P)).then_inc(bvec_in, 16)
            sp.dma_start(wout_sb[:, :], w_out).then_inc(attn_in, 16)
            sp.dma_start(r0_sb[:, :], router0).then_inc(attn_in, 16)

            def load_expert(e, u):
                sp.dma_start(ring_gu[u], gate_up[bass.ds(e, 1), :, :].squeeze(0)).then_inc(ring_in[u], 16)
                sp.dma_start(ring_dn[u][:, :], down[bass.ds(e, 1), :, :].squeeze(0)).then_inc(ring_in[u], 16)

            sp.dma_start(ring_gu[RING - 1], shared_gu).then_inc(ring_in[RING - 1], 16)
            sp.dma_start(ring_dn[RING - 1][:, :], shared_dn).then_inc(ring_in[RING - 1], 16)
            for e in range(RING - 1):
                load_expert(e, e)
            def load_w2(e):
                sp.dma_start(w2_sb[:, e * KF * D:(e + 1) * KF * D], w2[e]).then_inc(ffn_in, 16)

            for e in range(E1):
                sp.dma_start(w1_sb[:, e * KD * F1:(e + 1) * KD * F1], w1[e]).then_inc(ffn_in, 16)
            for e in range(E1 // 2):
                load_w2(e)
            sp.wait_ge(zero_set, 1)
            sp.dma_start(y0.rearrange("(c p) d -> p c d", p=P), spread(zeros, 1, T * K0 // P)).then_inc(zero_out, 16)
            sp.wait_ge(exp_done, HEADS * NT)
            for e in range(E1 // 2, E1):
                load_w2(e)
            sp.wait_ge(s_dn, NT)
            load_expert(RING - 1, RING - 1)

            with sp.Fori(0, E0 // RING - 1) as it:
                for u in range(RING):
                    e = sp.snap(it * RING + u)
                    sp.wait_ge(y_mm, e + 3)
                    load_expert(e + RING, u)
            for u in range(RING):
                sp.wait_ge(y_out[u], 16 * (E0 // RING))
            for i, k, n, there in ((0, 0, K0 // 2, take_half_in), (0, K0 // 2, K0 // 2, take_in[0]),
                                   *((i, 0, K0, take_in[i]) for i in range(1, NT))):
                if i == 3:
                    sp.wait_ge(wt_ready, 1)
                sp.dma_start(acc_in[i][:, k:k + n, :],
                             y0[i * P * K0:(i + 1) * P * K0, :].rearrange("(p k) d -> p k d", k=K0)[:, k:k + n, :]).then_inc(there, 16)

            for u in range(2):
                sp.wait_ge(g_out[u], 16 * ((TILES1 + 1 - u) // 2))
            for i in range(NT):
                sp.dma_start(acc_in1[:, i, :, :], y1[i * P * K1:(i + 1) * P * K1, :].rearrange("(p k) d -> p k d", k=K1)).then_inc(take1_in[i], 16)
            for i in range(NT):
                sp.wait_ge(final_ready, finals.index((i, K1 - 1)) + 1)
                sp.dma_start(out[tile(i), :], h[:, i, :]).then_inc(fin_out, 16)
            sp.wait_ge(fin_out, 16 * NT)

        @block.gpsimd
        def _(pool_e):
            for dst, src in ((wqk_sb[:, :], wqk), (wv_sb[:, :], wv),
                             (bv1_bc[:, :], bv1.partition_broadcast(P)), (r1_sb[:, :], router1),
                             (z_cols[:, 0:1], bqk), (z_cols[:, 1:3], gam1), (z_cols[:, 3:5], bet1),
                             (b1_sb[:, :], b1)):
                pool_e.dma_start(dst, src).then_inc(late_in, 16)
            pool_e.wait_ge(rows_ready, NT)
            pool_e.wait_ge(bvec_in, 16 * 2)
            nc.gpsimd.tensor_tensor(h[:, :, :], h[:, :, :], spread(bvec_bc[:, D:2 * D], 1, NT),
                                    ALU.add).then_inc(hb_ready, 1)

            def gather(e, u, value):
                nc.gpsimd.tensor_copy(idx_ring[:, u:u + 1], ptr(tok0, e)).then_inc(idx_ready, 1)
                pool_e.wait_ge(idx_ready, value)
                pool_e.sem_inc(gathers, 1)
                pool_e.indirect_dma_start(xg[:, u, :], None, rows0, bass.IndirectOffsetOnAxis(idx_ring[:, u:u + 1], 0),
                                          bounds_check=T - 1, oob_is_err=False).then_inc(xg_in[u], 16)

            pool_e.wait_ge(slots_ready, 1)
            pool_e.wait_ge(rows0_out, 16)
            pool_e.sem_inc(idx_ready, 1)
            pool_e.sem_inc(out_ready, 1)

            def scatter(e, u, value):
                pool_e.wait_ge(y_sb, e + 3)
                nc.gpsimd.tensor_copy(out_ring[:, u:u + 1], ptr(row0, e)).then_inc(out_ready, 1)
                pool_e.wait_ge(out_ready, value)
                pool_e.sem_inc(scatters, 1)
                pool_e.indirect_dma_start(y0, bass.IndirectOffsetOnAxis(out_ring[:, u:u + 1], 0), yb[:, u, :], None,
                                          bounds_check=T * K0 - 1, oob_is_err=False).then_inc(y_out[u], 16)

            def gather_next(e, u):
                pool_e.wait_ge(xT_mm, e + 1)
                gather(e, u, e + 2)

            for u in range(4):
                gather(u, u, u + 2)
            pool_e.wait_ge(rows_to_ready, 1)
            pool_e.wait_ge(zero_out, 16)
            for e in range(4, 8):
                gather_next(e, e % 4)
                if e >= LAG:
                    scatter(e - LAG, (e - LAG) % 4, e - LAG + 2)
            with pool_e.Fori(2, E0 // 4) as it:
                for u in range(4):
                    e = pool_e.snap(it * 4 + u)
                    gather_next(e, u)
                    scatter(e - LAG, (u - LAG) % 4, e - LAG + 2)
            for e in range(E0 - LAG, E0):
                scatter(e, e % 4, e + 2)

            def gather1(j):
                pool_e.indirect_dma_start(xg1[:, j % 2, :], None, rows1, bass.IndirectOffsetOnAxis(tok1[:, j:j + 1], 0),
                                          bounds_check=T - 1, oob_is_err=False).then_inc(g_in[j % 2], 16)

            pool_e.wait_ge(slots1_ready, 1)
            pool_e.wait_ge(rows1_out, 16)
            gather1(0)
            gather1(1)
            pool_e.wait_ge(rows1_to_ready, 1)
            pool_e.wait_ge(g_xT, 3)
            gather1(2)
            for j in range(TILES1):
                if j + 3 < TILES1:
                    pool_e.wait_ge(g_xT, j + 4)
                    gather1(j + 3)
                pool_e.wait_ge(g_ysb, j + 3)
                pool_e.indirect_dma_start(y1, bass.IndirectOffsetOnAxis(row1[:, j:j + 1], 0), yb1[:, j % 2, :], None,
                                          bounds_check=T * K1 - 1, oob_is_err=False).then_inc(g_out[j % 2], 16)

        @block.scalar
        def _(act):
            act.dma_start(con[:, :], consts).then_inc(con_in, 16)
            act.dma_start(gamma_bc[:, :], gamma.partition_broadcast(P)).then_inc(con_in, 16)
            for dst, src in ((counts_f, counters), (buck_sb[:, :], buckets), (rel_sb[0:BUCKETS, :], rel)):
                act.dma_start(dst, src).then_inc(con_in, 16)
            act.dma_start(bqk0[:, 0:2], bq_in).then_inc(attn_in, 16)
            act.dma_start(bqk0[:, 2:4], bk_in).then_inc(attn_in, 16)

            def roots(count, tiles):
                act.wait_ge(var_ready, count)
                nc.scalar.activation(std[:, tiles], mv[:, tiles, 1], ACT.Sqrt).then_inc(std_ready, 1)

            all_tiles = slice(0, NT)
            def rows_turned(n, bank):
                for i in range(NT):
                    act.wait_ge(T_mm, n * NT + i + 1)
                    nc.scalar.activation(aT[:, :, tile(i)], ps[bank(i)][:, 0:KD * P].rearrange("p (k t) -> p k t", k=KD),
                                         ACT.Copy).then_inc(T_sb, 1)

            roots(1, all_tiles)
            roots(2, all_tiles)
            rows_turned(0, lambda i: 4 + i)
            act.wait_ge(attn_in, 16 * 5)

            def key_block(c):
                act.wait_ge(k_mm, c + 1)
                nc.scalar.activation(kT[:, c, :], ps[2 + c][:, :], ACT.Identity, bias=bqk0[:, 2 + c:3 + c]).then_inc(k_ready, 1)

            key_block(0)
            act.wait_ge(q_mm, 2)
            act.wait_ge(qcol_ready, 1)
            for hd in range(8):
                if hd == 2:
                    key_block(1)
                nc.scalar.activation(q_one[:, 8 + hd, :], ps[1][:, :], ACT.Identity,
                                     scale=con[:, C_HEAD + hd:C_HEAD + hd + 1],
                                     bias=bq_one[:, 1, hd:hd + 1]).then_inc(q1_ready, 1)
            for u in range(NT * PAIRS):
                i, c, hd, bank = head_pair(u)
                act.wait_ge(max_done, u + 1)
                for par in range(2):
                    n = i * HEADS + 8 * c + hd + par
                    scores = ps[bank][:, par * SEQ:(par + 1) * SEQ]
                    nc.scalar.activation(scores, scores, ACT.Exp, scale=ATT_SCALE, bias=nmx[:, n:n + 1],
                                         accum_out=esum[:, n:n + 1]).then_inc(exp_done, 1)
            act.wait_ge(bias_sb, 1)
            act.dma_start(bias_rows, small[:, 0:2 * P]).then_inc(bias_out, 16)
            act.wait_ge(bias_out, 16)
            act.dma_start(bias1[:, :], bass.AP(bias_rows.tensor, P - 1, [[2 * P - 1, P], [1, P]])).then_inc(bias_in, 16)
            roots(3, all_tiles)
            rows_turned(2, lambda i: i)
            act.dma_start(rows0.rearrange("(i p) d -> p i d", p=P), a[:, :, :]).then_inc(rows0_out, 16)
            act.wait_ge(maskT_mm, 1)
            nc.scalar.activation(maskT, ps[7][0:E0, :], ACT.Copy).then_inc(maskT_sb, 1)
            act.wait_ge(nmax_ready, 1)
            for i in range(NT):
                nc.scalar.activation(pr[:, i, :], lg[:, i, :], ACT.Exp, bias=r_small[:, i:i + 1],
                                     accum_out=r_small[:, NT + i:NT + i + 1]).then_inc(soft_done, 1)

            def numbered(i):
                act.wait_ge(digits_ready, i + 1)
                if i >= 2:
                    act.wait_ge(disp_mm, i - 1)
                nc.scalar.activation(rhsB[:, i % 2, 1, :, :].rearrange("p g c -> p (g c)"),
                                     oneB[:, i % 2, :, :].rearrange("p e b -> p (e b)"), ACT.Copy,
                                     scale=con[:, C_HIGH_ROW + i:C_HIGH_ROW + i + 1]).then_inc(rhs_ready, 1)

            def shared_silu(i):
                act.wait_ge(s_gu, i + 1)
                if i >= 2:
                    act.wait_ge(s_hid, i - 1)
                nc.scalar.activation(sil[:, i % 2, :], ps[i % 2][:, 0:F0], ACT.Silu).then_inc(s_silu, 1)

            def shared_turned(i):
                act.wait_ge(s_hT, i + 1)
                if i >= 2:
                    act.wait_ge(s_dn, i - 1)
                nc.scalar.activation(hidT[:, i % 2, :], ps[2][0:FH, 0:D], ACT.Copy).then_inc(s_hTs, 1)

            shared_silu(0)
            numbered(0)
            shared_silu(1)
            numbered(1)
            shared_turned(0)
            numbered(2)
            numbered(3)
            shared_silu(2)
            shared_turned(1)
            shared_silu(3)
            shared_turned(2)
            shared_turned(3)

            act.sem_inc(hT_sb, 2)

            def silu(e, par):
                act.wait_ge(gu_mm, e + 3)
                act.wait_ge(hid_done, e + 1)
                nc.scalar.activation(sil[:, par, :], ps[par][:, 0:F0], ACT.Silu).then_inc(silu_done, 1)

            def turned(e, par):
                act.wait_ge(hT_mm, e + 3)
                act.wait_ge(y_mm, e + 1)
                nc.scalar.activation(hidT[:, par, :], ps[2 + par][0:FH, 0:D], ACT.Copy).then_inc(hT_sb, 1)

            silu(0, 0)
            with act.Fori(0, E0 // 4 - 1) as it:
                for u in range(4):
                    e = act.snap(it * 4 + u + 1)
                    turned(e - 1, u % 2)
                    silu(e, (u + 1) % 2)
            for e in range(E0 - 3, E0):
                turned(e - 1, (e - 1) % 2)
                silu(e, e % 2)
            turned(E0 - 1, (E0 - 1) % 2)

            act.wait_ge(wt_ready, 1)
            act.dma_start(b2_bc, b2.partition_broadcast(P)).then_inc(b2_in, 16)
            roots(4, all_tiles)
            rows_turned(3, lambda i: i % 2)
            for i in range(NT):
                act.wait_ge(z_mm, i + 1)
                nc.scalar.activation(z[:, i, :], ps[2 + i % 2][:, 0:P], ACT.Silu, bias=z_cols[:, 0:1]).then_inc(z_ready, 1)
                act.wait_ge(vb_ready, i + 1)
                nc.scalar.activation(v1[:, i, :], v1[:, i, :], ACT.Silu).then_inc(v1_ready, 1)
            for i in range(NT):
                one = slice(i, i + 1)
                act.wait_ge(nm_ready, i + 1)
                nc.scalar.activation(sc[:, i, :], sc[:, i, :], ACT.Exp, bias=m1[:, one],
                                     accum_out=s1[:, one]).then_inc(p_done, 1)
            roots(5, all_tiles)
            rows_turned(4, lambda i: 4 + i % 2)
            act.wait_ge(nm1_ready, 1)
            for i in range(NT):
                nc.scalar.activation(ww[:, i, 0:K1], top8[:, i, 0:K1], ACT.Exp, bias=m1[:, i:i + 1],
                                     accum_out=ww[:, i, K1:K1 + 1]).then_inc(ex1_done, 1)
            act.wait_ge(rows_ready, 5 * NT)
            act.dma_start(rows1.rearrange("(i p) d -> p i d", p=P), a[:, :, :]).then_inc(rows1_out, 16)

            act.sem_inc(g_gelu, 2)

            def gelu(j, par):
                act.wait_ge(g_b1, j + 1)
                act.wait_ge(g_y, j + 1)
                for n in range(2):
                    act.wait_ge(g_hT, 2 * j + n + 3)
                    for q in range(KF // 2):
                        f = n * (KF // 2) + q
                        ins = nc.scalar.activation(hT1[:, f, :], ps[2 + n][:, tile(q)], ACT.Gelu,
                                                   bias=b1j[:, par, f:f + 1])
                    ins.then_inc(g_gelu, 1)

            gelu(0, 0)
            with act.Fori(0, (TILES1 - 3) // 2) as it:
                for u in range(2):
                    gelu(act.snap(it * 2 + u + 1), (u + 1) % 2)
            for j in range(TILES1 - 2, TILES1):
                gelu(j, j % 2)

        @block.tensor
        def _(pe):
            def turn(count, i, bank, src):
                pe.wait_ge(rows_ready, count)
                for k in range(KD):
                    ins = nc.tensor.transpose(ps[bank][:, tile(k)], src[:, i, tile(k)], ident)
                ins.then_inc(T_mm, 1)

            def keep_clock(bank):
                for _ in range(2):
                    nc.tensor.matmul(ps[bank][:, :], ident, con[:, 0:512], start=True, stop=True)

            pe.wait_ge(tok_in, 16 * 2)
            for i in range(NT):
                nc.tensor.matmul(ps[i][:, 0:D], xa[:, tile(i)], wa, start=True, stop=False)
            pe.wait_ge(tokb_in, 16 * 2)
            for i in range(NT):
                for k in range(2):
                    ins = nc.tensor.matmul(ps[i][:, 0:D], xb[:, k, tile(i)], wb[:, k, :], start=False, stop=(k == 1))
                ins.then_inc(tok_mm, 1)
            for i in range(NT):
                turn(i + 1, i, 4 + i, a)
            pe.wait_ge(T_sb, NT)
            pe.wait_ge(attn_in, 16 * 5)
            for c in range(KD):
                for which, done in ((0, q_mm), (1, k_mm)):
                    for k in range(KD):
                        lo = which * D + c * P
                        ins = nc.tensor.matmul(ps[2 * which + c][:, :], win[:, k, lo:lo + P], aT[:, k, :],
                                               start=(k == 0), stop=(k == KD - 1))
                    ins.then_inc(done, 1)
            pe.wait_ge(con_in, 16 * 5)
            pe.wait_ge(zero_set, 2)
            nc.tensor.matmul(ps[7][:, 0:2 * P], rel_sb[:, :].broadcast_to([BUCKETS + 1, P]), buck_sb[:, :],
                             start=True, stop=True).then_inc(bias_mm, 1)
            def values(i):
                if i < 2:
                    pe.wait_ge((q0_ready, q1_ready)[i], 8)
                else:
                    pe.wait_ge(v_ready, i - 1)
                for k in range(KD):
                    ins = nc.tensor.matmul(ps[i % 2][:, 0:D], aT[:, k, tile(i)], win[:, k, 2 * D:3 * D],
                                           start=(k == 0), stop=(k == KD - 1))
                ins.then_inc(v_mm, 1)

            def project(i):
                pe.wait_ge(T_sb, NT + i + 1)
                for k in range(KD):
                    ins = nc.tensor.matmul(ps[1][:, 0:D], optT[:, k, tile(i)], wout_sb[:, k * D:(k + 1) * D],
                                           start=(k == 0), stop=(k == KD - 1))
                ins.then_inc(proj_mm, 1)

            for u in range(NT * PAIRS):
                i, c, hd, bank = head_pair(u)
                keys = slice((i // 2) * SEQ, (i // 2 + 1) * SEQ)
                if u < PAIRS:
                    pe.wait_ge(k_ready, c + 1)
                    pe.wait_ge((q0_ready, q1_ready)[c], hd + 2)
                if u == 5:
                    pe.wait_ge(bias_sb, 1)
                if u >= SCORE_BANKS:
                    pe.wait_ge(exp_done, 2 * (u - SCORE_BANKS) + 2)
                for par in range(2):
                    ins = nc.tensor.matmul(ps[bank][:, par * SEQ:(par + 1) * SEQ], q_one[:, 8 * c + hd + par, tile(i)],
                                           kT[:, c, keys], start=True, stop=True)
                ins.then_inc(score_mm, 1)
                if u < PAIRS and u >= PAIRS - NT:
                    values(u - (PAIRS - NT))
                if u >= PAIRS and u % PAIRS == 5:
                    turn(NT + i, i - 1, 0, opt)
                if u >= PAIRS and u % PAIRS == 7:
                    project(i - 1)
            turn(2 * NT, NT - 1, 0, opt)
            project(NT - 1)
            keep_clock(7)

            def logits(i):
                pe.wait_ge(T_sb, 2 * NT + i + 1)
                for k in range(KD):
                    ins = nc.tensor.matmul(ps[4 + i][:, 0:E0], aT[:, k, tile(i)],
                                           r0_sb[:, k * E0:(k + 1) * E0], start=(k == 0), stop=(k == KD - 1))
                ins.then_inc(log0_mm, 1)

            for i in range(NT):
                turn(2 * NT + i + 1, i, i, a)
            for i in range(NT):
                logits(i)

            def shared(i):
                u = RING - 1
                pe.wait_ge(ring_in[u], 32)
                if i >= 2:
                    pe.wait_ge(s_hid, i - 1)
                for k in range(KD):
                    ins = nc.tensor.matmul(ps[i % 2][:, 0:2 * F0], aT[:, k, tile(i)],
                                           ring_gu[u][:, k * 2 * F0:(k + 1) * 2 * F0], start=(k == 0), stop=(k == KD - 1))
                ins.then_inc(s_gu, 1)

            def shared_down(i):
                par, u = i % 2, RING - 1
                pe.wait_ge(s_hid, i + 1)
                for k in range(2):
                    ins = nc.tensor.transpose(ps[2][0:FH, tile(k)],
                                              hid[:, par, k * FH:(k + 1) * FH], ident)
                ins.then_inc(s_hT, 1)
                pe.wait_ge(s_hTs, i + 1)
                if i >= 2:
                    pe.wait_ge(s_res, i - 1)
                for k in range(2):
                    ins = nc.tensor.matmul(ps[4 + par][:, 0:D], hidT[:, par, tile(k)],
                                           ring_dn[u][:, k * D:(k + 1) * D], start=(k == 0), stop=(k == 1))
                ins.then_inc(s_dn, 1)

            def positions(bank, m, width, done, wanted):
                pe.wait_ge(wanted, 1)
                for i in range(NT):
                    for b in range(i + 1):
                        ins = nc.tensor.matmul(ps[bank][:, i * width:(i + 1) * width], upper if b == i else ones,
                                               m[:, b, :], start=(b == 0), stop=(b == i))
                ins.then_inc(done, 1)

            def dispatch(i):
                pe.wait_ge(rhs_ready, i + 1)
                pe.wait_ge(low_ready, i + 1)
                for g in range(8):
                    for n in range(2):
                        ins = nc.tensor.matmul(ps[7][:, g * 64:(g + 1) * 64],
                                               oneA[:, i % 2, 8 * g:8 * g + 8, :].rearrange("p a b -> p (a b)"),
                                               rhsB[:, i % 2, n, g, :], start=(i == 0 and g == 0 and n == 0),
                                               stop=(i == NT - 1 and n == 1), skip_group_check=True)
                ins.then_inc(disp_mm, 1)

            keep_clock(3)
            positions(6, mask, E0, pos_mm, mask_ready)
            pe.wait_ge(nmax_ready, 1)
            for i in range(NT):
                ins = nc.tensor.matmul(ps[7][0:E0, tile(i)], mask[:, i, :], ident_b, start=True, stop=True)
            ins.then_inc(maskT_mm, 1)
            shared(0)
            pe.wait_ge(maskT_sb, 1)
            for i in range(NT):
                ins = nc.tensor.matmul(ps[3][:, i * E0:(i + 1) * E0], maskT[:, tile(i)], upper[0:E0, 0:E0], start=True, stop=True)
            ins.then_inc(rank_mm, 1)
            shared(1)
            dispatch(0)
            shared_down(0)
            dispatch(1)
            dispatch(2)
            shared(2)
            dispatch(3)
            pe.wait_ge(mid_ready, 1)
            nc.tensor.matmul(ps[6][:, :], con[:, C_EXP0:C_EXP0 + P], mid, start=True, stop=True).then_inc(slot_mm, 1)
            shared_down(1)
            shared(3)
            shared_down(2)
            shared_down(3)

            for done, credit in ((xT_mm, 4), (gu_mm, 2), (hT_mm, 2), (y_mm, 2)):
                pe.sem_inc(done, credit)

            def turn_x(e, u, turn_no):
                pe.wait_ge(xg_in[u], 16 * turn_no)
                pe.wait_ge(xT_sb, e + 1)
                for k in range(KD):
                    ins = nc.tensor.transpose(ps[6 + u % 2][:, tile(k)], xg[:, u, tile(k)], ident)
                ins.then_inc(xT_mm, 1)

            def gate_up_mm(e, u, turn_no):
                pe.wait_ge(ring_in[u], 32 * (turn_no + (1 if u == RING - 1 else 0)))
                pe.wait_ge(xT_sb, e + 3)
                pe.wait_ge(hid_done, e + 1)
                for k in range(KD):
                    ins = nc.tensor.matmul(ps[u % 2][:, 0:2 * F0], xTs[:, u % 2, k, :],
                                           ring_gu[u][:, k * 2 * F0:(k + 1) * 2 * F0], start=(k == 0), stop=(k == KD - 1))
                ins.then_inc(gu_mm, 1)

            def turn_h(e, u):
                pe.wait_ge(hid_done, e + 3)
                pe.wait_ge(hT_sb, e + 1)
                for k in range(2):
                    ins = nc.tensor.transpose(ps[2 + u % 2][0:FH, tile(k)], hid[:, u % 2, k * FH:(k + 1) * FH], ident)
                ins.then_inc(hT_mm, 1)

            def down_mm(e, u):
                pe.wait_ge(hT_sb, e + 3)
                pe.wait_ge(y_sb, e + 1)
                for k in range(2):
                    ins = nc.tensor.matmul(ps[4 + u % 2][:, 0:D], hidT[:, u % 2, tile(k)],
                                           ring_dn[u][:, k * D:(k + 1) * D], start=(k == 0), stop=(k == 1))
                ins.then_inc(y_mm, 1)

            turn_x(0, 0, 1)
            turn_x(1, 1, 1)
            gate_up_mm(0, 0, 1)
            pe.wait_ge(s_res, NT)
            with pe.Fori(0, E0 // 4 - 1) as it:
                for v in range(4):
                    e = pe.snap(it * 4 + v + 1)
                    turn_x(e + 1, (v + 2) % 4, it + (v + 2) // 4 + 1)
                    turn_h(e - 1, v)
                    gate_up_mm(e, (v + 1) % 4, it + (v + 1) // 4 + 1)
                    down_mm(e - 1, v)
            for e in range(E0 - 3, E0):
                if e + 1 < E0:
                    turn_x(e + 1, (e + 1) % 4, (e + 1) // 4 + 1)
                turn_h(e - 1, (e - 1) % 4)
                gate_up_mm(e, e % 4, e // 4 + 1)
                down_mm(e - 1, (e - 1) % 4)
            turn_h(E0 - 1, 3)
            down_mm(E0 - 1, 3)

            def turn1(n, i, bank):
                if i >= 2:
                    pe.wait_ge(T_sb, n * NT + i - 1)
                turn(n * NT + i + 1, i, bank, a)

            def sims(i):
                pe.wait_ge(qk1_ready, 2 * (i + 1))
                if i >= 2:
                    pe.wait_ge(scored, i - 1)
                nc.tensor.matmul(ps[6 + i % 2][:, 0:P], qz[:, i, :], kz[:, i, :], start=True, stop=True).then_inc(sim_mm, 1)

            def attend(i):
                pe.wait_ge(pT_ready, i + 1)
                pe.wait_ge(v1_ready, i + 1)
                if i >= 2:
                    pe.wait_ge(o_added, i - 1)
                nc.tensor.matmul(ps[2 + i % 2][:, 0:D], pT[:, i, :], v1[:, i, :], start=True, stop=True).then_inc(o_mm, 1)

            for i in range(NT):
                turn1(3, i, i % 2)
            for i in range(NT):
                b = i % 2
                pe.wait_ge(T_sb, 3 * NT + i + 1)
                if i >= 2:
                    pe.wait_ge(z_ready, i - 1)
                for k in range(KD):
                    ins = nc.tensor.matmul(ps[2 + b][:, 0:P], wqk_sb[:, tile(k)], aT[:, k, tile(i)],
                                           start=(k == 0), stop=(k == KD - 1))
                ins.then_inc(z_mm, 1)
                if i >= 2:
                    pe.wait_ge(vb_ready, i - 1)
                for k in range(KD):
                    ins = nc.tensor.matmul(ps[4 + b][:, 0:D], aT[:, k, tile(i)], wv_sb[:, k * D:(k + 1) * D],
                                           start=(k == 0), stop=(k == KD - 1))
                ins.then_inc(v1_mm, 1)
                if i:
                    sims(i - 1)
            sims(NT - 1)
            for i in range(NT):
                pe.wait_ge(p_done, i + 1)
                if i >= 2:
                    pe.wait_ge(pT_ready, i - 1)
                nc.tensor.transpose(ps[i % 2][:, 0:P], sc[:, i, :], ident).then_inc(p_T, 1)
                if i:
                    attend(i - 1)
            attend(NT - 1)
            turn1(4, 0, 4)
            for i in range(NT):
                if i + 1 < NT:
                    turn1(4, i + 1, 5 - i % 2)
                pe.wait_ge(T_sb, 4 * NT + i + 1)
                for k in range(KD):
                    ins = nc.tensor.matmul(ps[7][:, i * E1:(i + 1) * E1], aT[:, k, tile(i)],
                                           r1_sb[:, k * E1:(k + 1) * E1], start=(k == 0), stop=(k == KD - 1))
            ins.then_inc(log1_mm, 1)
            pe.wait_ge(mask1_ready, 1)
            for b in range(NT):
                nc.tensor.matmul(ps[5][:, NT * E1:(NT + 1) * E1], ones, mask1[:, b, :], start=(b == 0), stop=(b == NT - 1))
            positions(5, mask1, E1, pos1_mm, mask1_ready)
            pe.wait_ge(hot1_ready, 1)
            for n in range(NT * K1):
                i, k = divmod(n, K1)
                for part in range(2):
                    ins = nc.tensor.matmul(ps[6][:, 0:CB], oneA1[:, i, k, :], rhsB1[:, part, i, k, :],
                                           start=(n + part == 0), stop=(n == NT * K1 - 1 and part == 1))
            ins.then_inc(disp1_mm, 1)
            pe.wait_ge(mid1_ready, 1)
            nc.tensor.matmul(ps[7][:, 0:16 * CB], con[:, C_EXP1:C_EXP1 + P], mid1.rearrange("p a b -> p (a b)"),
                             start=True, stop=True).then_inc(slot1_mm, 1)

            pe.wait_ge(slots1_ready, 1)
            pe.wait_ge(ffn_in, 16 * 2 * E1)
            for done, credit in ((g_xT, 2), (g_h1, 4), (g_hT, 2), (g_y, 1)):
                pe.sem_inc(done, credit)

            def turn_x1(j, par, turn_no):
                pe.wait_ge(g_in[par], 16 * turn_no)
                pe.wait_ge(g_xTs, j + 1)
                for k in range(KD):
                    ins = nc.tensor.transpose(ps[6 + par][:, tile(k)], xg1[:, par, tile(k)], ident)
                ins.then_inc(g_xT, 1)

            def expert_of(j):
                return pe.value_load(tile_e[0:1, bass.ds(j, 1)], min_val=0, max_val=E1 - 1)

            def first_mm(j, par):
                e = expert_of(j)
                pe.wait_ge(g_xTs, j + 3)
                for n in range(2):
                    pe.wait_ge(g_h1s, 2 * j + n + 1)
                    for k in range(KD):
                        ins = nc.tensor.matmul(ps[n][:, :], xT1[:, par, k, :],
                                               w1_sb[:, bass.ds(e * (KD * F1) + (k * F1 + n * 512), 512)],
                                               start=(k == 0), stop=(k == KD - 1))
                    ins.then_inc(g_h1, 1)

            def second_mm(j, par):
                e = expert_of(j)
                pe.wait_ge(g_gelu, 2 * j + 4)
                pe.wait_ge(g_ysb, j + 1)
                for f in range(KF):
                    ins = nc.tensor.matmul(ps[4 + par][:, 0:D], hT1[:, f, :],
                                           w2_sb[:, bass.ds(e * (KF * D) + f * D, D)], start=(f == 0), stop=(f == KF - 1))
                ins.then_inc(g_y, 1)

            def turn_h1(j):
                for n in range(2):
                    pe.wait_ge(g_h1s, 2 * j + n + 3)
                    pe.wait_ge(g_gelu, 2 * j + n + 1)
                    for q in range(KF // 2):
                        f = n * (KF // 2) + q
                        ins = nc.tensor.transpose(ps[2 + n][:, tile(q)], h1s[:, tile(f)], ident)
                    ins.then_inc(g_hT, 1)

            turn_x1(0, 0, 1)
            turn_x1(1, 1, 1)
            first_mm(0, 0)
            turn_h1(0)
            with pe.Fori(0, (TILES1 - 3) // 2) as it:
                for v in range(2):
                    j = pe.snap(it * 2 + v + 1)
                    turn_x1(j + 1, v, it + 2)
                    first_mm(j, (v + 1) % 2)
                    second_mm(j - 1, v)
                    turn_h1(j)
            for j in range(TILES1 - 2, TILES1):
                if j + 1 < TILES1:
                    turn_x1(j + 1, (j + 1) % 2, (j + 1) // 2 + 1)
                first_mm(j, j % 2)
                second_mm(j - 1, (j - 1) % 2)
                turn_h1(j)
            second_mm(TILES1 - 1, (TILES1 - 1) % 2)

        @block.vector
        def _(dve):
            count = [0]

            def link(ins):
                count[0] += 1
                ins.then_inc(dve_chain, 1)
                dve.wait_ge(dve_chain, count[0])

            V = nc.vector
            V.memset(zeros, 0.0).then_inc(zero_set, 1)
            V.memset(rel_sb[BUCKETS:BUCKETS + 1, :], 1.0).then_inc(zero_set, 1)

            def stats_of(i, src):
                return V.bn_stats(stats[:, i, :], src)

            def variances(tiles):
                for i in range(tiles.start, tiles.stop):
                    ins = V.bn_aggr(mv[:, i, :], stats[:, i, :])
                link(ins)
                V.tensor_scalar(mv[:, tiles, 1], mv[:, tiles, 1], EPS, None, ALU.add).then_inc(var_ready, 1)

            def reciprocals(count, tiles):
                dve.wait_ge(std_ready, count)
                link(V.reciprocal(rstd[:, tiles], std[:, tiles]))

            def normed(i):
                V.tensor_scalar(a[:, i, :], h[:, i, :], mv[:, i, 0:1], rstd[:, i:i + 1],
                                ALU.subtract, ALU.mult).then_inc(rows_ready, 1)

            def turned(count, i, bank, dst):
                dve.wait_ge(T_mm, count)
                V.tensor_copy(dst[:, :, tile(i)], ps[bank][:, 0:KD * P].rearrange("p (k t) -> p k t", k=KD)).then_inc(T_sb, 1)

            all_tiles = slice(0, NT)
            for i in range(NT):
                dve.wait_ge(tok_mm, i + 1)
                ins = stats_of(i, ps[i][:, 0:D])
            link(ins)
            variances(all_tiles)
            dve.wait_ge(con_in, 16 * 5)
            for i in range(NT):
                V.scalar_tensor_tensor(h[:, i, :], ps[i][:, 0:D], mv[:, i, 0:1], gamma_bc[:, :], ALU.subtract, ALU.mult)
            reciprocals(1, all_tiles)
            for i in range(NT):
                V.tensor_scalar(h[:, i, :], h[:, i, :], rstd[:, i:i + 1], None, ALU.mult).then_inc(emb_ready, 1)
            for i in range(NT):
                dve.wait_ge(emb_ready, i + 1)
                ins = stats_of(i, h[:, i, :])
            link(ins)
            variances(all_tiles)
            reciprocals(2, all_tiles)
            for i in range(NT):
                normed(i)
            V.tensor_copy(counts[:, :], counts_f)
            dve.wait_ge(attn_in, 16 * 5)
            for c in range(KD):
                ins = V.tensor_scalar(bq_one[:, c, :], con[:, C_HEAD:C_HEAD + 8], bqk0[:, c:c + 1], None, ALU.mult)
            ins.then_inc(qcol_ready, 1)
            dve.wait_ge(qcol_ready, 1)
            dve.wait_ge(q_mm, 1)

            def one_head(hd):
                V.tensor_scalar(q_one[:, hd, :], ps[0][:, :], con[:, C_HEAD + hd:C_HEAD + hd + 1],
                                bq_one[:, 0, hd:hd + 1], ALU.mult, ALU.add).then_inc(q0_ready, 1)

            for hd in range(8):
                one_head(hd)
            dve.wait_ge(bias_mm, 1)
            V.tensor_scalar(small[:, 0:2 * P], ps[7][:, 0:2 * P], float(ZQK) ** 0.5, None, ALU.mult).then_inc(bias_sb, 1)
            dve.wait_ge(bvec_in, 16 * 2)

            def values(i):
                dve.wait_ge(v_mm, i + 1)
                V.tensor_tensor(v0[:, i, :], ps[i % 2][:, 0:D], bvec_bc[:, 0:D], ALU.add).then_inc(v_ready, 1)

            def attended(i):
                cols = slice(i * HEADS, (i + 1) * HEADS)
                dve.wait_ge(exp_done, HEADS * (i + 1))
                link(V.reciprocal(erec[:, cols], esum[:, cols]))
                link(V.tensor_tensor(erec[:, cols], erec[:, cols], esum[:, cols], ALU.mult))
                V.tensor_tensor(opt[:, i, :].rearrange("p (h d) -> p h d", h=HEADS),
                                v0[:, i, :].rearrange("p (h d) -> p h d", h=HEADS),
                                spread(erec[:, cols], 2, HD), ALU.mult).then_inc(rows_ready, 1)

            def projected(i):
                if i == 0:
                    dve.wait_ge(hb_ready, 1)
                dve.wait_ge(proj_mm, i + 1)
                link(V.tensor_tensor(h[:, i, :], ps[1][:, 0:D], h[:, i, :], ALU.add))
                link(stats_of(i, h[:, i, :]))

            for u in range(NT * PAIRS):
                i, c, hd, bank = head_pair(u)
                n = i * HEADS + 8 * c + hd
                dve.wait_ge(score_mm, u + 1)
                link(V.tensor_reduce(mx[:, n:n + 2], ps[bank][:, :].rearrange("p (a b) -> p a b", a=2), AX_X, ALU.max))
                V.tensor_scalar(nmx[:, n:n + 2], mx[:, n:n + 2], -ATT_SCALE, None, ALU.mult).then_inc(max_done, 1)
                if u < PAIRS and u >= PAIRS - NT:
                    values(u - (PAIRS - NT))
                if u >= PAIRS and u % PAIRS == 3:
                    attended(i - 1)
                if u >= PAIRS and u % PAIRS == 5:
                    turned(NT + i, i - 1, 0, optT)
                if u >= PAIRS and u % PAIRS == 7:
                    projected(i - 1)
            attended(NT - 1)
            turned(2 * NT, NT - 1, 0, optT)
            projected(NT - 1)
            variances(all_tiles)
            reciprocals(3, all_tiles)
            for i in range(NT):
                normed(i)
            for i in range(NT):
                dve.wait_ge(log0_mm, i + 1)
                ins = V.tensor_copy(lg[:, i, :], ps[4 + i][:, 0:E0])
            link(ins)
            for i in range(NT):
                ins = V.max(top8[:, i, :], lg[:, i, :])
            link(ins)
            for i in range(NT):
                ins = V.match_replace(rp[:, i, :], top8[:, i, :], lg[:, i, :], -3e38)
            link(ins)
            V.tensor_tensor(mask, rp, lg, ALU.not_equal).then_inc(mask_ready, 1)
            V.tensor_scalar(r_small[:, 0:NT], top8[:, :, 0], -1.0, None, ALU.mult).then_inc(nmax_ready, 1)
            dve.wait_ge(mask_ready, 1)
            dve.wait_ge(bias_out, 16)
            dve.wait_ge(pos_mm, 1)
            pos = ps[6][:, 0:NT * E0].rearrange("p (i e) -> p i e", i=NT)
            link(V.scalar_tensor_tensor(kept, pos, float(CAP), mask, ALU.is_lt, ALU.mult))
            link(V.scalar_tensor_tensor(t1, pos, FAR, kept, ALU.subtract, ALU.mult))
            link(V.tensor_scalar(slot_i[:, :].rearrange("p (i e) -> p i e", i=NT), t1, FAR, None, ALU.add))
            V.tensor_scalar(dig_a[:, :], slot_i[:, :], 3, None, ALU.logical_shift_right)
            link(V.tensor_scalar(dig_b[:, :], slot_i[:, :], BB - 1, None, ALU.bitwise_and))
            dve.wait_ge(zero_out, 16)
            dve.wait_ge(rank_mm, 1)
            V.tensor_copy(rank, ps[3][:, 0:NT * E0].rearrange("p (i e) -> p i e", i=NT))
            iota_a = con[:, C_IOTA16:C_IOTA16 + BA]
            iota_b = con[:, C_IOTA16:C_IOTA16 + BB]

            def digits(i):
                if i >= 2:
                    dve.wait_ge(disp_mm, i - 1)
                    dve.wait_ge(rhs_ready, i - 1)
                V.tensor_tensor(oneA[:, i % 2, :, :], spread(iota_a, 1, E0), spread(dig_a[:, i * E0:(i + 1) * E0], 2, BA),
                                ALU.is_equal)
                V.tensor_tensor(oneB[:, i % 2, :, :], spread(iota_b, 1, E0), spread(dig_b[:, i * E0:(i + 1) * E0], 2, BB),
                                ALU.is_equal).then_inc(digits_ready, 1)
                dve.wait_ge(digits_ready, i + 1)
                V.scalar_tensor_tensor(rhsB[:, i % 2, 0, :, :].rearrange("p g (e b) -> p (g e) b", b=BB),
                                       spread(rank[:, i, :], 2, BB), con[:, C_LOW_ROW:C_LOW_ROW + 1],
                                       oneB[:, i % 2, :, :], ALU.add, ALU.mult).then_inc(low_ready, 1)

            def shared_hidden(i):
                dve.wait_ge(s_silu, i + 1)
                if i >= 2:
                    dve.wait_ge(s_hT, i - 1)
                V.tensor_tensor(hid[:, i % 2, :], ps[i % 2][:, F0:2 * F0], sil[:, i % 2, :], ALU.mult).then_inc(s_hid, 1)

            def shared_sum(i):
                dve.wait_ge(s_dn, i + 1)
                V.tensor_tensor(h[:, i, :], ps[4 + i % 2][:, 0:D], h[:, i, :], ALU.add).then_inc(s_res, 1)

            digits(0)
            shared_hidden(0)
            digits(1)
            shared_hidden(1)
            digits(2)
            digits(3)
            dve.wait_ge(disp_mm, NT)
            V.tensor_tensor(mid.rearrange("p (g c) -> p g c", g=8), ps[7][:, :].rearrange("p (g c) -> p g c", g=8),
                            spread(con[:, C_DIAG:C_DIAG + 64], 1, 8), ALU.mult).then_inc(mid_ready, 1)
            shared_hidden(2)
            dve.wait_ge(soft_done, NT)
            V.tensor_tensor(wt, pr, mask, ALU.mult)
            dve.wait_ge(slot_mm, 1)
            link(V.tensor_tensor(sel, ps[6][:, :].rearrange("p (e b) -> p e b", b=BB),
                                 spread(con[:, C_LOW0:C_LOW0 + BB], 1, E0), ALU.mult))
            link(V.tensor_reduce(row_f, sel, AX_X, ALU.add))

            def token_and_row(tok, row, f, bits):
                link(V.tensor_scalar(row, f, 1.0, 1.0, ALU.max, ALU.subtract))
                return V.tensor_scalar(tok, row, bits, None, ALU.logical_shift_right)

            def empty_nowhere(row, f, g):
                link(V.tensor_scalar(g, f, 0.0, NOWHERE + 1, ALU.is_equal, ALU.mult))
                return V.scalar_tensor_tensor(row, f, -1.0, g, ALU.add, ALU.add)

            token_and_row(tok0[:, :], row0[:, :], row_f, 3).then_inc(slots_ready, 1)
            dve.wait_ge(slots_ready, 1)
            empty_nowhere(row0[:, :], row_f, row_g).then_inc(rows_to_ready, 1)
            shared_sum(0)
            shared_sum(1)
            shared_hidden(3)
            shared_sum(2)
            shared_sum(3)

            dve.sem_inc(xT_sb, 2)
            dve.sem_inc(hid_done, 2)
            dve.sem_inc(y_sb, 2)

            def copy_x(e, par):
                dve.wait_ge(xT_mm, e + 5)
                dve.wait_ge(gu_mm, e + 1)
                V.tensor_copy(xTs[:, par, :, :].rearrange("p a b -> p (a b)"), ps[6 + par][:, 0:D]).then_inc(xT_sb, 1)

            def hidden(e, par):
                dve.wait_ge(silu_done, e + 1)
                dve.wait_ge(hT_mm, e + 1)
                V.tensor_tensor(hid[:, par, :], ps[par][:, F0:2 * F0], sil[:, par, :], ALU.mult).then_inc(hid_done, 1)

            def copy_y(e, u, turn_no):
                dve.wait_ge(y_mm, e + 3)
                if turn_no is not None:
                    dve.wait_ge(y_out[u], 16 * turn_no)
                V.tensor_copy(yb[:, u, :], ps[4 + u % 2][:, 0:D]).then_inc(y_sb, 1)

            def weights(i):
                one = slice(i, i + 1)
                link(V.tensor_tensor(hot8, spread(con[:, C_IOTA16:C_IOTA16 + K0], 2, E0), spread(rank[:, i, :], 1, K0), ALU.is_equal))
                link(V.tensor_tensor(hot8, hot8, spread(wt[:, i, :], 1, K0), ALU.mult))
                V.reciprocal(r_small[:, 2 * NT + i:2 * NT + i + 1], r_small[:, NT + i:NT + i + 1])
                link(V.tensor_reduce(wt8[:, i, :], hot8, AX_X, ALU.add))
                link(V.tensor_scalar(wt8[:, i, :], wt8[:, i, :], r_small[:, 2 * NT + i:2 * NT + i + 1], None, ALU.mult))
                link(V.tensor_reduce(r_small[:, 3 * NT + i:3 * NT + i + 1], wt8[:, i, :], AX_X, ALU.add))
                link(V.reciprocal(r_small[:, 2 * NT + i:2 * NT + i + 1], r_small[:, 3 * NT + i:3 * NT + i + 1]))
                link(V.tensor_scalar(wt8[:, i, :], wt8[:, i, :], r_small[:, 2 * NT + i:2 * NT + i + 1], None, ALU.mult))

            copy_x(0, 0)
            copy_x(1, 1)
            weights(0)
            hidden(0, 0)
            weights(1)
            for e in range(1, 5):
                copy_x(e + 1, (e + 1) % 2)
                hidden(e, e % 2)
                copy_y(e - 1, e - 1, None)
            with dve.Fori(1, E0 // 4 - 1) as it:
                for v in range(4):
                    e = dve.snap(it * 4 + v + 1)
                    copy_x(e + 1, v % 2)
                    hidden(e, (v + 1) % 2)
                    copy_y(e - 1, v, it)
            for e in range(E0 - 3, E0):
                if e + 1 < E0:
                    copy_x(e + 1, (e + 1) % 2)
                hidden(e, e % 2)
                copy_y(e - 1, (e - 1) % 4, (e - 1) // 4)
            copy_y(E0 - 1, 3, E0 // 4 - 1)

            for i in range(2, NT):
                weights(i)
            dve.sem_inc(wt_ready, 1)
            dve.wait_ge(late_in, 16 * 8)
            dve.wait_ge(bias_in, 16)

            for i, k in adds:
                if (i, k) == (0, 0):
                    dve.wait_ge(take_half_in, 16)
                elif (i, k) == (0, K0 // 2) or k == 0:
                    dve.wait_ge(take_in[i], 16)
                if k:
                    dve.wait_ge(h2_ready, added(i, k - 1))
                V.scalar_tensor_tensor(h[:, i, :], acc_in[i][:, k, :], wt8[:, i, k:k + 1], h[:, i, :],
                                       ALU.mult, ALU.add).then_inc(h2_ready, 1)
                if i == NT - 1 and k >= K0 - NT:
                    t = k - (K0 - NT)
                    dve.wait_ge(h2_ready, added(t, K0 - 1))
                    ins = stats_of(t, h[:, t, :])

            link(ins)
            variances(all_tiles)
            reciprocals(4, all_tiles)
            for i in range(NT):
                normed(i)

            def score(i):
                one = slice(i, i + 1)
                dve.wait_ge(sim_mm, i + 1)
                V.scalar_tensor_tensor(sc[:, i, :], ps[6 + i % 2][:, 0:P], L1_SCALE, bias1[:, :],
                                       ALU.mult, ALU.add).then_inc(scored, 1)
                dve.wait_ge(scored, i + 1)
                link(V.tensor_reduce(s1[:, one], sc[:, i, :], AX_X, ALU.max))
                V.tensor_scalar(m1[:, one], s1[:, one], -1.0, None, ALU.mult).then_inc(nm_ready, 1)

            for i in range(NT):
                dve.wait_ge(z_ready, i + 1)
                for m, dst in enumerate((qz, kz)):
                    V.tensor_scalar(dst[:, i, :], z[:, i, :], z_cols[:, 1 + m:2 + m], z_cols[:, 3 + m:4 + m],
                                    ALU.mult, ALU.add).then_inc(qk1_ready, 1)
                dve.wait_ge(v1_mm, i + 1)
                V.tensor_tensor(v1[:, i, :], ps[4 + i % 2][:, 0:D], bv1_bc[:, :], ALU.add).then_inc(vb_ready, 1)
                if i:
                    score(i - 1)
            score(NT - 1)

            def add_attention(i):
                dve.wait_ge(o_mm, i + 1)
                V.scalar_tensor_tensor(h[:, i, :], ps[2 + i % 2][:, 0:D], i1[:, i:i + 1], h[:, i, :],
                                       ALU.mult, ALU.add).then_inc(o_added, 1)

            for i in range(NT):
                dve.wait_ge(p_done, i + 1)
                link(V.reciprocal(i1[:, i:i + 1], s1[:, i:i + 1]))
                dve.wait_ge(p_T, i + 1)
                V.tensor_copy(pT[:, i, :], ps[i % 2][:, 0:P]).then_inc(pT_ready, 1)
                if i:
                    add_attention(i - 1)
                if i >= 2:
                    dve.wait_ge(o_added, i - 1)
                    stats_of(i - 2, h[:, i - 2, :])
            dve.wait_ge(o_added, NT - 1)
            stats_of(NT - 2, h[:, NT - 2, :])
            add_attention(NT - 1)
            dve.wait_ge(o_added, NT)
            link(stats_of(NT - 1, h[:, NT - 1, :]))
            variances(all_tiles)
            reciprocals(5, all_tiles)
            for i in range(NT):
                normed(i)
            dve.wait_ge(log1_mm, 1)
            link(V.tensor_copy(lg1.rearrange("p i e -> p (i e)"), ps[7][:, 0:NT * E1]))
            for i in range(NT):
                ins = V.max(top8[:, i, :], lg1[:, i, :])
            link(ins)
            V.tensor_scalar(m1[:, :], top8[:, :, 0], -1.0, None, ALU.mult).then_inc(nm1_ready, 1)
            for i in range(NT):
                ins = V.max_index(idx8[:, i, :], top8[:, i, :], lg1[:, i, :])
            link(ins)

            link(V.tensor_tensor(hot, spread(spread(con[:, C_IOTA16:C_IOTA16 + E1], 1, K1), 1, NT),
                                 spread(idx8[:, :, 0:K1], 3, E1), ALU.is_equal))
            V.tensor_tensor(mask1, hot[:, :, 0, :], hot[:, :, 1, :], ALU.add).then_inc(mask1_ready, 1)
            dve.wait_ge(pos1_mm, 1)
            link(V.tensor_tensor(over, spread(ps[5][:, NT * E1:(NT + 1) * E1], 2, NT), spread(con[:, C_128J:C_128J + NT], 1, E1), ALU.is_gt))
            link(V.tensor_reduce(tiles, over, AX_X, ALU.add))
            link(V.tensor_tensor(running, spread(tiles, 1, E1),
                                 con[:, C_ENDS:C_ENDS + E1 * E1].rearrange("p (e f) -> p e f", e=E1), ALU.mult))
            link(V.tensor_reduce(ends, running, AX_X, ALU.add))
            link(V.scalar_tensor_tensor(starts, tiles, -float(P), ends, ALU.mult, ALU.add))
            link(V.tensor_tensor(addr1, ps[5][:, 0:NT * E1].rearrange("p (i e) -> p i e", i=NT), spread(starts, 1, NT), ALU.add))
            link(V.tensor_tensor(picked, hot, spread(addr1, 2, K1), ALU.mult))
            link(V.tensor_reduce(ad, picked, AX_X, ALU.add))
            link(V.tensor_copy(adr_i[:, :].rearrange("p (i k) -> p i k", k=K1), ad))
            V.tensor_scalar(low_digit[:, :], adr_i[:, :], CB - 1, None, ALU.bitwise_and)
            link(V.tensor_scalar(high_digit[:, :], adr_i[:, :], 4, None, ALU.logical_shift_right))
            V.tensor_tensor(oneB1.rearrange("p i k s -> p (i k) s"), spread(con[:, C_IOTA16:C_IOTA16 + CB], 1, NT * K1),
                            spread(low_digit[:, :], 2, CB), ALU.is_equal)
            link(V.tensor_tensor(oneA1.rearrange("p i k s -> p (i k) s"), spread(con[:, C_ROW128:C_ROW128 + P], 1, NT * K1),
                                 spread(high_digit[:, :], 2, P), ALU.is_equal))
            for k in range(K1):
                V.tensor_scalar(rhsB1[:, 0, :, k, :], oneB1[:, :, k, :], con[:, C_ROW1 + k:C_ROW1 + k + 1], None, ALU.mult)
            V.tensor_tensor(rhsB1[:, 1, :, :, :].rearrange("p i k s -> p i (k s)"), oneB1.rearrange("p i k s -> p i (k s)"),
                            spread(con[:, C_TILE1:C_TILE1 + NT], 2, K1 * CB), ALU.mult).then_inc(hot1_ready, 1)
            dve.wait_ge(disp1_mm, 1)
            V.tensor_tensor(mid1, spread(ps[6][:, 0:CB], 1, 16), spread(con[:, C_TILE:C_TILE + 16], 2, CB),
                            ALU.mult).then_inc(mid1_ready, 1)
            link(V.tensor_tensor(tend, spread(ends, 1, 16), spread(con[:, C_128J:C_128J + 16], 2, E1), ALU.is_le))
            link(V.tensor_reduce(ecol, tend, AX_X, ALU.add))
            V.tensor_scalar(tile_e[:, :], ecol, float(E1 - 1), None, ALU.min)
            dve.wait_ge(ex1_done, NT)
            link(V.reciprocal(ww[:, :, 3:4], ww[:, :, K1:K1 + 1]))
            link(V.tensor_tensor(ww[:, :, 0:K1], ww[:, :, 0:K1], ww[:, :, 3:4].broadcast_to([P, NT, K1]), ALU.mult))
            dve.wait_ge(slot1_mm, 1)
            link(V.tensor_tensor(sel1, ps[7][:, 0:16 * CB].rearrange("p (g b) -> p g b", b=CB),
                                 spread(con[:, C_LOW1:C_LOW1 + CB], 1, 16), ALU.mult))
            link(V.tensor_reduce(row1_f, sel1, AX_X, ALU.add))
            token_and_row(tok1[:, :], row1[:, :], row1_f, 1).then_inc(slots1_ready, 1)
            dve.wait_ge(slots1_ready, 1)
            empty_nowhere(row1[:, :], row1_f, row1_g).then_inc(rows1_to_ready, 1)

            dve.wait_ge(slots1_ready, 1)
            dve.wait_ge(b2_in, 16)
            for done, credit in ((g_xTs, 2), (g_h1s, 2), (g_ysb, 2)):
                dve.sem_inc(done, credit)

            def expert_of(j):
                return dve.value_load(tile_e[0:1, bass.ds(j, 1)], min_val=0, max_val=E1 - 1)

            def copy_x1(j, par):
                dve.wait_ge(g_xT, j + 3)
                dve.wait_ge(g_h1, 2 * j + 2)
                V.tensor_copy(xT1[:, par, :, :].rearrange("p a b -> p (a b)"), ps[6 + par][:, 0:D]).then_inc(g_xTs, 1)

            def hidden1(j, par, first=False):
                e = expert_of(j)
                if not first:
                    dve.wait_ge(g_gelu, 2 * j)
                V.tensor_scalar(b1j[:, par, :], ptr(b1_sb, e * KF, KF), 1.0, None, ALU.mult).then_inc(g_b1, 1)
                for n in range(2):
                    dve.wait_ge(g_h1, 2 * j + n + 5)
                    dve.wait_ge(g_hT, 2 * j + n + 1)
                    V.tensor_copy(h1s[:, n * 512:(n + 1) * 512], ps[n][:, :]).then_inc(g_h1s, 1)

            def copy_y1(j, par, turn_no):
                e = expert_of(j)
                dve.wait_ge(g_y, j + 2)
                if turn_no is not None:
                    dve.wait_ge(g_out[par], 16 * turn_no)
                V.scalar_tensor_tensor(yb1[:, par, :], ps[4 + par][:, 0:D], 1.0, ptr(b2_bc, e * D, D),
                                       ALU.mult, ALU.add).then_inc(g_ysb, 1)

            copy_x1(0, 0)
            copy_x1(1, 1)
            hidden1(0, 0, first=True)
            for j in range(1, 3):
                copy_x1(j + 1, (j + 1) % 2)
                hidden1(j, j % 2)
                copy_y1(j - 1, j - 1, None)
            with dve.Fori(1, (TILES1 - 3) // 2) as it:
                for v in range(2):
                    j = dve.snap(it * 2 + v + 1)
                    copy_x1(j + 1, v)
                    hidden1(j, (v + 1) % 2)
                    copy_y1(j - 1, v, it)
            for j in range(TILES1 - 2, TILES1):
                if j + 1 < TILES1:
                    copy_x1(j + 1, (j + 1) % 2)
                hidden1(j, j % 2)
                copy_y1(j - 1, (j - 1) % 2, (j - 1) // 2)
            copy_y1(TILES1 - 1, (TILES1 - 1) % 2, (TILES1 - 1) // 2)
            for i, k in finals:
                dve.wait_ge(take1_in[i], 16)
                if k:
                    dve.wait_ge(final_ready, finals.index((i, k - 1)) + 1)
                V.scalar_tensor_tensor(h[:, i, :], acc_in1[:, i, k, :], ww[:, i, k:k + 1], h[:, i, :],
                                       ALU.mult, ALU.add).then_inc(final_ready, 1)


def laid_out(v):
    c = np.ascontiguousarray

    def blocks(m):
        return c(m.reshape(-1, P, m.shape[-1]).transpose(1, 0, 2).reshape(P, -1))

    x = v["x"].reshape(2, 5, 16, PATCH, 16, PATCH).transpose(1, 3, 5, 0, 2, 4).reshape(FEAT, T)
    w_in = v["L0_attn_w_in"].reshape(HEADS, 3, HD, D).transpose(1, 0, 2, 3).reshape(3 * D, D)
    b_in = v["L0_attn_b_in"].reshape(HEADS, 3, HD).transpose(1, 0, 2).reshape(3, D)
    gu = np.concatenate([v["L0_ffn_w_gate"], v["L0_ffn_w_up"]], axis=-1)
    return {
        "x_in": c(x), "tok_w": c(v["L0_tok_W"]), "gamma": v["L0_tok_gamma"], "consts": constants(), "counters": counting(), "buckets": bucket_rows(),
        "w_in": c(w_in.T.reshape(KD, P, 3 * D).transpose(1, 0, 2)),
        "bq_in": c(b_in[0].reshape(KD, P).T), "bk_in": c(b_in[1].reshape(KD, P).T), "bv_in": c(b_in[2]),
        "w_out": blocks(v["L0_attn_w_out"].T), "b_out": v["L0_attn_b_out"], "router0": blocks(v["L0_ffn_router_w"].T),
        "gate_up": c(gu.reshape(E0, KD, P, 2 * F0).transpose(0, 2, 1, 3).reshape(E0, P, GU)),
        "down": c(v["L0_ffn_w_down"].reshape(E0, 2, FH, D).transpose(0, 2, 1, 3).reshape(E0, FH, DN)),
        "shared_gu": blocks(v["L0_ffn_ws_gate_up"]),
        "shared_dn": c(v["L0_ffn_ws_down"].reshape(2, FH, D).transpose(1, 0, 2).reshape(FH, DN)),
        "wqk": blocks(v["L1_attn_Wqk"]), "bqk": c(v["L1_attn_bqk"].reshape(P, 1)), "wv": blocks(v["L1_attn_Wv"]),
        "bv1": v["L1_attn_bv"], "gam1": c(v["L1_attn_gamma"].T), "bet1": c(v["L1_attn_beta"].T), "rel": v["L1_attn_rel_emb"],
        "router1": blocks(v["L1_ffn_router_w"].T),
        "w1": c(v["L1_ffn_w1"].transpose(0, 2, 1).reshape(E1, KD, P, F1).transpose(0, 2, 1, 3).reshape(E1, P, KD * F1)),
        "w2": c(v["L1_ffn_w2"].transpose(0, 2, 1).reshape(E1, KF, P, D).transpose(0, 2, 1, 3).reshape(E1, P, KF * D)),
        "b1": c(v["L1_ffn_b1"].reshape(E1, KF, P).transpose(2, 0, 1).reshape(P, E1 * KF)),
        "b2": c(v["L1_ffn_b2"].reshape(-1)),
    }


def kernel(**inputs):
    import concourse.bacc as bacc
    from concourse.bass_utils import run_bass_kernel_spmd as run

    nc = bacc.Bacc("TRN2", target_bir_lowering=False, num_devices=1)
    arrays = laid_out({k: np.asarray(v) for k, v in inputs.items()})
    args = {k: nc.dram_tensor(k, a.shape, mybir.dt.from_np(a.dtype), kind="ExternalInput").ap() for k, a in arrays.items()}
    out = nc.dram_tensor("out", (T, D), F32, kind="ExternalOutput").ap()
    vit_tower(nc, out=out, **args)
    r = run(nc, [arrays], core_ids=[0])
    return r.results[0]["out"].reshape(2, SEQ, D)
```
